# Optimizing a Trainium2 kernel written in Bass

```python
import numpy as np
import jax
import jax.numpy as jnp

def _softmax(x, axis=-1):
    return jax.nn.softmax(x, axis=axis)
def _gelu(x):
    return jax.nn.gelu(x, approximate=True)
def _silu(x):
    return jax.nn.silu(x)
def _sigmoid(x):
    return jax.nn.sigmoid(x)
def _layernorm(x, axis=-1, eps=1e-5):
    m = jnp.mean(x, axis=axis, keepdims=True)
    v = jnp.var(x, axis=axis, keepdims=True)
    return (x - m) / jnp.sqrt(v + eps)
def _scatter_add(tgt, idx, src, axis=0):
    return tgt.at[idx].add(src)
def _segment_sum(src, seg, n):
    return jax.ops.segment_sum(src, seg, n)

kernel_name = 'mk_conv_attn_hybrid_d2_conv_nhwc128_66354e'

def setup_inputs(seed: int = 0):
    np.random.seed(seed)
    _w = jnp.asarray
    def _rec_inputs():
        import jax
        import jax.numpy as jnp
        _gk = jax.random.key(seed)
        x = -0.000929 + 1 * jax.random.normal(jax.random.fold_in(_gk, 1), (2, 64, 64, 128), jnp.float32)
        return x
    x = _rec_inputs()
    def _L0_conv_setup():
        import jax, jax.numpy as jnp
        import numpy as np
        B, H, W, C = (2, 64, 64, 128)
        NH, K = (4, 7)
        HD = C // NH
        SCALE = HD ** (-0.5)

        def _window_starts(L):
            i = jnp.arange(L)
            return jnp.clip(i - K // 2, 0, L - K)
        key = jax.random.key(seed)
        ks = jax.random.split(key, 5)
        return {'x': jax.random.normal(ks[0], (B, H, W, C), jnp.float32), 'w_qkv': jax.random.normal(ks[1], (C, 3 * C), jnp.float32) * 0.02, 'b_qkv': jnp.zeros((3 * C,), jnp.float32), 'rpb': jax.random.normal(ks[2], (NH, 2 * K - 1, 2 * K - 1), jnp.float32) * 0.02, 'w_proj': jax.random.normal(ks[3], (C, C), jnp.float32) * 0.02, 'b_proj': jnp.zeros((C,), jnp.float32)}
    _L0_conv_all = _L0_conv_setup()
    _L0_conv_in = {k: v for k, v in _L0_conv_all.items() if k in ('w_qkv', 'b_qkv', 'rpb', 'w_proj', 'b_proj', )}
    del _L0_conv_all

    def _L1_attn_setup():
        import jax, jax.numpy as jnp
        import numpy as np
        B, T, D = (4, 2048, 128)
        key = jax.random.key(seed)
        k1, k2, k3 = jax.random.split(key, 3)
        x = jax.random.normal(k1, (B, T, D), dtype=jnp.float32)
        lim = 1.0 / np.sqrt(D)
        W = jax.random.uniform(k2, (3 * D, D), dtype=jnp.float32, minval=-lim, maxval=lim)
        b = jax.random.uniform(k3, (3 * D,), dtype=jnp.float32, minval=-lim, maxval=lim)
        return {'x': x, 'W': W, 'b': b}
    _L1_attn_all = _L1_attn_setup()
    _L1_attn_in = {k: v for k, v in _L1_attn_all.items() if k in ('W', 'b', )}
    del _L1_attn_all

    def _L1_ffn_setup():
        import jax, jax.numpy as jnp
        import numpy as np
        BN_EPS = 1e-05
        key = jax.random.key(seed)
        k1, k2, k3 = jax.random.split(key, 3)
        B, T, I, H = (64, 2048, 128, 128)
        x = jax.random.normal(k1, (B, T, I), dtype=jnp.float32)
        W = jax.random.normal(k2, (H, I), dtype=jnp.float32) * (1.0 / np.sqrt(I))
        V = jnp.linalg.qr(jax.random.normal(k3, (H, H), dtype=jnp.float32))[0]
        gamma = jnp.ones((H,), dtype=jnp.float32)
        beta = jnp.zeros((H,), dtype=jnp.float32)
        return {'x': x, 'W': W, 'V': V, 'gamma': gamma, 'beta': beta}
    _L1_ffn_all = _L1_ffn_setup()
    _L1_ffn_in = {k: v for k, v in _L1_ffn_all.items() if k in ('W', 'V', 'gamma', 'beta', )}
    del _L1_ffn_all

    return {
        "x": x,
        "L0_conv_w_qkv": _L0_conv_in["w_qkv"],
        "L0_conv_b_qkv": _L0_conv_in["b_qkv"],
        "L0_conv_rpb": _L0_conv_in["rpb"],
        "L0_conv_w_proj": _L0_conv_in["w_proj"],
        "L0_conv_b_proj": _L0_conv_in["b_proj"],
        "L1_attn_W": _L1_attn_in["W"],
        "L1_attn_b": _L1_attn_in["b"],
        "L1_ffn_W": _L1_ffn_in["W"],
        "L1_ffn_V": _L1_ffn_in["V"],
        "L1_ffn_gamma": _L1_ffn_in["gamma"],
        "L1_ffn_beta": _L1_ffn_in["beta"],
    }

def reference(x, L0_conv_w_qkv, L0_conv_b_qkv, L0_conv_rpb, L0_conv_w_proj, L0_conv_b_proj, L1_attn_W, L1_attn_b, L1_ffn_W, L1_ffn_V, L1_ffn_gamma, L1_ffn_beta):
    import jax
    import jax.numpy as jnp
    def _L0_conv_ref(x, w_qkv, b_qkv, rpb, w_proj, b_proj):
        import jax, jax.numpy as jnp
        import numpy as np
        B, H, W, C = (2, 64, 64, 128)
        NH, K = (4, 7)
        HD = C // NH
        SCALE = HD ** (-0.5)

        def _window_starts(L):
            i = jnp.arange(L)
            return jnp.clip(i - K // 2, 0, L - K)
        qkv = (x @ w_qkv + b_qkv).reshape(B, H, W, 3, NH, HD)
        q = qkv[..., 0, :, :] * SCALE
        k = qkv[..., 1, :, :]
        v = qkv[..., 2, :, :]
        a = jnp.arange(K)
        idx_h = _window_starts(H)[:, None] + a[None, :]
        idx_w = _window_starts(W)[:, None] + a[None, :]
        k_nb = k[:, idx_h][:, :, :, idx_w]
        v_nb = v[:, idx_h][:, :, :, idx_w]
        attn = jnp.einsum('bhwnd,bhpwqnd->bnhwpq', q, k_nb)
        bidx_h = idx_h - jnp.arange(H)[:, None] + (K - 1)
        bidx_w = idx_w - jnp.arange(W)[:, None] + (K - 1)
        bias = rpb[:, bidx_h[:, :, None, None], bidx_w[None, None]]
        attn = attn + bias.transpose(0, 1, 3, 2, 4)[None]
        attn = jax.nn.softmax(attn.reshape(B, NH, H, W, K * K), axis=-1)
        attn = attn.reshape(B, NH, H, W, K, K)
        out = jnp.einsum('bnhwpq,bhpwqnd->bhwnd', attn, v_nb).reshape(B, H, W, C)
        return out @ w_proj + b_proj

    def _L1_attn_ref(x, W, b):
        import jax, jax.numpy as jnp
        import numpy as np
        B, T, D = (4, 2048, 128)
        Bx, Tx, Dx = x.shape
        qkv = (x @ W.T + b).reshape(Bx, Tx, 3, Dx)
        q, k, v = (qkv[:, :, 0], qkv[:, :, 1], qkv[:, :, 2])
        q = jax.nn.elu(q) + 1.0
        k = jax.nn.elu(k) + 1.0
        kv = jnp.einsum('bti,btj->btij', k, v)
        kv_cum = jnp.cumsum(kv, axis=1)
        k_cum = jnp.cumsum(k, axis=1)
        num = jnp.einsum('bti,btij->btj', q, kv_cum)
        den = jnp.einsum('bti,bti->bt', q, k_cum)[..., None] + 1e-06
        return num / den

    def _L1_ffn_ref(x, W, V, gamma, beta):
        import jax, jax.numpy as jnp
        import numpy as np
        BN_EPS = 1e-05
        B, T, H = (x.shape[0], x.shape[1], W.shape[0])
        Wx = jnp.einsum('bti,hi->bth', x, W)
        flat = Wx.reshape(B * T, H)
        mean = jnp.mean(flat, axis=0)
        var = jnp.var(flat, axis=0)
        Wx = ((flat - mean) * jax.lax.rsqrt(var + BN_EPS) * gamma + beta).reshape(B, T, H)
        Vt = V.T

        def step(yt, wx_t):
            yt = jax.nn.sigmoid(wx_t + yt @ Vt)
            return (yt, yt)
        y0 = jnp.zeros((B, H), dtype=Wx.dtype)
        _, ys = jax.lax.scan(step, y0, jnp.swapaxes(Wx, 0, 1))
        return jnp.swapaxes(ys, 0, 1)

    def _gn(v, G=32, eps=1e-5):
        B_, H_, W_, C_ = v.shape
        g = v.reshape(B_, H_, W_, G, C_ // G)
        m = jnp.mean(g, axis=(1, 2, 4), keepdims=True)
        s = jnp.var(g, axis=(1, 2, 4), keepdims=True)
        return ((g - m) / jnp.sqrt(s + eps)).reshape(v.shape)

    def _ln_c(v, eps=1e-6):
        m = jnp.mean(v, axis=-1, keepdims=True)
        s = jnp.var(v, axis=-1, keepdims=True)
        return (v - m) / jnp.sqrt(s + eps)

    def _ln_t(v, eps=1e-5):
        m = jnp.mean(v, axis=-1, keepdims=True)
        s = jnp.var(v, axis=-1, keepdims=True)
        return (v - m) / jnp.sqrt(s + eps)

    def _to_tokens(v):
        B_, H_, W_, C_ = v.shape
        return v.reshape(B_, H_ * W_, C_)
    def _from_tokens(t, like):
        return t.reshape(like.shape)

    x = x + _L0_conv_ref(_gn(x), L0_conv_w_qkv, L0_conv_b_qkv, L0_conv_rpb, L0_conv_w_proj, L0_conv_b_proj)
    t = _to_tokens(x)
    t = t + _L1_attn_ref(_ln_t(t), L1_attn_W, L1_attn_b)
    t = t + _L1_ffn_ref(_ln_t(t), L1_ffn_W, L1_ffn_V, L1_ffn_gamma, L1_ffn_beta)
    x = _from_tokens(t, x)
    return x


_drawn_inputs = setup_inputs


def setup_inputs(seed=0):
    import zlib

    import numpy as np

    out = dict(_drawn_inputs(seed))
    spreads = {'L0_conv_b_qkv': (0.0, 0.367),
     'L0_conv_b_proj': (0.0, 0.1),
     'L1_ffn_gamma': (1.0, 0.576),
     'L1_ffn_beta': (0.0, 0.453)}
    factors = {'L0_conv_w_qkv': 8.0, 'L0_conv_rpb': 8.0, 'L0_conv_w_proj': 2.689}
    for name, (base, spread) in spreads.items():
        noise = np.random.default_rng([zlib.crc32(name.encode()), seed]).standard_normal(out[name].shape)
        drawn = base * np.exp(spread * noise) if base else spread * noise
        out[name] = jnp.asarray(drawn.astype(out[name].dtype))
    for name, factor in factors.items():
        out[name] = (out[name] * factor).astype(out[name].dtype)
    return out
```

```python
import concourse.bass as bass
from concourse import mybir
from contextlib import ExitStack


def neighborhood_attention_linear_attention_rnn_kernel(
    nc: bass.Bass,
    x: bass.AP,
    w_qkv: bass.AP,
    b_qkv: bass.AP,
    rpb: bass.AP,
    w_proj: bass.AP,
    b_proj: bass.AP,
    attn_w: bass.AP,
    attn_b: bass.AP,
    ffn_w: bass.AP,
    ffn_v: bass.AP,
    gamma: bass.AP,
    beta: bass.AP,
    window_mask: bass.AP,
    group_mean: bass.AP,
    identity: bass.AP,
    causal: bass.AP,
    out: bass.AP,
):
    f32 = mybir.dt.float32
    i32 = mybir.dt.int32
    ALU = mybir.AluOpType
    ACT = mybir.ActivationFunctionType
    AX = mybir.AxisListType
    ds = bass.ds

    B, H, W, C = 2, 64, 64, 128
    NH, K = 4, 7
    HD = C // NH
    SCALE = HD ** -0.5
    PAD = K // 2
    HP, WP = H + 2 * PAD, W + 2 * PAD
    T = H * W
    NT = B * T // 128
    QR, QC = 4, 8
    Q = QR * QC
    KR, KC = QR + K - 1, QC + K - 1
    KEYS = KR * KC
    HALF = KEYS // 2
    HR = KR // 2
    NB = W // QC
    SB = H // QR
    ST = QR * W // 128
    GN_EPS, LN_EPS, BN_EPS, DEN_EPS = 1e-5, 1e-5, 1e-5, 1e-6
    G = 512
    NG = B * T // G
    GB = T // G
    GR = G // W
    TG = G // 128
    CH = 128
    L = T // CH
    WARM = 16
    COLS = B * CH
    CG = G // L
    AGREE = 2.0 ** -21

    def row(v):
        return v.rearrange("(a n) -> a n", a=1)

    def column(v):
        return v.rearrange("(p a) -> p a", a=1)

    def tile(a, t):
        return a[:, bass.ds(t, 1), :].rearrange("p t c -> p (t c)")

    def wait(e, s, value):
        if not isinstance(value, int) or value > 0:
            e.wait_ge(s, value)

    with ExitStack() as whole:
        def tensors(stack):
            return lambda name, shape, dt=f32: stack.enter_context(nc.sbuf_tensor(name, shape, dt))

        def banks(stack):
            return lambda name, shape: stack.enter_context(nc.psum_tensor(name, shape, f32))

        def sem(name):
            return whole.enter_context(nc.semaphore(name))

        v_map = nc.dram_tensor("v_map", (B, HP, WP, C), f32, kind="Internal").ap()
        rpb_pad = nc.dram_tensor("rpb_pad", (NH, 2 * K - 1, KC + QC - 1), f32, kind="Internal").ap()

        sb = tensors(whole)
        res = sb("res", [128, NT, C])
        ident = sb("ident", [128, 128])
        ln_stats = sb("ln_stats", [128, NT, 6])
        ln_diff = sb("ln_diff", [128, NT])
        ln_var = sb("ln_var", [128, NT])
        ln_std = sb("ln_std", [128, NT])
        ln_mean = sb("ln_mean", [128, NT])
        ln_rstd = sb("ln_rstd", [128, NT])

        x_tok = x.rearrange("b h w c -> (b h w) c").rearrange("(t p) c -> p t c", p=128)
        out_tok = out.rearrange("b h w c -> (b h w) c").rearrange("(t p) c -> p t c", p=128)

        def layernorm_vector(dve, step, root):
            me, mo = ln_stats[:, :, 1], ln_stats[:, :, 4]
            se, so = ln_stats[:, :, 2], ln_stats[:, :, 5]
            nc.vector.tensor_tensor(ln_diff[:], me, mo, ALU.subtract).then_inc(step, 1)
            nc.vector.tensor_tensor(ln_mean[:], me, mo, ALU.add).then_inc(step, 1)
            nc.vector.tensor_tensor(ln_var[:], se, so, ALU.add).then_inc(step, 1)
            dve.wait_ge(step, 3)
            nc.vector.tensor_tensor(ln_diff[:], ln_diff[:], ln_diff[:], ALU.mult).then_inc(step, 1)
            nc.vector.tensor_scalar(ln_mean[:], ln_mean[:], 0.5, None, ALU.mult).then_inc(step, 1)
            nc.vector.tensor_scalar(ln_var[:], ln_var[:], 1.0 / C, LN_EPS, ALU.mult, ALU.add).then_inc(step, 1)
            dve.wait_ge(step, 6)
            nc.vector.scalar_tensor_tensor(out=ln_var[:], in0=ln_diff[:], scalar=0.25, in1=ln_var[:],
                                           op0=ALU.mult, op1=ALU.add).then_inc(step, 1)
            dve.wait_ge(root, 1)
            nc.vector.reciprocal(ln_rstd[:], ln_std[:]).then_inc(step, 1)

        def layernorm_scalar(act, step, root):
            act.wait_ge(step, 7)
            nc.scalar.activation(ln_std[:], ln_var[:], ACT.Sqrt).then_inc(root, 1)

        with ExitStack() as layer0:
            sb = tensors(layer0)
            q_map = sb("q_map", [128, B * H, W])
            k_map = sb("k_map", [128, B, HP, WP])
            bias_tab = sb("bias_tab", [128, 3, 3, KEYS])
            wp = sb("wp", [128, C])
            bp = sb("bp", [128, C])
            q_heads = sb("q_heads", [128, 2, NB, 128])
            q_cleared = sem("q_cleared")

            with ExitStack() as stage:
                sb = tensors(stage)
                pb = banks(stage)
                x_stage = sb("x_stage", [128, 4, TG, C])
                x_t = sb("x_t", [128, B * T])
                gm = sb("gm", [128, 128])
                wqkv = sb("wqkv", [128, 3 * C])
                wn = sb("wn", [128, B, 3 * C])
                bqk = sb("bqk", [128, 2])
                bqk_n = sb("bqk_n", [128, B, 2])
                bv = sb("bv", [128, C])
                bv_n = sb("bv_n", [128, B, C])
                gstats = sb("gstats", [128, NG, 6])
                moments = sb("moments", [128, B, 2])
                group = sb("group", [128, B, 2])
                gsq = sb("gsq", [128, B])
                gstd = sb("gstd", [128, B])
                gscale = sb("gscale", [128, B])
                gshift = sb("gshift", [128, B])
                gshift_cols = sb("gshift_cols", [128, B, 128])
                zeros = sb("zeros", [128, PAD * C])
                v_tok = sb("v_tok", [128, 2, TG, C])
                toeplitz = sb("toeplitz", [128, KEYS])
                x_now = sb("x_now", [128, 2, G])

                ps_t = [pb(f"ps_t{i}", [128, G]) for i in range(2)]
                ps_q = pb("ps_q", [128, G])
                ps_k = pb("ps_k", [128, G])
                ps_v = [pb(f"ps_v{i}", [128, TG, C]) for i in range(2)]
                ps_g = pb("ps_g", [128, G])

                ident_in = sem("ident_in")
                weights_in = sem("weights_in")
                bp_in = sem("bp_in")
                x_in = [sem(f"x_in{i}") for i in range(4)]
                transposed = sem("transposed")
                xt_ready = sem("xt_ready")
                res_in = sem("res_in")
                gn_stats = sem("gn_stats")
                gn_step = sem("gn_step")
                gn_group = sem("gn_group")
                gn_root = sem("gn_root")
                gn_fold = sem("gn_fold")
                zero_set = sem("zero_set")
                k_border_set = sem("k_border_set")
                v_border_set = sem("v_border_set")
                rpb_zeroed = sem("rpb_zeroed")
                rpb_placed = sem("rpb_placed")
                toeplitz_in = sem("toeplitz_in")
                mask_in = sem("mask_in")
                bias_built = sem("bias_built")
                folded = sem("folded")
                bias_mm = sem("bias_mm")
                bias_folded = sem("bias_folded")
                staged = sem("staged")
                qk_mm = sem("qk_mm")
                v_mm = sem("v_mm")
                q_out = sem("q_out")
                k_out = sem("k_out")
                v_out = sem("v_out")
                v_stored = [sem(f"v_stored{i}") for i in range(2)]

                with nc.Block() as block:
                    @block.sync
                    def _(sp):
                        sp.dma_start(ident[:], identity).then_inc(ident_in, 16)
                        for s in range(4):
                            sp.dma_start(x_stage[:, s], x_tok[:, s * TG:(s + 1) * TG, :]).then_inc(x_in[s], 16)
                        with sp.Fori(1, NG // 4) as r:
                            for s in range(4):
                                sp.wait_ge(transposed, r * 4 + (s - 3))
                                sp.dma_start(x_stage[:, s], x_tok[:, ds(r * (4 * TG) + s * TG, TG), :])\
                                    .then_inc(x_in[s], 16)
                        sp.wait_ge(zero_set, 1)
                        sp.dma_start(rpb_pad.rearrange("h a b -> (h a) b"),
                                     zeros[0:NH * (2 * K - 1), 0:KC + QC - 1]).then_inc(rpb_zeroed, 16)
                        sp.wait_ge(rpb_zeroed, 16)
                        sp.dma_start(rpb_pad[:, :, QC - PAD - 1:QC - PAD - 1 + 2 * K - 1], rpb)\
                            .then_inc(rpb_placed, 16)
                        sp.dma_start(res[:], x_tok).then_inc(res_in, 16)

                    @block.scalar
                    def _(act):
                        act.dma_start(bp[:], row(b_proj).partition_broadcast(128)).then_inc(bp_in, 16)
                        act.dma_start(wqkv[:], w_qkv).then_inc(weights_in, 16)
                        act.dma_start(gm[:], group_mean).then_inc(weights_in, 16)
                        act.dma_start(bqk[:, 0:1], column(b_qkv[0:C])).then_inc(weights_in, 16)
                        act.dma_start(bqk[:, 1:2], column(b_qkv[C:2 * C])).then_inc(weights_in, 16)
                        act.dma_start(bv[:], row(b_qkv[2 * C:3 * C]).partition_broadcast(128)).then_inc(weights_in, 16)
                        act.dma_start(wp[:], w_proj).then_inc(weights_in, 16)
                        act.dma_start(bias_tab[:], window_mask).then_inc(mask_in, 16)
                        nc.scalar.preload_act_table(ACT.Identity)
                        act.sem_inc(xt_ready, 2)
                        with act.Fori(0, NG // 2) as r:
                            for s in range(2):
                                act.wait_ge(transposed, r * 2 + (s + 1))
                                nc.scalar.activation(x_t[:, ds(r * (2 * G) + s * G, G)], ps_t[s][:],
                                                     ACT.Identity).then_inc(xt_ready, 1)
                        act.wait_ge(gn_step, 5)
                        nc.scalar.activation(gstd[:], gsq[:], ACT.Sqrt).then_inc(gn_root, 1)

                    @block.tensor
                    def _(pe):
                        pe.wait_ge(ident_in, 16)
                        with pe.Fori(0, NG // 4) as r:
                            for s in range(4):
                                pe.wait_ge(x_in[s], r * 16 + 16)
                                pe.wait_ge(xt_ready, r * 4 + (s + 1))
                                for i in range(TG):
                                    last = nc.tensor.transpose(ps_t[s % 2][:, i * 128:(i + 1) * 128],
                                                               x_stage[:, s, i, :], ident[:])
                                last.then_inc(transposed, 1)
                        pe.wait_ge(weights_in, 16 * 6)
                        pe.wait_ge(gn_step, 4)
                        nc.tensor.matmul(ps_g[:, 0:2 * B], gm[:], moments[:].rearrange("p b m -> p (b m)"),
                                         start=True, stop=True).then_inc(gn_group, 1)
                        pe.wait_ge(gn_step, 8)
                        for b in range(B):
                            for m in range(2):
                                n = 2 * b + m
                                nc.tensor.matmul(ps_q[:, n:n + 1], wqkv[:, m * C:(m + 1) * C],
                                                 gshift[:, b:b + 1], start=True, stop=True)
                        for b in range(B):
                            last = nc.tensor.matmul(ps_v[0][:, b, :], gshift_cols[:, b, :], wqkv[:, 2 * C:3 * C],
                                                    start=True, stop=True)
                        last.then_inc(bias_mm, 1)

                    @block.vector
                    def _(dve):
                        with dve.Fori(0, NG) as g:
                            dve.wait_ge(xt_ready, g + 3)
                            nc.vector.bn_stats(gstats[:, ds(g, 1), :], x_t[:, ds(g * G, G)]).then_inc(gn_stats, 1)
                        dve.wait_ge(gn_stats, NG)
                        for b in range(B):
                            nc.vector.bn_aggr(moments[:, b, :], gstats[:, b * GB:(b + 1) * GB, :]
                                              .rearrange("p g s -> p (g s)")).then_inc(gn_step, 1)
                        dve.wait_ge(gn_step, 2)
                        nc.vector.tensor_tensor(gsq[:], moments[:, :, 0], moments[:, :, 0], ALU.mult)\
                            .then_inc(gn_step, 1)
                        dve.wait_ge(gn_step, 3)
                        nc.vector.tensor_tensor(moments[:, :, 1], moments[:, :, 1], gsq[:], ALU.add)\
                            .then_inc(gn_step, 1)
                        dve.wait_ge(gn_group, 1)
                        nc.vector.tensor_copy(group[:].rearrange("p b m -> p (b m)"), ps_g[:, 0:2 * B])\
                            .then_inc(gn_fold, 1)
                        dve.wait_ge(gn_fold, 1)
                        nc.vector.tensor_tensor(gstd[:], group[:, :, 0], group[:, :, 0], ALU.mult).then_inc(gn_fold, 1)
                        nc.vector.tensor_scalar(gshift[:], group[:, :, 1], GN_EPS, None, ALU.add).then_inc(gn_fold, 1)
                        dve.wait_ge(gn_fold, 3)
                        nc.vector.tensor_tensor(gsq[:], gshift[:], gstd[:], ALU.subtract).then_inc(gn_step, 1)
                        dve.wait_ge(gn_root, 1)
                        nc.vector.reciprocal(gscale[:], gstd[:]).then_inc(gn_step, 1)
                        dve.wait_ge(gn_step, 6)
                        nc.vector.scalar_tensor_tensor(out=gshift[:], in0=group[:, :, 0], scalar=-1.0,
                                                       in1=gscale[:], op0=ALU.mult, op1=ALU.mult).then_inc(gn_step, 1)
                        dve.wait_ge(gn_step, 7)
                        nc.vector.tensor_copy(gshift_cols[:], gshift[:].unsqueeze(2).broadcast_to([128, B, 128]))\
                            .then_inc(gn_step, 1)
                        dve.wait_ge(weights_in, 16 * 6)
                        for b in range(B):
                            nc.vector.tensor_scalar(wn[:, b, :], wqkv[:], gscale[:, b:b + 1], None, ALU.mult)\
                                .then_inc(folded, 1)
                        dve.wait_ge(bias_mm, 1)
                        nc.vector.tensor_tensor(bqk_n[:], ps_q[:, 0:2 * B].rearrange("p (b m) -> p b m", b=B),
                                                bqk[:].unsqueeze(1).broadcast_to([128, B, 2]), ALU.add)\
                            .then_inc(folded, 1)
                        nc.vector.tensor_tensor(bv_n[:], ps_v[0][:, 0:B, :],
                                                bv[:].unsqueeze(1).broadcast_to([128, B, C]), ALU.add)\
                            .then_inc(folded, 1)
                        dve.wait_ge(folded, 4)
                        nc.vector.tensor_scalar(bqk_n[:, :, 0], bqk_n[:, :, 0], SCALE, None, ALU.mult)\
                            .then_inc(folded, 1)

                    @block.gpsimd
                    def _(pool):
                        nc.gpsimd.memset(zeros[:], 0.0).then_inc(zero_set, 1)
                        for b in range(B):
                            for edge in (slice(0, PAD), slice(HP - PAD, HP)):
                                nc.gpsimd.memset(k_map[:, b, edge, :], 0.0).then_inc(k_border_set, 1)
                            for edge in (slice(0, PAD), slice(WP - PAD, WP)):
                                nc.gpsimd.memset(k_map[:, b, PAD:PAD + H, edge], 0.0).then_inc(k_border_set, 1)

                with nc.Block() as block:
                    @block.gpsimd
                    def _(pool):
                        nc.gpsimd.memset(q_heads[:], 0.0).then_inc(q_cleared, 1)
                        pool.wait_ge(rpb_placed, 16)
                        for i in range(QR):
                            for j in range(QC):
                                first = i * QC + j
                                pool.dma_start(
                                    toeplitz[first:first + Q * (NH - 1) + 1:Q, :].rearrange("h (a b) -> h a b", a=KR),
                                    rpb_pad[:, PAD - i:PAD - i + KR, QC - 1 - j:QC - 1 - j + KC])\
                                    .then_inc(toeplitz_in, 16)
                        for b in range(B):
                            for c in (0, WP - PAD):
                                pool.dma_start(v_map[b, PAD:PAD + H, c:c + PAD, :],
                                               zeros[0:H, :].rearrange("p (a c) -> p a c", a=PAD))\
                                    .then_inc(v_border_set, 16)
                            for r in (0, HP - PAD):
                                pool.dma_start(v_map[b, r:r + PAD].rearrange("h w c -> (h w c)")
                                               .rearrange("(p n) -> p n", n=2 * C),
                                               zeros[0:PAD * WP // 2, 0:2 * C]).then_inc(v_border_set, 16)
                        pool.wait_ge(mask_in, 16)
                        pool.wait_ge(toeplitz_in, 16 * Q)
                        nc.gpsimd.tensor_tensor(bias_tab[:].rearrange("p r c k -> p (r c) k"),
                                                bias_tab[:].rearrange("p r c k -> p (r c) k"),
                                                toeplitz[:].unsqueeze(1).broadcast_to([128, 9, KEYS]), ALU.add)\
                            .then_inc(bias_built, 1)

                    @block.tensor
                    def _(pe):
                        pe.sem_inc(v_mm, 2)
                        for b in range(B):
                            with pe.Fori(b * GB // 2, (b + 1) * GB // 2) as r:
                                for s in range(2):
                                    pe.wait_ge(q_out, r * 2 + (s + 1))
                                    nc.tensor.matmul(ps_q[:], wn[:, b, 0:C], x_t[:, ds(r * (2 * G) + s * G, G)],
                                                     start=True, stop=True).then_inc(qk_mm, 1)
                                    pe.wait_ge(k_out, r * 2 + (s + 1))
                                    nc.tensor.matmul(ps_k[:], wn[:, b, C:2 * C], x_t[:, ds(r * (2 * G) + s * G, G)],
                                                     start=True, stop=True).then_inc(qk_mm, 1)
                                    pe.wait_ge(staged, r * 2 + (s + 1))
                                    pe.wait_ge(v_out, r * 2 + (s + 1))
                                    for i in range(TG):
                                        last = nc.tensor.matmul(ps_v[s][:, i, :], x_now[:, s, i * 128:(i + 1) * 128],
                                                                wn[:, b, 2 * C:3 * C], start=True, stop=True)
                                    last.then_inc(v_mm, 1)

                    @block.scalar
                    def _(act):
                        nc.scalar.preload_act_table(ACT.Identity)
                        act.sem_inc(q_out, 1)
                        for b in range(B):
                            with act.Fori(b * GB, (b + 1) * GB) as g:
                                act.wait_ge(qk_mm, g * 2 + 1)
                                nc.scalar.activation(q_map[:, ds(g * GR, GR), :].rearrange("p h w -> p (h w)"),
                                                     ps_q[:], ACT.Identity,
                                                     bias=bqk_n[:, b, 0:1], scale=SCALE).then_inc(q_out, 1)

                    @block.vector
                    def _(dve):
                        dve.sem_inc(k_out, 1)
                        dve.sem_inc(v_out, 2)
                        for b in range(B):
                            with dve.Fori(b * GB // 2, (b + 1) * GB // 2) as r:
                                for s in range(2):
                                    dve.wait_ge(v_mm, r * 2 + (s + 1))
                                    nc.vector.tensor_copy(x_now[:, s, :], x_t[:, ds(r * (2 * G) + s * G, G)])\
                                        .then_inc(staged, 1)
                                    dve.wait_ge(qk_mm, r * 4 + (2 * s + 2))
                                    nc.vector.tensor_scalar(
                                        k_map[:, b, ds(r * (2 * GR) + (s * GR + PAD - b * H), GR), PAD:PAD + W],
                                        ps_k[:].rearrange("p (h w) -> p h w", w=W),
                                        bqk_n[:, b, 1:2], None, ALU.add).then_inc(k_out, 1)
                                    dve.wait_ge(v_mm, r * 2 + (s + 3))
                                    dve.wait_ge(v_stored[s], r * 32 + 32)
                                    nc.vector.tensor_tensor(v_tok[:, s], ps_v[s][:],
                                                            bv_n[:, b, :].unsqueeze(1).broadcast_to([128, TG, C]),
                                                            ALU.add).then_inc(v_out, 1)

                    @block.sync
                    def _(sp):
                        for s in range(2):
                            sp.sem_inc(v_stored[s], 32)
                        for b in range(B):
                            with sp.Fori(b * GB // 2, (b + 1) * GB // 2) as r:
                                for s in range(2):
                                    sp.wait_ge(v_out, r * 2 + (s + 3))
                                    for odd in range(2):
                                        sp.dma_start(
                                            v_map[b, ds(r * (2 * GR) + (s * GR + PAD - b * H), GR), PAD:PAD + W, :]
                                            .rearrange("(t o) w c -> o w t c", o=2)[odd],
                                            v_tok[odd * W:(odd + 1) * W, s]).then_inc(v_stored[s], 16)
                        for s in range(2):
                            sp.wait_ge(v_stored[s], 32 * (NG // 2 + 1))
                        sp.wait_ge(v_border_set, 16 * B * 4)
                        sp.wait_ge(res_in, 16)
                        sp.wait_ge(bp_in, 16)

            with ExitStack() as stage:
                sb = tensors(stage)
                pb = banks(stage)
                scores = sb("scores", [128, 2, KEYS])
                negmax = sb("negmax", [128, NB])
                probs = sb("probs", [128, NB, KEYS])
                total = sb("total", [128, NB])
                inverse = sb("inverse", [128, NB])
                probs_t = sb("probs_t", [HALF, 4, 2, 128])
                v_win = sb("v_win", [HALF, 2, 2, NB, C])
                o_t = sb("o_t", [128, 2, QR * W])

                ps_s = [pb(f"ps_s{i}", [128, 512]) for i in range(2)]
                ps_p = [pb(f"ps_p{i}", [128, 4, 128]) for i in range(2)]
                ps_o = [pb(f"ps_o{i}", [128, 2, NB, Q]) for i in range(2)]
                ps_y = pb("ps_y", [128, 4, C])

                q_placed = sem("q_placed")
                scored = sem("scored")
                biased = sem("biased")
                exponentiated = sem("exponentiated")
                inverted = sem("inverted")
                normalised = sem("normalised")
                turned = sem("turned")
                turned_out = sem("turned_out")
                weighed = sem("weighed")
                v_in = [sem(f"v_in{i}") for i in range(2)]
                o_out = sem("o_out")
                projected = sem("projected")
                added = sem("added")
                measured = sem("measured")
                bias_added = sem("bias_added")

                PB = SB // 2
                LN, LT, LC, LW = 2, 3, 4, 5

                def pairs(e, classes=False):
                    yield 0, 0, (0, 1)
                    with e.Fori(1, PB - 1 if classes else PB) as p:
                        yield 0, p, (1, 1)
                    if classes:
                        yield 0, PB - 1, (1, 2)
                        yield 1, PB, (0, 1)
                        with e.Fori(PB + 1, 2 * PB - 1) as p:
                            yield 1, p, (1, 1)
                        yield 1, 2 * PB - 1, (1, 2)
                    else:
                        with e.Fori(PB, 2 * PB) as p:
                            yield 1, p, (1, 1)

                BLOCKS = B * SB * NB
                STRIPS = B * SB

                def weigh(pe, n, j, k, s):
                    pe.wait_ge(turned_out, k + 1)
                    if j == 0:
                        pe.wait_ge(v_in[s], (n - s) * (8 * KR) + 16 * KR)
                        wait(pe, o_out, n - 1)
                    for half in range(2):
                        for h in range(NH):
                            hd = slice(h * HD, (h + 1) * HD)
                            last = nc.tensor.matmul(ps_o[s][hd, 0, j, :], v_win[:, s, half, j, hd],
                                                    probs_t[:, k_slot(j, 4), half, hd],
                                                    start=(half == 0), stop=(half == 1), tile_position=(0, h * HD))
                    last.then_inc(weighed, 1)

                def k_slot(j, slots):
                    return j % slots

                def turn(pe, j, k):
                    pe.wait_ge(normalised, k + 1)
                    wait(pe, turned_out, k - 1)
                    for half in range(2):
                        last = nc.tensor.transpose(ps_p[k_slot(j, 2)][0:HALF, half, :],
                                                   probs[:, j, half * HALF:(half + 1) * HALF], ident[:])
                    last.then_inc(turned, 1)

                def project(pe, n, s):
                    pe.wait_ge(o_out, n + 1)
                    wait(pe, added, n)
                    for i in range(ST):
                        last = nc.tensor.matmul(ps_y[:, i, :], o_t[:, s, i * 128:(i + 1) * 128], wp[:],
                                                start=True, stop=True)
                    last.then_inc(projected, 1)

                with nc.Block() as block:
                    @block.gpsimd
                    def _(pool):
                        def add_bias(n):
                            pool.wait_ge(q_placed, n + 1)
                            nc.gpsimd.tensor_tensor(res[:, ds(n * ST, ST), :], res[:, ds(n * ST, ST), :],
                                                    bp[:].unsqueeze(1).broadcast_to([128, ST, C]), ALU.add)\
                                .then_inc(bias_added, 1)

                        def place(n, s):
                            wait(pool, scored, (n - 1) * NB)
                            wait(pool, bias_added, n)
                            for h in range(NH):
                                hd = slice(h * HD, (h + 1) * HD)
                                last = nc.gpsimd.tensor_copy(
                                    q_heads[hd, s, :, hd].rearrange("p j (r c) -> p r j c", r=QR),
                                    q_map[hd, ds(n * QR, QR), :].rearrange("p r (j c) -> p r j c", j=NB))
                            last.then_inc(q_placed, 1)

                        place(0, 0)
                        add_bias(0)
                        place(1, 1)
                        add_bias(1)
                        with pool.Fori(1, STRIPS // 2) as p:
                            for s in range(2):
                                place(p * 2 + s, s)
                                add_bias(p * 2 + s)

                    @block.sync
                    def _(sp):
                        for b, p, _ in pairs(sp):
                            for s in range(2):
                                n = p * 2 + s
                                if isinstance(p, int) and p == 0:
                                    pass
                                else:
                                    sp.wait_ge(weighed, (n - 1) * NB)
                                for a in range(KR):
                                    src = v_map[b, ds(n * QR + (a - b * H), 1), 0:KC, :]
                                    win = bass.AP(src.tensor, src.offset, [[C, KC], [QC * C, NB], [1, C]])
                                    lane = (a % HR) * KC
                                    sp.dma_start(v_win[lane:lane + KC, s, a // HR], win).then_inc(v_in[s], 16)

                    @block.tensor
                    def _(pe):
                        for b, p, _ in pairs(pe):
                            first = isinstance(p, int) and p == 0
                            for s in range(2):
                                n = p * 2 + s
                                for j in range(NB):
                                    k = n * NB + j
                                    if j == 0:
                                        pe.wait_ge(q_placed, n + 1)
                                    wait(pe, biased, k - 1)
                                    nc.tensor.matmul(
                                        ps_s[j % 2][:, 0:KEYS], q_heads[:, s, j, :],
                                        k_map[:, b, ds(n * QR - b * H, KR), j * QC:j * QC + KC],
                                        start=True, stop=True).then_inc(scored, 1)
                                    if not (first and s == 0 and j < LW):
                                        own = j >= LW
                                        weigh(pe, n if own else n - 1, (j - LW) % NB, k - LW, s if own else 1 - s)
                                    if not (first and s == 0 and j < LT):
                                        turn(pe, (j - LT) % NB, k - LT)
                                    if j == LW + 2 and not (first and s == 0):
                                        project(pe, n - 1, 1 - s)
                        for i in range(LW, 0, -1):
                            weigh(pe, STRIPS - 1, NB - i, BLOCKS - i, 1)
                            if i > LW - LT:
                                turn(pe, NB + LW - LT - i, BLOCKS + LW - LT - i)
                        project(pe, STRIPS - 1, 1)

                    @block.vector
                    def _(dve):
                        def invert(j, k):
                            c = j
                            dve.wait_ge(exponentiated, k + 1)
                            nc.vector.reciprocal(inverse[:, c:c + 1], total[:, c:c + 1]).then_inc(inverted, 1)

                        def normalise(j, k):
                            c = j
                            dve.wait_ge(inverted, k + 1)
                            nc.vector.tensor_scalar(probs[:, c, :], probs[:, c, :], inverse[:, c:c + 1], None,
                                                    ALU.mult).then_inc(normalised, 1)

                        def residual(n):
                            dve.wait_ge(projected, n + 1)
                            dve.wait_ge(bias_added, n + 1)
                            nc.vector.tensor_tensor(res[:, ds(n * ST, ST), :], ps_y[:, 0:ST, :],
                                                    res[:, ds(n * ST, ST), :], ALU.add).then_inc(added, 1)
                            dve.wait_ge(added, n + 1)
                            for i in range(ST):
                                nc.vector.bn_stats(
                                    ln_stats[:, ds(n * ST + i, 1), :].rearrange("p t s -> p (t s)"),
                                    res[:, ds(n * ST + i, 1), :].rearrange("p t c -> p (t c)")).then_inc(measured, 1)

                        for b, p, windows in pairs(dve, classes=True):
                            first = isinstance(p, int) and p == 0
                            for s in range(2):
                                n = p * 2 + s
                                for j in range(NB):
                                    k = n * NB + j
                                    c = 0 if j == 0 else 2 if j == NB - 1 else 1
                                    dve.wait_ge(scored, k + 1)
                                    if not (first and s == 0 and j < LN):
                                        invert((j - LN) % NB, k - LN)
                                    nc.vector.tensor_tensor_reduce(
                                        out=scores[:, j % 2, :], in0=ps_s[j % 2][:, 0:KEYS],
                                        in1=bias_tab[:, windows[s], c, :], scale=-1.0, scalar=3.0e38,
                                        op0=ALU.add, op1=ALU.min,
                                        accum_out=negmax[:, j:j + 1]).then_inc(biased, 1)
                                    if not (first and s == 0 and j < LN):
                                        normalise((j - LN) % NB, k - LN)
                                    if j == 0 and not first:
                                        residual(n - 2)
                        for i in range(LN, 0, -1):
                            invert(NB - i, BLOCKS - i)
                            normalise(NB - i, BLOCKS - i)
                        residual(STRIPS - 2)
                        residual(STRIPS - 1)

                    @block.scalar
                    def _(act):
                        nc.scalar.preload_act_table(ACT.Exp)

                        def turned_copy(j, k):
                            act.wait_ge(turned, k + 1)
                            wait(act, weighed, k - 3)
                            nc.scalar.activation(probs_t[:, j % 4], ps_p[j % 2][0:HALF, 0:2, :], ACT.Copy)\
                                .then_inc(turned_out, 1)

                        def strip_out(n, s):
                            act.wait_ge(weighed, n * NB + NB)
                            wait(act, projected, n - 1)
                            nc.scalar.activation(
                                o_t[:, s, :].rearrange("p (r j c) -> p j r c", r=QR, j=NB),
                                ps_o[s][:, 0].rearrange("p j (r c) -> p j r c", r=QR), ACT.Copy).then_inc(o_out, 1)

                        for b, p, _ in pairs(act):
                            first = isinstance(p, int) and p == 0
                            for s in range(2):
                                n = p * 2 + s
                                for j in range(NB):
                                    k = n * NB + j
                                    c = j
                                    if not (first and s == 0 and j < LC):
                                        turned_copy((j - LC) % NB, k - LC)
                                    act.wait_ge(biased, k + 1)
                                    wait(act, turned, k - NB + 1)
                                    nc.scalar.activation(probs[:, c, :], scores[:, j % 2, :], ACT.Exp,
                                                         bias=negmax[:, c:c + 1], scale=-1.0,
                                                         accum_out=total[:, c:c + 1]).then_inc(exponentiated, 1)
                                    if j == LW and not (first and s == 0):
                                        strip_out(n - 1, 1 - s)
                        for i in range(LC, 0, -1):
                            turned_copy(NB - i, BLOCKS - i)
                        strip_out(STRIPS - 1, 1)

        with ExitStack() as stage:
            sb = tensors(stage)
            pb = banks(stage)
            w_nat = sb("w_nat", [128, 3, C])
            w_t = sb("w_t", [128, 3, C])
            bqk = sb("attn_bqk", [128, 2])
            bv = sb("attn_bv", [128, C])
            tri = sb("tri", [128, 128])
            z = sb("z", [128, 2, TG, C])
            z_t = sb("z_t", [128, 2, G])
            expo = sb("expo", [128, 2, 2, G])
            relu = sb("relu", [128, 2, 2, G])
            qk_t = sb("qk_t", [128, 2, 2, G])
            k_tok = sb("k_tok", [128, 2, TG, C])
            v_one = sb("v_one", [128, 2, TG, C + 1])
            weights = sb("weights", [128, TG, 128])
            kv = sb("kv", [128, TG + 1, C + 1])
            den = sb("den", [128, TG])

            z_shift = ln_diff

            ps_z = pb("ps_z", [128, TG, 128])
            ps_q = pb("ps1_q", [128, G])
            ps_k = pb("ps1_k", [128, G])
            ps_v = pb("ps1_v", [128, TG, C])
            ps_w = pb("ps_w", [128, TG, 128])
            ps_kv = pb("ps_kv", [128, 512])
            ps_n = pb("ps_n", [128, 512])
            ps_last = pb("ps_last", [128, 512])

            w_in = sem("w_in")
            w_turned = sem("w_turned")
            w_ready = sem("w_ready")
            ln_step = sem("ln_step")
            ln_root = sem("ln_root")
            one_set = sem("one_set")
            shifted = sem("shifted")
            z_ready = sem("z_ready")
            z_turned = sem("z_turned")
            z_out = sem("z_out")
            clipped = sem("clipped")
            clip_begun = sem("clip_begun")
            qk_made = sem("qk_made")
            qk_read = sem("qk_read")
            qk_ready = sem("qk_ready")
            v_made = sem("v_made")
            v_ready = sem("v_ready")
            k_turned = sem("k_turned")
            k_out2 = sem("k_out2")
            w_made = sem("w_made")
            w_masked = sem("w_masked")
            kv_made = sem("kv_made")
            kv_zeroed = sem("kv_zeroed")
            kv_step = sem("kv_step")
            n_made = sem("n_made")
            den_ready = sem("den_ready")
            res_ready = sem("res_ready")
            stats_ready = sem("stats_ready")

            KVC = C + 1

            def kv_bank(t):
                return ps_kv[:, t * KVC:(t + 1) * KVC] if t < 3 else ps_last[:, 0:KVC]

            def n_bank(t):
                return ps_n[:, t * KVC:(t + 1) * KVC] if t < 3 else ps_last[:, KVC:2 * KVC]

            def steps(e, ahead, step, between=None):
                ahead()
                for b in range(B):
                    if b and between:
                        between()
                    with e.Fori(b * GB // 2, (b + 1) * GB // 2 - (b == B - 1)) as r:
                        step(r * 2, 0)
                        step(r * 2 + 1, 1)
                step(NG - 2, 0)
                step(NG - 1, 1)

            def is_last(g, n=1):
                return isinstance(g, int) and g >= NG - n

            with nc.Block() as block:
                @block.sync
                def _(sp):
                    sp.dma_start(w_nat[:], attn_w.rearrange("(m p) c -> p m c", p=128)).then_inc(w_in, 16)
                    sp.dma_start(bqk[:, 0:1], column(attn_b[0:C])).then_inc(w_in, 16)
                    sp.dma_start(bqk[:, 1:2], column(attn_b[C:2 * C])).then_inc(w_in, 16)
                    sp.dma_start(bv[:], row(attn_b[2 * C:3 * C]).partition_broadcast(128)).then_inc(w_in, 16)
                    sp.dma_start(tri[:], causal).then_inc(w_in, 16)

                @block.gpsimd
                def _(pool):
                    nc.gpsimd.memset(v_one[:], 1.0).then_inc(one_set, 1)
                    pool.wait_ge(one_set, 1)
                    pool.sem_inc(qk_ready, 4)

                    def combine(g, s):
                        for m in range(2):
                            pool.wait_ge(qk_read, g * 2 + (m + 3))
                            pool.sem_inc(clip_begun, 1)
                            nc.gpsimd.tensor_scalar(expo[:, s, m, :], expo[:, s, m, :], 1.0, None, ALU.min)\
                                .then_inc(clipped, 1)
                            pool.wait_ge(clipped, g * 2 + (m + 1))
                            nc.gpsimd.tensor_tensor(qk_t[:, s, m, :], expo[:, s, m, :], relu[:, s, m, :], ALU.add)\
                                .then_inc(qk_ready, 1)

                    def step(g, s):
                        if not is_last(g):
                            pool.wait_ge(n_made, g + 1)
                            combine(g + 1, 1 - s)

                    steps(pool, lambda: combine(0, 0), step)

                @block.tensor
                def _(pe):
                    pe.wait_ge(w_in, 16 * 5)
                    for m in range(3):
                        last = nc.tensor.transpose(ps_z[:, m, :], w_nat[:, m, :], ident[:])
                    last.then_inc(w_turned, 1)
                    pe.wait_ge(w_ready, 1)
                    pe.sem_inc(n_made, 1)

                    def turn_z(g, s):
                        pe.wait_ge(z_ready, g + 1)
                        for i in range(TG):
                            last = nc.tensor.transpose(ps_z[:, i, :], z[:, s, i, :], ident[:])
                        last.then_inc(z_turned, 1)

                    def make_qk(g, s):
                        pe.wait_ge(z_out, g + 1)
                        for m, bank in ((0, ps_q), (1, ps_k)):
                            pe.wait_ge(qk_read, g * 2 + (m + 1))
                            nc.tensor.matmul(bank[:], w_t[:, m, :], z_t[:, s, :], start=True, stop=True)\
                                .then_inc(qk_made, 1)

                    def make_v(s):
                        for i in range(TG):
                            last = nc.tensor.matmul(ps_v[:, i, :], z_t[:, s, i * 128:(i + 1) * 128], w_t[:, 2, :],
                                                    start=True, stop=True)
                        last.then_inc(v_made, 1)

                    def ahead():
                        turn_z(0, 0)
                        make_qk(0, 0)
                        make_v(0)

                    def step(g, s):
                        if not is_last(g):
                            pe.wait_ge(k_out2, g + 1)
                            turn_z(g + 1, 1 - s)
                        pe.wait_ge(w_masked, g + 1)
                        pe.wait_ge(qk_ready, g * 2 + 6)
                        for i in range(TG):
                            t = slice(i * 128, (i + 1) * 128)
                            last = nc.tensor.matmul(ps_w[:, i, :], qk_t[:, s, 1, t], qk_t[:, s, 0, t],
                                                    start=True, stop=True)
                        last.then_inc(w_made, 1)
                        if is_last(g):
                            pe.wait_ge(k_out2, g + 1)
                        else:
                            pe.wait_ge(z_out, g + 2)
                        for i in range(TG):
                            last = nc.tensor.transpose(ps_z[:, i, :], qk_t[:, s, 1, i * 128:(i + 1) * 128], ident[:])
                        last.then_inc(k_turned, 1)
                        if not is_last(g):
                            make_qk(g + 1, 1 - s)
                        pe.wait_ge(k_out2, g + 2)
                        pe.wait_ge(v_ready, g + 1)
                        pe.wait_ge(res_ready, g * TG + 1)
                        for i in range(TG):
                            last = nc.tensor.matmul(kv_bank(i), k_tok[:, s, i, :], v_one[:, s, i, :],
                                                    start=True, stop=True)
                        last.then_inc(kv_made, 1)
                        if not is_last(g):
                            make_v(1 - s)
                        pe.wait_ge(w_masked, g + 2)
                        pe.wait_ge(kv_step, g * (TG + 1) + (TG + 1))
                        for i in range(TG):
                            nc.tensor.matmul(n_bank(i), weights[:, i, :], v_one[:, s, i, :], start=True, stop=False)
                            last = nc.tensor.matmul(n_bank(i), qk_t[:, s, 0, i * 128:(i + 1) * 128], kv[:, i, :],
                                                    start=False, stop=True)
                        last.then_inc(n_made, 1)

                    steps(pe, ahead, step)

                @block.scalar
                def _(act):
                    layernorm_scalar(act, ln_step, ln_root)
                    act.wait_ge(w_turned, 1)
                    nc.scalar.activation(w_t[:], ps_z[:, 0:3, :], ACT.Copy).then_inc(w_ready, 1)
                    nc.scalar.preload_act_table(ACT.Exp)
                    act.sem_inc(qk_read, 2)
                    act.sem_inc(k_out2, 1)
                    act.wait_ge(shifted, 1)
                    act.wait_ge(w_in, 16 * 5)

                    def normalise(g, s):
                        for i in range(TG):
                            t = g * TG + i
                            last = nc.scalar.activation(z[:, s, i, :], tile(res, t), ACT.Identity,
                                                        bias=z_shift[:, ds(t, 1)], scale=ln_rstd[:, ds(t, 1)])
                        last.then_inc(z_ready, 1)

                    def copy_z(g, s):
                        act.wait_ge(z_turned, g + 1)
                        nc.scalar.activation(z_t[:, s, :], ps_z[:].rearrange("p t c -> p (t c)"), ACT.Copy)\
                            .then_inc(z_out, 1)

                    def exponentials(g, s):
                        for m, bank in ((0, ps_q), (1, ps_k)):
                            act.wait_ge(qk_made, g * 2 + (m + 1))
                            act.wait_ge(qk_ready, g * 2 + (m + 1))
                            nc.scalar.activation(expo[:, s, m, :], bank[:], ACT.Exp, bias=bqk[:, m:m + 1])
                            nc.scalar.activation(relu[:, s, m, :], bank[:], ACT.Relu, bias=bqk[:, m:m + 1])\
                                .then_inc(qk_read, 1)

                    def ahead():
                        normalise(0, 0)
                        normalise(1, 1)
                        copy_z(0, 0)
                        exponentials(0, 0)

                    def step(g, s):
                        if not is_last(g):
                            copy_z(g + 1, 1 - s)
                        act.wait_ge(k_turned, g + 1)
                        nc.scalar.activation(k_tok[:, s], ps_z[:], ACT.Copy).then_inc(k_out2, 1)
                        if not is_last(g):
                            exponentials(g + 1, 1 - s)
                        if not is_last(g, 2):
                            normalise(g + 2, s)

                    steps(act, ahead, step)

                @block.vector
                def _(dve):
                    layernorm_vector(dve, ln_step, ln_root)
                    dve.wait_ge(ln_step, 8)
                    nc.vector.scalar_tensor_tensor(out=z_shift[:], in0=ln_mean[:], scalar=-1.0, in1=ln_rstd[:],
                                                   op0=ALU.mult, op1=ALU.mult).then_inc(shifted, 1)
                    dve.wait_ge(one_set, 1)
                    dve.wait_ge(w_in, 16 * 5)
                    dve.sem_inc(w_masked, 1)
                    dve.sem_inc(res_ready, 1)
                    nc.vector.memset(kv[:, TG, :], 0.0).then_inc(kv_zeroed, 1)
                    dve.wait_ge(kv_zeroed, 1)

                    def values(g, s):
                        dve.wait_ge(v_made, g + 1)
                        nc.vector.tensor_tensor(v_one[:, s, :, 0:C], ps_v[:],
                                                bv[:].unsqueeze(1).broadcast_to([128, TG, C]), ALU.add)\
                            .then_inc(v_ready, 1)

                    def step(g, s):
                        dve.wait_ge(w_made, g + 1)
                        nc.vector.tensor_tensor(weights[:], ps_w[:],
                                                tri[:].unsqueeze(1).broadcast_to([128, TG, 128]), ALU.mult)\
                            .then_inc(w_masked, 1)
                        dve.wait_ge(kv_made, g + 1)
                        nc.vector.tensor_copy(kv[:, 0, :], kv[:, TG, :]).then_inc(kv_step, 1)
                        for i in range(TG):
                            dve.wait_ge(kv_step, g * (TG + 1) + (i + 1))
                            nc.vector.tensor_tensor(kv[:, i + 1, :], kv_bank(i), kv[:, i, :], ALU.add)\
                                .then_inc(kv_step, 1)
                        dve.wait_ge(kv_step, g * (TG + 1) + (TG + 1))
                        if not is_last(g):
                            values(g + 1, 1 - s)
                        dve.wait_ge(n_made, g + 2)
                        nc.vector.tensor_scalar(den[:, 0:3], ps_n[:, 0:3 * KVC]
                                                .rearrange("p (t c) -> p t c", c=KVC)[:, :, C],
                                                DEN_EPS, None, ALU.add).then_inc(den_ready, 1)
                        nc.vector.tensor_scalar(den[:, 3:4], ps_last[:, 2 * KVC - 1:2 * KVC], DEN_EPS, None, ALU.add)\
                            .then_inc(den_ready, 1)
                        dve.wait_ge(den_ready, g * 3 + 2)
                        nc.vector.reciprocal(den[:], den[:]).then_inc(den_ready, 1)
                        dve.wait_ge(den_ready, g * 3 + 3)
                        for i in range(TG):
                            t = g * TG + i
                            nc.vector.scalar_tensor_tensor(out=tile(res, t), in0=n_bank(i)[:, 0:C],
                                                           scalar=den[:, i:i + 1], in1=tile(res, t),
                                                           op0=ALU.mult, op1=ALU.add).then_inc(res_ready, 1)
                        dve.wait_ge(res_ready, g * TG + (TG + 1))
                        for i in range(TG):
                            t = g * TG + i
                            nc.vector.bn_stats(tile(ln_stats, t), tile(res, t)).then_inc(stats_ready, 1)

                    def new_batch():
                        nc.vector.memset(kv[:, TG, :], 0.0).then_inc(kv_zeroed, 1)
                        dve.wait_ge(kv_zeroed, 2)

                    steps(dve, lambda: values(0, 0), step, new_batch)

        with ExitStack() as stage:
            sb = tensors(stage)
            w_nat = sb("w4_nat", [128, C])
            v_nat = sb("v4_nat", [128, C])
            w_t = sb("w4_t", [128, C])
            v_t = sb("v4_t", [128, C])
            w_scaled = sb("w_scaled", [128, C])
            wn_t = sb("wn_t", [128, C])
            gamma_c = sb("gamma_c", [128, 1])
            beta_c = sb("beta_c", [128, 1])
            z = sb("z4", [128, 2, TG, C])
            z_t = sb("z4_t", [128, L, COLS])
            states = sb("states", [128, L, COLS])
            bstats = sb("bstats", [128, L // 2, 6])
            bmv = sb("bmv", [128, 2])
            bvar = sb("bvar", [128, 1])
            bstd = sb("bstd", [128, 1])
            bscale = sb("bscale", [128, 1])
            bshift = sb("bshift", [128, 1])
            warm = sb("warm", [128, 2, COLS])
            start = sb("start", [128, B, CH])
            gap = sb("gap", [128, COLS])
            worst = sb("worst", [128, 1])
            worst_all = sb("worst_all", [1, 1])
            apart = sb("apart", [1, 1], i32)
            one_state = sb("one_state", [128, B])

            ln_step = sem("ln4_step")
            ln_root = sem("ln4_root")
            w_in = sem("w4_in")
            w_turned = sem("w4_turned")
            w_ready = sem("w4_ready")
            z_ready = sem("z4_ready")
            z_turned = sem("z4_turned")
            z_out = sem("z4_out")
            wx_made = sem("wx_made")
            wx_read = sem("wx_read")
            bn_step = sem("bn_step")
            bn_root = sem("bn_root")
            wn_turned = sem("wn_turned")
            wn_ready = sem("wn_ready")

            with ExitStack() as stage4:
                pb = banks(stage4)
                ps_z = [pb(f"ps4_z{i}", [128, TG, 128]) for i in range(2)]
                ps_x = [pb(f"ps4_x{i}", [128, G]) for i in range(2)]
                ps_w = pb("ps4_w", [128, 3, C])
                with nc.Block() as block:
                    @block.sync
                    def _(sp):
                        sp.dma_start(w_nat[:], ffn_w).then_inc(w_in, 16)
                        sp.dma_start(v_nat[:], ffn_v).then_inc(w_in, 16)
                        sp.dma_start(gamma_c[:], column(gamma)).then_inc(w_in, 16)
                        sp.dma_start(beta_c[:], column(beta)).then_inc(w_in, 16)

                    @block.tensor
                    def _(pe):
                        pe.wait_ge(w_in, 16 * 4)
                        nc.tensor.transpose(ps_w[:, 0, :], w_nat[:], ident[:])
                        nc.tensor.transpose(ps_w[:, 1, :], v_nat[:], ident[:]).then_inc(w_turned, 1)
                        with pe.Fori(0, NG // 2) as r:
                            for s in range(2):
                                pe.wait_ge(z_ready, r * 2 + (s + 1))
                                pe.wait_ge(z_out, r * 2 + (s + 1))
                                for i in range(TG):
                                    last = nc.tensor.transpose(ps_z[s][:, i, :], z[:, s, i, :], ident[:])
                                last.then_inc(z_turned, 1)
                        pe.wait_ge(z_out, NG + 2)
                        pe.wait_ge(w_ready, 1)
                        with pe.Fori(0, L // 4) as r:
                            for s in range(2):
                                pe.wait_ge(wx_read, r * 2 + (s + 1))
                                nc.tensor.matmul(ps_x[s][:], w_t[:], z_t[:, ds(r * 4 + 2 * s, 2), :]
                                                 .rearrange("p s c -> p (s c)"), start=True, stop=True)\
                                    .then_inc(wx_made, 1)
                        pe.wait_ge(bn_step, 4)
                        nc.tensor.transpose(ps_w[:, 2, :], w_scaled[:], ident[:]).then_inc(wn_turned, 1)

                    @block.scalar
                    def _(act):
                        layernorm_scalar(act, ln_step, ln_root)
                        act.wait_ge(w_turned, 1)
                        nc.scalar.activation(w_t[:], ps_w[:, 0, :], ACT.Copy)
                        nc.scalar.activation(v_t[:], ps_w[:, 1, :], ACT.Copy).then_inc(w_ready, 1)
                        act.sem_inc(z_out, 2)
                        with act.Fori(0, NG // 2) as r:
                            for s in range(2):
                                act.wait_ge(z_turned, r * 2 + (s + 1))
                                nc.scalar.activation(
                                    z_t[:, :, ds(r * (2 * CG) + s * CG, CG)].rearrange("p s c -> p c s"),
                                    ps_z[s][:].rearrange("p t (c s) -> p (t c) s", s=L), ACT.Copy).then_inc(z_out, 1)
                        act.wait_ge(bn_step, 2)
                        nc.scalar.activation(bstd[:], bvar[:], ACT.Sqrt).then_inc(bn_root, 1)
                        act.wait_ge(wn_turned, 1)
                        nc.scalar.activation(wn_t[:], ps_w[:, 2, :], ACT.Copy).then_inc(wn_ready, 1)

                    @block.vector
                    def _(dve):
                        layernorm_vector(dve, ln_step, ln_root)
                        dve.wait_ge(ln_step, 8)
                        dve.sem_inc(wx_read, 2)
                        with dve.Fori(0, NG // 2) as r:
                            for s in range(2):
                                dve.wait_ge(z_out, r * 2 + (s + 1))
                                for i in range(TG):
                                    t = r * (2 * TG) + (s * TG + i)
                                    last = nc.vector.tensor_scalar(z[:, s, i, :], tile(res, t),
                                                                   ln_mean[:, ds(t, 1)], ln_rstd[:, ds(t, 1)],
                                                                   ALU.subtract, ALU.mult)
                                last.then_inc(z_ready, 1)
                        with dve.Fori(0, L // 4) as r:
                            for s in range(2):
                                dve.wait_ge(wx_made, r * 2 + (s + 1))
                                nc.vector.bn_stats(tile(bstats, r * 2 + s), ps_x[s][:]).then_inc(wx_read, 1)
                        dve.wait_ge(wx_read, L // 2 + 2)
                        nc.vector.bn_aggr(bmv[:], bstats[:].rearrange("p g s -> p (g s)")).then_inc(bn_step, 1)
                        dve.wait_ge(bn_step, 1)
                        nc.vector.tensor_scalar(bvar[:], bmv[:, 1:2], BN_EPS, None, ALU.add).then_inc(bn_step, 1)
                        dve.wait_ge(bn_root, 1)
                        dve.wait_ge(w_in, 16 * 4)
                        nc.vector.reciprocal(bscale[:], bstd[:]).then_inc(bn_step, 1)
                        dve.wait_ge(bn_step, 3)
                        nc.vector.tensor_scalar(w_scaled[:], w_nat[:], bscale[:], gamma_c[:], ALU.mult, ALU.mult)\
                            .then_inc(bn_step, 1)
                        nc.vector.scalar_tensor_tensor(out=bshift[:], in0=bmv[:, 0:1], scalar=bscale[:],
                                                       in1=gamma_c[:], op0=ALU.mult, op1=ALU.mult).then_inc(bn_step, 1)
                        dve.wait_ge(bn_step, 5)
                        nc.vector.tensor_tensor(bshift[:], beta_c[:], bshift[:], ALU.subtract).then_inc(bn_step, 1)

            warmed = sem("warmed")
            warm_made = sem("warm_made")
            started = sem("started")
            step_made = sem("step_made")
            step_done = sem("step_done")
            seam_step = sem("seam_step")
            gap_turned = sem("gap_turned")
            apart_set = sem("apart_set")
            single_made = sem("single_made")
            single_done = sem("single_done")
            single_start = sem("single_start")
            with ExitStack() as stage5:
                pb = banks(stage5)
                ps_r = [pb(f"ps_r{i}", [128, 512]) for i in range(2)]
                ps_1 = pb("ps_one", [128, 512])

                with nc.Block() as block:
                    @block.tensor
                    def _(pe):
                        pe.wait_ge(warmed, 1)
                        with pe.Fori(0, WARM // 2) as r:
                            for s in range(2):
                                nc.tensor.matmul(ps_r[s][:, 0:COLS], wn_t[:], z_t[:, ds(r * 2 + (s + L - WARM), 1), :]
                                                 .rearrange("p s c -> p (s c)"), start=True, stop=False)
                                pe.wait_ge(warmed, r * 2 + (s + 1))
                                nc.tensor.matmul(ps_r[s][:, 0:COLS], v_t[:], warm[:, s, :], start=False, stop=True)\
                                    .then_inc(warm_made, 1)

                        def step(s, x_cols, y, ahead):
                            nc.tensor.matmul(ps_r[s][:, 0:COLS], wn_t[:], x_cols, start=True, stop=False)
                            pe.wait_ge(*ahead)
                            nc.tensor.matmul(ps_r[s][:, 0:COLS], v_t[:], y, start=False, stop=True)\
                                .then_inc(step_made, 1)

                        pe.wait_ge(warmed, WARM + 1)
                        step(0, z_t[:, 0, :], start[:].rearrange("p b c -> p (b c)"), (started, 1))
                        step(1, z_t[:, 1, :], states[:, 0, :], (step_done, 1))
                        with pe.Fori(1, L // 2) as r:
                            for s in range(2):
                                step(s, tile(z_t, r * 2 + s), tile(states, r * 2 + (s - 1)),
                                     (step_done, r * 2 + s))
                        pe.wait_ge(seam_step, 3)
                        nc.tensor.transpose(ps_1[0:1, 0:128], worst[:], ident[:]).then_inc(gap_turned, 1)

                    @block.scalar
                    def _(act):
                        nc.scalar.preload_act_table(ACT.Sigmoid)
                        with act.Fori(0, WARM // 2) as r:
                            for s in range(2):
                                act.wait_ge(warm_made, r * 2 + (s + 1))
                                nc.scalar.activation(warm[:, 1 - s, :], ps_r[s][:, 0:COLS], ACT.Sigmoid,
                                                     bias=bshift[:]).then_inc(warmed, 1)
                        with act.Fori(0, L // 2) as r:
                            for s in range(2):
                                act.wait_ge(step_made, r * 2 + (s + 1))
                                nc.scalar.activation(tile(states, r * 2 + s), ps_r[s][:, 0:COLS], ACT.Sigmoid,
                                                     bias=bshift[:]).then_inc(step_done, 1)

                    @block.vector
                    def _(dve):
                        nc.vector.memset(start[:], 0.0).then_inc(seam_step, 1)
                        nc.vector.memset(warm[:, 0, :], 0.0).then_inc(warmed, 1)
                        dve.wait_ge(warmed, WARM + 1)
                        dve.wait_ge(seam_step, 1)
                        nc.vector.tensor_copy(start[:, :, 1:CH], warm[:, 0, :].rearrange("p (b c) -> p b c", b=B)
                                              [:, :, 0:CH - 1]).then_inc(started, 1)
                        dve.wait_ge(step_done, L)
                        nc.vector.tensor_tensor(gap[:], states[:, L - 1, :], warm[:, 0, :], ALU.subtract)\
                            .then_inc(seam_step, 1)
                        dve.wait_ge(seam_step, 2)
                        nc.vector.tensor_reduce(worst[:], gap[:], AX.X, ALU.max, apply_absolute_value=True)\
                            .then_inc(seam_step, 1)
                        dve.wait_ge(gap_turned, 1)
                        nc.vector.tensor_reduce(worst_all[:], ps_1[0:1, 0:128], AX.X, ALU.max).then_inc(seam_step, 1)
                        dve.wait_ge(seam_step, 4)
                        nc.vector.tensor_scalar(apart[:], worst_all[:], AGREE, None, ALU.is_gt).then_inc(apart_set, 1)

                with nc.Block() as block:
                    @block.tensor
                    def _(pe):
                        flag = pe.alloc_register("pe_apart")
                        pe.reg_load(flag, apart[0:1, 0:1])
                        with pe.If_ne(flag, 0):
                            pe.wait_ge(single_start, 1)
                            with pe.Fori(0, CH) as c:
                                with pe.Fori(0, L) as i:
                                    cols = z_t[:, ds(i, 1), :].rearrange("p s (b c) -> p (s b) c", b=B)[:, :, ds(c, 1)]\
                                        .rearrange("p b c -> p (b c)")
                                    pe.wait_ge(single_done, c * L + i + 1)
                                    nc.tensor.matmul(ps_1[:, 0:B], wn_t[:], cols, start=True, stop=False)
                                    nc.tensor.matmul(ps_1[:, 0:B], v_t[:], one_state[:], start=False, stop=True)\
                                        .then_inc(single_made, 1)

                    @block.scalar
                    def _(act):
                        flag = act.alloc_register("act_apart")
                        act.reg_load(flag, apart[0:1, 0:1])
                        with act.If_ne(flag, 0):
                            act.wait_ge(single_start, 1)
                            act.sem_inc(single_done, 1)
                            with act.Fori(0, CH) as c:
                                with act.Fori(0, L) as i:
                                    act.wait_ge(single_made, c * L + i + 1)
                                    cols = states[:, ds(i, 1), :].rearrange("p s (b c) -> p (s b) c", b=B)\
                                        [:, :, ds(c, 1)].rearrange("p b c -> p (b c)")
                                    nc.scalar.activation(cols, ps_1[:, 0:B], ACT.Sigmoid, bias=bshift[:])
                                    nc.scalar.activation(one_state[:], ps_1[:, 0:B], ACT.Sigmoid, bias=bshift[:])\
                                        .then_inc(single_done, 1)

                    @block.vector
                    def _(dve):
                        nc.vector.memset(one_state[:], 0.0).then_inc(single_start, 1)

            with ExitStack() as stage6:
                pb = banks(stage6)
                sb = tensors(stage6)
                y_t = sb("y_t", [128, 2, CG, L])
                y_out = sb("y_out", [128, 4, TG, C])
                ps_y = [pb(f"ps6_y{i}", [128, TG, 128]) for i in range(2)]
                y_ready = sem("y_ready")
                y_turned = sem("y_turned")
                y_added = sem("y_added")
                y_stored = [sem(f"y_stored{i}") for i in range(4)]
                with nc.Block() as block:
                    @block.scalar
                    def _(act):
                        act.sem_inc(y_turned, 2)
                        with act.Fori(0, NG // 2) as r:
                            for s in range(2):
                                act.wait_ge(y_turned, r * 2 + (s + 1))
                                nc.scalar.activation(
                                    y_t[:, s], states[:, :, ds(r * (2 * CG) + s * CG, CG)]
                                    .rearrange("p s c -> p c s"), ACT.Copy).then_inc(y_ready, 1)

                    @block.tensor
                    def _(pe):
                        with pe.Fori(0, NG // 2) as r:
                            for s in range(2):
                                pe.wait_ge(y_ready, r * 2 + (s + 1))
                                pe.wait_ge(y_added, r * 2 + (s + 1))
                                flat = y_t[:, s].rearrange("p c s -> p (c s)")
                                for i in range(TG):
                                    last = nc.tensor.transpose(ps_y[s][:, i, :], flat[:, i * 128:(i + 1) * 128],
                                                               ident[:])
                                last.then_inc(y_turned, 1)

                    @block.vector
                    def _(dve):
                        dve.sem_inc(y_added, 2)
                        with dve.Fori(0, NG // 4) as r:
                            for s in range(4):
                                dve.wait_ge(y_turned, r * 4 + (s + 3))
                                dve.wait_ge(y_stored[s], r * 16 + 16)
                                nc.vector.tensor_tensor(y_out[:, s], ps_y[s % 2][:],
                                                        res[:, ds(r * (4 * TG) + s * TG, TG), :], ALU.add)\
                                    .then_inc(y_added, 1)

                    @block.sync
                    def _(sp):
                        for s in range(4):
                            sp.sem_inc(y_stored[s], 16)
                        with sp.Fori(0, NG // 4) as r:
                            for s in range(4):
                                sp.wait_ge(y_added, r * 4 + (s + 3))
                                sp.dma_start(out_tok[:, ds(r * (4 * TG) + s * TG, TG), :], y_out[:, s])\
                                    .then_inc(y_stored[s], 16)
                        for s in range(4):
                            sp.wait_ge(y_stored[s], 16 * (NG // 4 + 1))


_INS = ["x", "L0_conv_w_qkv", "L0_conv_b_qkv", "L0_conv_rpb", "L0_conv_w_proj", "L0_conv_b_proj",
        "L1_attn_W", "L1_attn_b", "L1_ffn_W", "L1_ffn_V", "L1_ffn_gamma", "L1_ffn_beta"]


def _window_mask():
    import numpy as np

    size, k, qr, qc, heads = 64, 7, 4, 8, 4
    kr, kc = qr + k - 1, qc + k - 1

    def inside(first, n, keys):
        at = first + np.arange(n)
        start = np.clip(at - k // 2, 0, size - k)
        key = first - k // 2 + np.arange(keys)
        return (key[None] >= start[:, None]) & (key[None] < start[:, None] + k)

    rows = [inside(f, qr, kr) for f in (0, qr, size - qr)]
    cols = [inside(f, qc, kc) for f in (0, qc, size - qc)]
    mask = np.empty((heads, qr, qc, 3, 3, kr, kc), np.float32)
    for a, r in enumerate(rows):
        for b, c in enumerate(cols):
            both = r[:, None, :, None] & c[None, :, None, :]
            mask[:, :, :, a, b] = np.where(both, 0.0, -1e30)
    return mask.reshape(128, 3, 3, kr * kc)


def _constants():
    import numpy as np

    group = np.kron(np.eye(32), np.full((4, 4), 0.25)).astype(np.float32)
    return {"window_mask": _window_mask(), "group_mean": group, "identity": np.eye(128, dtype=np.float32),
            "causal": np.triu(np.ones((128, 128), np.float32))}


def kernel(**inputs):
    import numpy as np
    import concourse.bacc as bacc
    from concourse import mybir
    from concourse.bass_utils import run_bass_kernel_spmd

    nc = bacc.Bacc("TRN2", target_bir_lowering=False, num_devices=1)
    arrays, args = {}, []
    for name, a in [(n, inputs[n]) for n in _INS] + list(_constants().items()):
        a = np.ascontiguousarray(a)
        arrays[f"in_{name}"] = a
        args.append(nc.dram_tensor(f"in_{name}", a.shape, mybir.dt.from_np(a.dtype), kind="ExternalInput").ap())
    args.append(nc.dram_tensor("out_0", (2, 64, 64, 128), mybir.dt.float32, kind="ExternalOutput").ap())
    neighborhood_attention_linear_attention_rnn_kernel(nc, *args)
    r = run_bass_kernel_spmd(nc, [arrays], core_ids=[0])
    return r.results[0]["out_0"]
```

```python
import concourse.bass as bass
from concourse import mybir
from contextlib import ExitStack


def neighborhood_attention_linear_attention_rnn_kernel(
    nc: bass.Bass,
    x: bass.AP,
    w_qkv: bass.AP,
    b_qkv: bass.AP,
    rpb: bass.AP,
    w_proj: bass.AP,
    b_proj: bass.AP,
    attn_w: bass.AP,
    attn_b: bass.AP,
    ffn_w: bass.AP,
    ffn_v: bass.AP,
    gamma: bass.AP,
    beta: bass.AP,
    window_mask: bass.AP,
    group_mean: bass.AP,
    identity: bass.AP,
    causal: bass.AP,
    out: bass.AP,
):
    f32 = mybir.dt.float32
    i32 = mybir.dt.int32
    ALU = mybir.AluOpType
    ACT = mybir.ActivationFunctionType
    AX = mybir.AxisListType
    ds = bass.ds

    B, H, W, C = 2, 64, 64, 128
    NH, K = 4, 7
    HD = C // NH
    SCALE = HD ** -0.5
    PAD = K // 2
    HP, WP = H + 2 * PAD, W + 2 * PAD
    T = H * W
    NT = B * T // 128
    QR, QC = 4, 8
    Q = QR * QC
    KR, KC = QR + K - 1, QC + K - 1
    KEYS = KR * KC
    MR = 128 // KC - 1
    MAIN = MR * KC
    REST = KEYS - MAIN
    RB = 4
    NB = W // QC
    SB = H // QR
    ST = QR * W // 128
    GN_EPS, LN_EPS, BN_EPS, DEN_EPS = 1e-5, 1e-5, 1e-5, 1e-6
    G = 512
    NG = B * T // G
    GB = T // G
    GR = G // W
    TG = G // 128
    CH = 128
    L = T // CH
    WARM = 12
    COLS = B * CH
    CG = G // L
    AGREE = 2.0 ** -21

    def row(v):
        return v.rearrange("(a n) -> a n", a=1)

    def column(v):
        return v.rearrange("(p a) -> p a", a=1)

    def tile(a, t):
        return a[:, bass.ds(t, 1), :].rearrange("p t c -> p (t c)")

    def wait(e, s, value):
        if not isinstance(value, int) or value > 0:
            e.wait_ge(s, value)

    with ExitStack() as whole:
        def tensors(stack):
            return lambda name, shape, dt=f32: stack.enter_context(nc.sbuf_tensor(name, shape, dt))

        def banks(stack):
            return lambda name, shape: stack.enter_context(nc.psum_tensor(name, shape, f32))

        def sem(name):
            return whole.enter_context(nc.semaphore(name))

        v_map = nc.dram_tensor("v_map", (B, H, WP, C), f32, kind="Internal").ap()
        v_windows = nc.dram_tensor("v_windows", (B, NB, HP, KC * C), f32, kind="Internal").ap()
        rpb_pad = nc.dram_tensor("rpb_pad", (NH, 2 * K - 1, KC + QC - 1), f32, kind="Internal").ap()

        sb = tensors(whole)
        res = sb("res", [128, NT, C])
        ident = sb("ident", [128, 128])
        ln_stats = sb("ln_stats", [128, NT, 6])
        ln_diff = sb("ln_diff", [128, NT])
        ln_var = sb("ln_var", [128, NT])
        ln_std = sb("ln_std", [128, NT])
        ln_mean = sb("ln_mean", [128, NT])
        ln_rstd = sb("ln_rstd", [128, NT])
        weights1 = sb("weights1", [128, 5, C])
        weights1_t = sb("weights1_t", [128, 5, C])
        attn_wt, ffn_wt, v_t = weights1_t[:, 0:3, :], weights1_t[:, 3, :], weights1_t[:, 4, :]
        attn_bqk = sb("attn_bqk", [128, 2])
        attn_bv = sb("attn_bv", [128, C])
        tri = sb("tri", [128, 128])
        gamma_c = sb("gamma_c", [128, 1])
        beta_c = sb("beta_c", [128, 1])
        weights1_in = sem("weights1_in")
        weights1_turned = sem("weights1_turned")
        weights1_ready = sem("weights1_ready")

        x_tok = x.rearrange("b h w c -> (b h w) c").rearrange("(t p) c -> p t c", p=128)
        out_tok = out.rearrange("b h w c -> (b h w) c").rearrange("(t p) c -> p t c", p=128)

        def layernorm_vector(dve, step, root):
            me, mo = ln_stats[:, :, 1], ln_stats[:, :, 4]
            se, so = ln_stats[:, :, 2], ln_stats[:, :, 5]
            nc.vector.tensor_tensor(ln_diff[:], me, mo, ALU.subtract).then_inc(step, 1)
            nc.vector.tensor_tensor(ln_mean[:], me, mo, ALU.add).then_inc(step, 1)
            nc.vector.tensor_tensor(ln_var[:], se, so, ALU.add).then_inc(step, 1)
            dve.wait_ge(step, 3)
            nc.vector.tensor_tensor(ln_diff[:], ln_diff[:], ln_diff[:], ALU.mult).then_inc(step, 1)
            nc.vector.tensor_scalar(ln_mean[:], ln_mean[:], 0.5, None, ALU.mult).then_inc(step, 1)
            nc.vector.tensor_scalar(ln_var[:], ln_var[:], 1.0 / C, LN_EPS, ALU.mult, ALU.add).then_inc(step, 1)
            dve.wait_ge(step, 6)
            nc.vector.scalar_tensor_tensor(out=ln_var[:], in0=ln_diff[:], scalar=0.25, in1=ln_var[:],
                                           op0=ALU.mult, op1=ALU.add).then_inc(step, 1)
            dve.wait_ge(root, 1)
            nc.vector.reciprocal(ln_rstd[:], ln_std[:]).then_inc(step, 1)

        def layernorm_scalar(act, step, root):
            act.wait_ge(step, 7)
            nc.scalar.activation(ln_std[:], ln_var[:], ACT.Sqrt).then_inc(root, 1)

        with ExitStack() as layer0:
            sb = tensors(layer0)
            q_map = sb("q_map", [128, B * H, W])
            k_map = sb("k_map", [128, B, HP, WP])
            bias_tab = sb("bias_tab", [128, 3, 3, KEYS])
            wp = sb("wp", [128, C])
            bp = sb("bp", [128, C])
            q_heads = sb("q_heads", [128, 2, NB, 128])
            v_rest = sb("v_rest", [RB * REST, 2, NB, C])
            q_cleared = sem("q_cleared")

            q_placed = sem("q_placed")
            v_stored = [sem(f"v_stored{i}") for i in range(2)]
            v_border_set = sem("v_border_set")
            v_side_set = sem("v_side_set")
            v_windowed = [sem(f"v_windowed{b}") for b in range(B)]
            v_cleared = sem("v_cleared")
            res_in = sem("res_in")
            bp_in = sem("bp_in")

            def place_queries(n, s):
                for h in range(NH):
                    hd = slice(h * HD, (h + 1) * HD)
                    last = nc.gpsimd.tensor_copy(
                        q_heads[hd, s, :, hd].rearrange("p j (r c) -> p r j c", r=QR),
                        q_map[hd, ds(n * QR, QR), :].rearrange("p r (j c) -> p r j c", j=NB))
                last.then_inc(q_placed, 1)

            with ExitStack() as stage:
                sb = tensors(stage)
                pb = banks(stage)
                x_stage = sb("x_stage", [128, 4, TG, C])
                x_t = sb("x_t", [128, B * T])
                gm = sb("gm", [128, 128])
                wqkv = sb("wqkv", [128, 3 * C])
                wn = sb("wn", [128, B, 3 * C])
                bqk = sb("bqk", [128, 2])
                bqk_n = sb("bqk_n", [128, B, 2])
                bv = sb("bv", [128, C])
                bv_n = sb("bv_n", [128, B, C])
                gstats = sb("gstats", [128, NG, 6])
                moments = sb("moments", [128, B, 2])
                group = sb("group", [128, B, 2])
                gsq = sb("gsq", [128, B])
                gstd = sb("gstd", [128, B])
                gscale = sb("gscale", [128, B])
                gshift = sb("gshift", [128, B])
                gshift_cols = sb("gshift_cols", [128, B, 128])
                zeros = sb("zeros", [128, PAD * C])
                v_tok = sb("v_tok", [128, 2, TG, C])
                toeplitz = sb("toeplitz", [128, KEYS])
                x_now = sb("x_now", [128, 2, G])

                ps_t = [pb(f"ps_t{i}", [128, G]) for i in range(2)]
                ps_q = pb("ps_q", [128, G])
                ps_k = pb("ps_k", [128, G])
                ps_v = [pb(f"ps_v{i}", [128, TG, C]) for i in range(2)]
                ps_g = pb("ps_g", [128, G])

                ident_in = sem("ident_in")
                weights_in = sem("weights_in")
                x_in = [sem(f"x_in{i}") for i in range(4)]
                transposed = sem("transposed")
                xt_ready = sem("xt_ready")
                gn_stats = sem("gn_stats")
                gn_step = sem("gn_step")
                gn_group = sem("gn_group")
                gn_root = sem("gn_root")
                gn_fold = sem("gn_fold")
                zero_set = sem("zero_set")
                k_border_set = sem("k_border_set")
                rpb_zeroed = sem("rpb_zeroed")
                rpb_placed = sem("rpb_placed")
                toeplitz_in = sem("toeplitz_in")
                mask_in = sem("mask_in")
                bias_built = sem("bias_built")
                folded = sem("folded")
                bias_mm = sem("bias_mm")
                bias_folded = sem("bias_folded")
                staged = sem("staged")
                qk_mm = sem("qk_mm")
                v_mm = sem("v_mm")
                q_out = sem("q_out")
                k_out = sem("k_out")
                v_out = sem("v_out")

                with nc.Block() as block:
                    @block.sync
                    def _(sp):
                        sp.dma_start(ident[:], identity).then_inc(ident_in, 16)
                        for s in range(4):
                            sp.dma_start(x_stage[:, s], x_tok[:, s * TG:(s + 1) * TG, :]).then_inc(x_in[s], 16)
                        with sp.Fori(1, NG // 4) as r:
                            for s in range(4):
                                sp.wait_ge(transposed, r * 4 + (s - 3))
                                sp.dma_start(x_stage[:, s], x_tok[:, ds(r * (4 * TG) + s * TG, TG), :])\
                                    .then_inc(x_in[s], 16)
                        sp.wait_ge(zero_set, 1)
                        sp.dma_start(rpb_pad.rearrange("h a b -> (h a) b"),
                                     zeros[0:NH * (2 * K - 1), 0:KC + QC - 1]).then_inc(rpb_zeroed, 16)
                        sp.wait_ge(rpb_zeroed, 16)
                        sp.dma_start(rpb_pad[:, :, QC - PAD - 1:QC - PAD - 1 + 2 * K - 1], rpb)\
                            .then_inc(rpb_placed, 16)
                        sp.dma_start(weights1[:, 0:3, :], attn_w.rearrange("(m p) c -> p m c", p=128))\
                            .then_inc(weights1_in, 16)
                        sp.dma_start(weights1[:, 3, :], ffn_w).then_inc(weights1_in, 16)
                        sp.dma_start(weights1[:, 4, :], ffn_v).then_inc(weights1_in, 16)
                        sp.dma_start(attn_bqk[:, 0:1], column(attn_b[0:C])).then_inc(weights1_in, 16)
                        sp.dma_start(attn_bqk[:, 1:2], column(attn_b[C:2 * C])).then_inc(weights1_in, 16)
                        sp.dma_start(attn_bv[:], row(attn_b[2 * C:3 * C]).partition_broadcast(128))\
                            .then_inc(weights1_in, 16)
                        sp.dma_start(tri[:], causal).then_inc(weights1_in, 16)
                        sp.dma_start(gamma_c[:], column(gamma)).then_inc(weights1_in, 16)
                        sp.dma_start(beta_c[:], column(beta)).then_inc(weights1_in, 16)
                        sp.dma_start(res[:], x_tok).then_inc(res_in, 16)

                    @block.scalar
                    def _(act):
                        act.dma_start(bp[:], row(b_proj).partition_broadcast(128)).then_inc(bp_in, 16)
                        act.dma_start(wqkv[:], w_qkv).then_inc(weights_in, 16)
                        act.dma_start(gm[:], group_mean).then_inc(weights_in, 16)
                        act.dma_start(bqk[:, 0:1], column(b_qkv[0:C])).then_inc(weights_in, 16)
                        act.dma_start(bqk[:, 1:2], column(b_qkv[C:2 * C])).then_inc(weights_in, 16)
                        act.dma_start(bv[:], row(b_qkv[2 * C:3 * C]).partition_broadcast(128)).then_inc(weights_in, 16)
                        act.dma_start(wp[:], w_proj).then_inc(weights_in, 16)
                        act.dma_start(bias_tab[:], window_mask).then_inc(mask_in, 16)
                        nc.scalar.preload_act_table(ACT.Identity)
                        act.sem_inc(xt_ready, 2)
                        with act.Fori(0, NG // 2) as r:
                            for s in range(2):
                                act.wait_ge(transposed, r * 2 + (s + 1))
                                nc.scalar.activation(x_t[:, ds(r * (2 * G) + s * G, G)], ps_t[s][:],
                                                     ACT.Identity).then_inc(xt_ready, 1)
                        act.wait_ge(gn_step, 5)
                        nc.scalar.activation(gstd[:], gsq[:], ACT.Sqrt).then_inc(gn_root, 1)

                    @block.tensor
                    def _(pe):
                        pe.wait_ge(ident_in, 16)
                        with pe.Fori(0, NG // 4) as r:
                            for s in range(4):
                                pe.wait_ge(x_in[s], r * 16 + 16)
                                pe.wait_ge(xt_ready, r * 4 + (s + 1))
                                for i in range(TG):
                                    last = nc.tensor.transpose(ps_t[s % 2][:, i * 128:(i + 1) * 128],
                                                               x_stage[:, s, i, :], ident[:])
                                last.then_inc(transposed, 1)
                        pe.wait_ge(weights_in, 16 * 6)
                        pe.wait_ge(gn_step, 4)
                        nc.tensor.matmul(ps_g[:, 0:2 * B], gm[:], moments[:].rearrange("p b m -> p (b m)"),
                                         start=True, stop=True).then_inc(gn_group, 1)
                        pe.wait_ge(gn_step, 8)
                        for b in range(B):
                            for m in range(2):
                                n = 2 * b + m
                                nc.tensor.matmul(ps_q[:, n:n + 1], wqkv[:, m * C:(m + 1) * C],
                                                 gshift[:, b:b + 1], start=True, stop=True)
                        for b in range(B):
                            last = nc.tensor.matmul(ps_v[0][:, b, :], gshift_cols[:, b, :], wqkv[:, 2 * C:3 * C],
                                                    start=True, stop=True)
                        last.then_inc(bias_mm, 1)

                    @block.vector
                    def _(dve):
                        with dve.Fori(0, NG) as g:
                            dve.wait_ge(xt_ready, g + 3)
                            nc.vector.bn_stats(gstats[:, ds(g, 1), :], x_t[:, ds(g * G, G)]).then_inc(gn_stats, 1)
                        dve.wait_ge(gn_stats, NG)
                        for b in range(B):
                            nc.vector.bn_aggr(moments[:, b, :], gstats[:, b * GB:(b + 1) * GB, :]
                                              .rearrange("p g s -> p (g s)")).then_inc(gn_step, 1)
                        dve.wait_ge(gn_step, 2)
                        nc.vector.tensor_tensor(gsq[:], moments[:, :, 0], moments[:, :, 0], ALU.mult)\
                            .then_inc(gn_step, 1)
                        dve.wait_ge(gn_step, 3)
                        nc.vector.tensor_tensor(moments[:, :, 1], moments[:, :, 1], gsq[:], ALU.add)\
                            .then_inc(gn_step, 1)
                        dve.wait_ge(gn_group, 1)
                        nc.vector.tensor_copy(group[:].rearrange("p b m -> p (b m)"), ps_g[:, 0:2 * B])\
                            .then_inc(gn_fold, 1)
                        dve.wait_ge(gn_fold, 1)
                        nc.vector.tensor_tensor(gstd[:], group[:, :, 0], group[:, :, 0], ALU.mult).then_inc(gn_fold, 1)
                        nc.vector.tensor_scalar(gshift[:], group[:, :, 1], GN_EPS, None, ALU.add).then_inc(gn_fold, 1)
                        dve.wait_ge(gn_fold, 3)
                        nc.vector.tensor_tensor(gsq[:], gshift[:], gstd[:], ALU.subtract).then_inc(gn_step, 1)
                        dve.wait_ge(gn_root, 1)
                        nc.vector.reciprocal(gscale[:], gstd[:]).then_inc(gn_step, 1)
                        dve.wait_ge(gn_step, 6)
                        nc.vector.scalar_tensor_tensor(out=gshift[:], in0=group[:, :, 0], scalar=-1.0,
                                                       in1=gscale[:], op0=ALU.mult, op1=ALU.mult).then_inc(gn_step, 1)
                        dve.wait_ge(gn_step, 7)
                        nc.vector.tensor_copy(gshift_cols[:], gshift[:].unsqueeze(2).broadcast_to([128, B, 128]))\
                            .then_inc(gn_step, 1)
                        dve.wait_ge(weights_in, 16 * 6)
                        for b in range(B):
                            nc.vector.tensor_scalar(wn[:, b, :], wqkv[:], gscale[:, b:b + 1], None, ALU.mult)\
                                .then_inc(folded, 1)
                        dve.wait_ge(bias_mm, 1)
                        nc.vector.tensor_tensor(bqk_n[:], ps_q[:, 0:2 * B].rearrange("p (b m) -> p b m", b=B),
                                                bqk[:].unsqueeze(1).broadcast_to([128, B, 2]), ALU.add)\
                            .then_inc(folded, 1)
                        nc.vector.tensor_tensor(bv_n[:], ps_v[0][:, 0:B, :],
                                                bv[:].unsqueeze(1).broadcast_to([128, B, C]), ALU.add)\
                            .then_inc(folded, 1)
                        dve.wait_ge(folded, 4)
                        nc.vector.tensor_scalar(bqk_n[:, :, 0], bqk_n[:, :, 0], SCALE, None, ALU.mult)\
                            .then_inc(folded, 1)

                    @block.gpsimd
                    def _(pool):
                        nc.gpsimd.memset(zeros[:], 0.0).then_inc(zero_set, 1)
                        for b in range(B):
                            for edge in (slice(0, PAD), slice(HP - PAD, HP)):
                                nc.gpsimd.memset(k_map[:, b, edge, :], 0.0).then_inc(k_border_set, 1)
                            for edge in (slice(0, PAD), slice(WP - PAD, WP)):
                                nc.gpsimd.memset(k_map[:, b, PAD:PAD + H, edge], 0.0).then_inc(k_border_set, 1)

                with nc.Block() as block:
                    @block.gpsimd
                    def _(pool):
                        nc.gpsimd.memset(q_heads[:], 0.0).then_inc(q_cleared, 1)
                        nc.gpsimd.memset(v_rest[:], 0.0).then_inc(v_cleared, 1)
                        pool.wait_ge(rpb_placed, 16)
                        for i in range(QR):
                            for j in range(QC):
                                first = i * QC + j
                                pool.dma_start(
                                    toeplitz[first:first + Q * (NH - 1) + 1:Q, :].rearrange("h (a b) -> h a b", a=KR),
                                    rpb_pad[:, PAD - i:PAD - i + KR, QC - 1 - j:QC - 1 - j + KC])\
                                    .then_inc(toeplitz_in, 16)
                        pool.wait_ge(q_cleared, 1)
                        pool.wait_ge(v_cleared, 1)
                        pool.wait_ge(q_out, 2)
                        for n in range(2):
                            place_queries(n, n)

                    @block.tensor
                    def _(pe):
                        pe.sem_inc(v_mm, 2)
                        for b in range(B):
                            with pe.Fori(b * GB // 2, (b + 1) * GB // 2) as r:
                                for s in range(2):
                                    pe.wait_ge(q_out, r * 2 + (s + 1))
                                    nc.tensor.matmul(ps_q[:], wn[:, b, 0:C], x_t[:, ds(r * (2 * G) + s * G, G)],
                                                     start=True, stop=True).then_inc(qk_mm, 1)
                                    pe.wait_ge(k_out, r * 2 + (s + 1))
                                    nc.tensor.matmul(ps_k[:], wn[:, b, C:2 * C], x_t[:, ds(r * (2 * G) + s * G, G)],
                                                     start=True, stop=True).then_inc(qk_mm, 1)
                                    pe.wait_ge(staged, r * 2 + (s + 1))
                                    pe.wait_ge(v_out, r * 2 + (s + 1))
                                    for i in range(TG):
                                        last = nc.tensor.matmul(ps_v[s][:, i, :], x_now[:, s, i * 128:(i + 1) * 128],
                                                                wn[:, b, 2 * C:3 * C], start=True, stop=True)
                                    last.then_inc(v_mm, 1)
                        pe.wait_ge(weights1_in, 16 * 9)
                        for m in range(5):
                            last = nc.tensor.transpose(ps_t[m // 4][:, m % 4 * 128:(m % 4 + 1) * 128],
                                                       weights1[:, m, :], ident[:])
                        last.then_inc(weights1_turned, 1)

                    @block.scalar
                    def _(act):
                        nc.scalar.preload_act_table(ACT.Identity)
                        act.sem_inc(q_out, 1)
                        for b in range(B):
                            with act.Fori(b * GB, (b + 1) * GB) as g:
                                act.wait_ge(qk_mm, g * 2 + 1)
                                nc.scalar.activation(q_map[:, ds(g * GR, GR), :].rearrange("p h w -> p (h w)"),
                                                     ps_q[:], ACT.Identity,
                                                     bias=bqk_n[:, b, 0:1], scale=SCALE).then_inc(q_out, 1)
                        act.wait_ge(weights1_turned, 1)
                        nc.scalar.activation(weights1_t[:, 0:4, :].rearrange("p m c -> p (m c)"), ps_t[0][:], ACT.Copy)
                        nc.scalar.activation(weights1_t[:, 4, :], ps_t[1][:, 0:128], ACT.Copy)\
                            .then_inc(weights1_ready, 1)

                    @block.vector
                    def _(dve):
                        dve.sem_inc(k_out, 1)
                        dve.sem_inc(v_out, 2)
                        for b in range(B):
                            with dve.Fori(b * GB // 2, (b + 1) * GB // 2) as r:
                                for s in range(2):
                                    dve.wait_ge(v_mm, r * 2 + (s + 1))
                                    nc.vector.tensor_copy(x_now[:, s, :], x_t[:, ds(r * (2 * G) + s * G, G)])\
                                        .then_inc(staged, 1)
                                    dve.wait_ge(qk_mm, r * 4 + (2 * s + 2))
                                    nc.vector.tensor_scalar(
                                        k_map[:, b, ds(r * (2 * GR) + (s * GR + PAD - b * H), GR), PAD:PAD + W],
                                        ps_k[:].rearrange("p (h w) -> p h w", w=W),
                                        bqk_n[:, b, 1:2], None, ALU.add).then_inc(k_out, 1)
                                    dve.wait_ge(v_mm, r * 2 + (s + 3))
                                    dve.wait_ge(v_stored[s], r * 32 + 32)
                                    nc.vector.tensor_tensor(v_tok[:, s], ps_v[s][:],
                                                            bv_n[:, b, :].unsqueeze(1).broadcast_to([128, TG, C]),
                                                            ALU.add).then_inc(v_out, 1)
                        dve.wait_ge(mask_in, 16)
                        dve.wait_ge(toeplitz_in, 16 * Q)
                        nc.vector.tensor_tensor(bias_tab[:].rearrange("p r c k -> p (r c) k"),
                                                bias_tab[:].rearrange("p r c k -> p (r c) k"),
                                                toeplitz[:].unsqueeze(1).broadcast_to([128, 9, KEYS]), ALU.add)\
                            .then_inc(bias_built, 1)

                    @block.sync
                    def _(sp):
                        for b in range(B):
                            for c in (0, WP - PAD):
                                sp.dma_start(v_map[b, :, c:c + PAD, :],
                                             zeros[0:H, :].rearrange("p (a c) -> p a c", a=PAD))\
                                    .then_inc(v_side_set, 16)
                        for b in range(B):
                            for r in (0, HP - PAD):
                                edge = v_windows[b, 0, r, :]
                                n = NB * PAD * KC * C // 128
                                sp.dma_start(bass.AP(edge.tensor, edge.offset,
                                                     [[HP * KC * C, NB], [n, 128 // NB], [1, n]]),
                                             zeros[:, 0:n]).then_inc(v_border_set, 16)
                        for s in range(2):
                            sp.sem_inc(v_stored[s], 32)

                        def store(b, r):
                            for s in range(2):
                                sp.wait_ge(v_out, r * 2 + (s + 3))
                                for odd in range(2):
                                    sp.dma_start(
                                        v_map[b, ds(r * (2 * GR) + (s * GR - b * H), GR), PAD:PAD + W, :]
                                        .rearrange("(t o) w c -> o w t c", o=2)[odd],
                                        v_tok[odd * W:(odd + 1) * W, s]).then_inc(v_stored[s], 16)

                        def window(b, r):
                            for s in range(2):
                                sp.wait_ge(v_stored[s], r * 32 + 64)
                            rows = v_map[b, ds(r * (2 * GR) - b * H, 1), 0, :]
                            wins = v_windows[b, 0, ds(r * (2 * GR) + (PAD - b * H), 1), :]
                            sp.dma_start(bass.AP(wins.tensor, wins.offset,
                                                 [[HP * KC * C, NB], [KC * C, 2 * GR], [1, KC * C]]),
                                         bass.AP(rows.tensor, rows.offset,
                                                 [[QC * C, NB], [WP * C, 2 * GR], [1, KC * C]]))\
                                .then_inc(v_windowed[b], 16)

                        GP = GB // 2
                        for b in range(B):
                            store(b, b * GP)
                            if b == 0:
                                sp.wait_ge(v_side_set, 16 * 2 * B)
                            else:
                                window(b - 1, b * GP - 1)
                            with sp.Fori(b * GP + 1, (b + 1) * GP) as r:
                                store(b, r)
                                window(b, r - 1)
                        window(B - 1, B * GP - 1)

            with ExitStack() as stage:
                sb = tensors(stage)
                pb = banks(stage)
                scores = sb("scores", [128, 4, KEYS])
                negmax = sb("negmax", [128, NB])
                probs = sb("probs", [128, NB // RB, KEYS, RB])
                total = sb("total", [128, NB])
                inverse = sb("inverse", [128, NB])
                main_t = sb("main_t", [MAIN, NB, 128])
                rest_t = sb("rest_t", [RB * REST, NB // RB, 128])
                v_main = sb("v_main", [MAIN, 2, NB, C])
                o_t = sb("o_t", [128, 2, QR * W])

                ps_s = [pb(f"ps_s{i}", [128, 512]) for i in range(2)]
                ps_m = [pb(f"ps_m{i}", [128, 512]) for i in range(2)]
                ps_r = pb("ps_r", [128, 512])
                ps_o = [pb(f"ps_o{i}", [128, 2, NB, Q]) for i in range(2)]
                ps_y = pb("ps_y", [128, 4, C])

                scored = sem("scored")
                biased = sem("biased")
                exponentiated = sem("exponentiated")
                inverted = sem("inverted")
                normalised = sem("normalised")
                turned = sem("turned")
                turned_out = sem("turned_out")
                rest_turned = sem("rest_turned")
                rest_out = sem("rest_out")
                weighed = sem("weighed")
                v_in = [sem(f"v_in{i}") for i in range(2)]
                o_out = sem("o_out")
                projected = sem("projected")
                added = sem("added")
                measured = sem("measured")
                bias_added = sem("bias_added")

                PB = SB // 2
                LN, LT, LC = 2, 3, 4

                def pairs(e, classes=False):
                    yield 0, 0, (0, 1)
                    with e.Fori(1, PB - 1 if classes else PB) as p:
                        yield 0, p, (1, 1)
                    if classes:
                        yield 0, PB - 1, (1, 2)
                        yield 1, PB, (0, 1)
                        with e.Fori(PB + 1, 2 * PB - 1) as p:
                            yield 1, p, (1, 1)
                        yield 1, 2 * PB - 1, (1, 2)
                    else:
                        with e.Fori(PB, 2 * PB) as p:
                            yield 1, p, (1, 1)

                BLOCKS = B * SB * NB
                STRIPS = B * SB

                def weigh(pe, n, j, k, s):
                    pe.wait_ge(turned_out, k + 1)
                    if j % RB == 0:
                        pe.wait_ge(rest_out, n * (NB // RB) + (j // RB + 1))
                    if j == 0:
                        pe.wait_ge(v_in[s], (n - s) * 40 + 80)
                        pe.wait_ge(o_out, n + 1)
                    for values, by_key in ((v_main, main_t[:, j, :]), (v_rest, rest_t[:, j // RB, :])):
                        for h in range(NH):
                            hd = slice(h * HD, (h + 1) * HD)
                            last = nc.tensor.matmul(ps_o[s][hd, 0, j, :], values[:, s, j, hd], by_key[:, hd],
                                                    start=(values is v_main), stop=(values is v_rest),
                                                    tile_position=(0, h * HD))
                    last.then_inc(weighed, 1)

                def turn(pe, n, j, k):
                    pe.wait_ge(normalised, k + 1)
                    wait(pe, turned_out, k - 1)
                    nc.tensor.transpose(ps_m[j % 2][0:MAIN, 0:128], probs[:, j // RB, 0:MAIN, j % RB], ident[:])\
                        .then_inc(turned, 1)
                    if j % RB == RB - 1:
                        wait(pe, rest_out, n * (NB // RB) + j // RB)
                        nc.tensor.transpose(ps_r[0:RB * REST, 0:128], probs[:, j // RB, MAIN:KEYS, :].rearrange("p k i -> p (k i)"), ident[:])\
                            .then_inc(rest_turned, 1)

                def project(pe, n, s):
                    pe.wait_ge(o_out, n + 3)
                    pe.wait_ge(added, n + 1)
                    for i in range(ST):
                        last = nc.tensor.matmul(ps_y[:, i, :], o_t[:, s, i * 128:(i + 1) * 128], wp[:],
                                                start=True, stop=True)
                    last.then_inc(projected, 1)

                with nc.Block() as block:
                    @block.gpsimd
                    def _(pool):
                        def add_bias(n):
                            pool.wait_ge(q_placed, n + 1)
                            nc.gpsimd.tensor_tensor(res[:, ds(n * ST, ST), :], res[:, ds(n * ST, ST), :],
                                                    bp[:].unsqueeze(1).broadcast_to([128, ST, C]), ALU.add)\
                                .then_inc(bias_added, 1)

                        def place(n, s):
                            wait(pool, scored, (n - 1) * NB)
                            wait(pool, bias_added, n)
                            place_queries(n, s)

                        pool.wait_ge(res_in, 16)
                        pool.wait_ge(bp_in, 16)
                        add_bias(0)
                        pool.wait_ge(bias_added, 1)
                        add_bias(1)
                        with pool.Fori(1, STRIPS // 2) as p:
                            for s in range(2):
                                place(p * 2 + s, s)
                                add_bias(p * 2 + s)

                    @block.sync
                    def _(sp):
                        sp.wait_ge(v_border_set, 16 * 2 * B)
                        sp.wait_ge(v_cleared, 1)
                        for b, p, _ in pairs(sp):
                            sp.wait_ge(v_windowed[b], 16 * GB // 2)
                            for s in range(2):
                                n = p * 2 + s
                                if not (isinstance(p, int) and p == 0):
                                    sp.wait_ge(weighed, (n - 1) * NB)
                                win = v_windows[b, 0, ds(n * QR - b * H, 1), :]
                                sp.dma_start(v_main[:, s], bass.AP(win.tensor, win.offset,
                                                                   [[C, MAIN], [HP * KC * C, NB], [1, C]]))\
                                    .then_inc(v_in[s], 16)
                                for i in range(RB):
                                    win = v_windows[b, i, ds(n * QR + (MR - b * H), 1), :]
                                    sp.dma_start(v_rest[i:RB * REST:RB, s, i:NB:RB, :],
                                                 bass.AP(win.tensor, win.offset,
                                                         [[C, REST], [RB * HP * KC * C, NB // RB], [1, C]]))\
                                        .then_inc(v_in[s], 16)

                    @block.tensor
                    def _(pe):
                        pe.sem_inc(projected, 2)
                        for b, p, _ in pairs(pe):
                            first = isinstance(p, int) and p == 0
                            for s in range(2):
                                n = p * 2 + s
                                for j in range(NB):
                                    k = n * NB + j
                                    if j == 0:
                                        pe.wait_ge(q_placed, n + 1)
                                    wait(pe, biased, k - 1)
                                    nc.tensor.matmul(
                                        ps_s[j % 2][:, 0:KEYS], q_heads[:, s, j, :],
                                        k_map[:, b, ds(n * QR - b * H, KR), j * QC:j * QC + KC],
                                        start=True, stop=True).then_inc(scored, 1)
                                    if not (first and s == 0):
                                        weigh(pe, n - 1, j, k - NB, 1 - s)
                                    if not (first and s == 0 and j < LT):
                                        turn(pe, n if j >= LT else n - 1, (j - LT) % NB, k - LT)
                                    if j == 3 and not first:
                                        project(pe, n - 2, s)
                        for i in range(LT, 0, -1):
                            turn(pe, STRIPS - 1, NB - i, BLOCKS - i)
                        project(pe, STRIPS - 2, 0)
                        for j in range(NB):
                            weigh(pe, STRIPS - 1, j, BLOCKS - NB + j, 1)
                        project(pe, STRIPS - 1, 1)

                    @block.vector
                    def _(dve):
                        dve.sem_inc(added, 1)

                        def invert(j, k):
                            dve.wait_ge(exponentiated, k + 1)
                            nc.vector.reciprocal(inverse[:, j:j + 1], total[:, j:j + 1]).then_inc(inverted, 1)

                        def normalise(j, k):
                            dve.wait_ge(inverted, k + 1)
                            nc.vector.tensor_scalar(probs[:, j // RB, :, j % RB], probs[:, j // RB, :, j % RB],
                                                    inverse[:, j:j + 1], None, ALU.mult).then_inc(normalised, 1)

                        def residual(n):
                            dve.wait_ge(projected, n + 3)
                            dve.wait_ge(bias_added, n + 1)
                            nc.vector.tensor_tensor(res[:, ds(n * ST, ST), :], ps_y[:, 0:ST, :],
                                                    res[:, ds(n * ST, ST), :], ALU.add).then_inc(added, 1)

                        def measure(n, i):
                            dve.wait_ge(added, n + 2)
                            nc.vector.bn_stats(
                                ln_stats[:, ds(n * ST + i, 1), :].rearrange("p t s -> p (t s)"),
                                res[:, ds(n * ST + i, 1), :].rearrange("p t c -> p (t c)")).then_inc(measured, 1)

                        for b, p, windows in pairs(dve, classes=True):
                            first = isinstance(p, int) and p == 0
                            for s in range(2):
                                n = p * 2 + s
                                for j in range(NB):
                                    k = n * NB + j
                                    c = 0 if j == 0 else 2 if j == NB - 1 else 1
                                    dve.wait_ge(scored, k + 1)
                                    if not (first and s == 0 and j < LN):
                                        invert((j - LN) % NB, k - LN)
                                    nc.vector.tensor_tensor_reduce(
                                        out=scores[:, j % 4, :], in0=ps_s[j % 2][:, 0:KEYS],
                                        in1=bias_tab[:, windows[s], c, :], scale=-1.0, scalar=3.0e38,
                                        op0=ALU.add, op1=ALU.min,
                                        accum_out=negmax[:, j:j + 1]).then_inc(biased, 1)
                                    if not (first and s == 0 and j < LN):
                                        normalise((j - LN) % NB, k - LN)
                                    if j == 5 and not first:
                                        residual(n - 2)
                                    if 5 < j <= 5 + ST and not first:
                                        measure(n - 2, j - 6)
                        for i in range(LN, 0, -1):
                            invert(NB - i, BLOCKS - i)
                            normalise(NB - i, BLOCKS - i)
                        for n in (STRIPS - 2, STRIPS - 1):
                            residual(n)
                            for i in range(ST):
                                measure(n, i)

                    @block.scalar
                    def _(act):
                        nc.scalar.preload_act_table(ACT.Exp)
                        act.sem_inc(o_out, 2)

                        def turned_copy(n, j, k):
                            act.wait_ge(turned, k + 1)
                            wait(act, weighed, k - (NB - 1))
                            nc.scalar.activation(main_t[:, j, :], ps_m[j % 2][0:MAIN, 0:128], ACT.Copy)\
                                .then_inc(turned_out, 1)
                            if j % RB == RB - 1:
                                act.wait_ge(rest_turned, n * (NB // RB) + (j // RB + 1))
                                nc.scalar.activation(rest_t[:, j // RB, :], ps_r[0:RB * REST, 0:128], ACT.Copy)\
                                    .then_inc(rest_out, 1)

                        def strip_out(n, s):
                            act.wait_ge(weighed, n * NB + NB)
                            act.wait_ge(projected, n + 1)
                            nc.scalar.activation(
                                o_t[:, s, :].rearrange("p (r j c) -> p j r c", r=QR, j=NB),
                                ps_o[s][:, 0].rearrange("p j (r c) -> p j r c", r=QR), ACT.Copy).then_inc(o_out, 1)

                        for b, p, _ in pairs(act):
                            first = isinstance(p, int) and p == 0
                            for s in range(2):
                                n = p * 2 + s
                                for j in range(NB):
                                    k = n * NB + j
                                    if not (first and s == 0 and j < LC):
                                        turned_copy(n if j >= LC else n - 1, (j - LC) % NB, k - LC)
                                    act.wait_ge(biased, k + 1)
                                    if not (first and s == 0) and j % RB == 0:
                                        act.wait_ge(rest_turned, n * (NB // RB) - (NB // RB - j // RB - 1))
                                    nc.scalar.activation(probs[:, j // RB, :, j % RB], scores[:, j % 4, :], ACT.Exp,
                                                         bias=negmax[:, j:j + 1], scale=-1.0,
                                                         accum_out=total[:, j:j + 1]).then_inc(exponentiated, 1)
                                    if j == 1 and not first:
                                        strip_out(n - 2, s)
                        for i in range(LC, 0, -1):
                            turned_copy(STRIPS - 1, NB - i, BLOCKS - i)
                        strip_out(STRIPS - 2, 0)
                        strip_out(STRIPS - 1, 1)

        with ExitStack() as stage:
            sb = tensors(stage)
            pb = banks(stage)
            z = sb("z", [128, 2, TG, C])
            z_t = sb("z_t", [128, 2, G])
            expo = sb("expo", [128, 2, 2, G])
            relu = sb("relu", [128, 2, 2, G])
            qk_t = sb("qk_t", [128, 2, 2, G])
            k_tok = sb("k_tok", [128, 2, TG, C])
            v_one = sb("v_one", [128, 2, TG, C + 1])
            weights = sb("weights", [128, 2, TG, 128])
            kv = sb("kv", [128, 2, TG + 1, C + 1])
            den = sb("den", [128, TG])

            z_shift = ln_diff

            ps_z = pb("ps_z", [128, TG, 128])
            ps_q = pb("ps1_q", [128, G])
            ps_k = pb("ps1_k", [128, G])
            ps_v = pb("ps1_v", [128, TG, C])
            ps_w = pb("ps_w", [128, TG, 128])
            ps_kv = pb("ps_kv", [128, 512])
            ps_n = pb("ps_n", [128, 512])
            ps_last = pb("ps_last", [128, 512])

            ln_step = sem("ln_step")
            ln_root = sem("ln_root")
            one_set = sem("one_set")
            shifted = sem("shifted")
            z_ready = sem("z_ready")
            z_turned = sem("z_turned")
            z_out = sem("z_out")
            clipped = sem("clipped")
            clip_begun = sem("clip_begun")
            qk_made = sem("qk_made")
            qk_read = sem("qk_read")
            q_ready = sem("q_ready")
            k_ready = sem("k_ready")
            v_made = sem("v_made")
            v_ready = sem("v_ready")
            k_turned = sem("k_turned")
            k_out2 = sem("k_out2")
            w_made = sem("w_made")
            w_masked = sem("w_masked")
            kv_made = sem("kv_made")
            kv_zeroed = sem("kv_zeroed")
            kv_step = sem("kv_step")
            n_made = sem("n_made")
            den_ready = sem("den_ready")
            res_ready = sem("res_ready")
            stats_ready = sem("stats_ready")

            KVC = C + 1

            def kv_bank(t):
                return ps_kv[:, t * KVC:(t + 1) * KVC] if t < 3 else ps_last[:, 0:KVC]

            def n_bank(t):
                return ps_n[:, t * KVC:(t + 1) * KVC] if t < 3 else ps_last[:, KVC:2 * KVC]

            def steps(e, ahead, step, between=None):
                ahead()
                step(0, 0)
                step(1, 1)
                for b in range(B):
                    if b and between:
                        between()
                    with e.Fori(b * GB // 2 + (b == 0), (b + 1) * GB // 2 - (b == B - 1)) as r:
                        step(r * 2, 0)
                        step(r * 2 + 1, 1)
                step(NG - 2, 0)
                step(NG - 1, 1)

            def is_first(g):
                return isinstance(g, int) and g == 0

            def is_last(g, n=1):
                return isinstance(g, int) and g >= NG - n

            with nc.Block() as block:
                @block.gpsimd
                def _(pool):
                    nc.gpsimd.memset(v_one[:], 1.0).then_inc(one_set, 1)
                    pool.wait_ge(one_set, 1)
                    pool.sem_inc(q_ready, 2)

                    def combine(g, s):
                        pool.wait_ge(qk_read, g * 2 + 3)
                        pool.sem_inc(clip_begun, 1)
                        nc.gpsimd.tensor_scalar(expo[:, s, 0, :], expo[:, s, 0, :], 1.0, None, ALU.min)\
                            .then_inc(clipped, 1)
                        pool.wait_ge(clipped, g + 1)
                        wait(pool, n_made, g)
                        nc.gpsimd.tensor_tensor(qk_t[:, s, 0, :], expo[:, s, 0, :], relu[:, s, 0, :], ALU.add)\
                            .then_inc(q_ready, 1)

                    def step(g, s):
                        if not is_last(g):
                            combine(g + 1, 1 - s)

                    steps(pool, lambda: combine(0, 0), step)

                @block.tensor
                def _(pe):
                    pe.sem_inc(n_made, 1)

                    def turn_z(g, s):
                        pe.wait_ge(z_ready, g + 1)
                        for i in range(TG):
                            last = nc.tensor.transpose(ps_z[:, i, :], z[:, s, i, :], ident[:])
                        last.then_inc(z_turned, 1)

                    def make_qk(g, s):
                        pe.wait_ge(z_out, g + 1)
                        for m, bank in ((0, ps_q), (1, ps_k)):
                            pe.wait_ge(qk_read, g * 2 + (m + 1))
                            nc.tensor.matmul(bank[:], attn_wt[:, m, :], z_t[:, s, :], start=True, stop=True)\
                                .then_inc(qk_made, 1)

                    def make_v(s):
                        for i in range(TG):
                            last = nc.tensor.matmul(ps_v[:, i, :], z_t[:, s, i * 128:(i + 1) * 128], attn_wt[:, 2, :],
                                                    start=True, stop=True)
                        last.then_inc(v_made, 1)

                    def ahead():
                        turn_z(0, 0)
                        make_qk(0, 0)
                        make_v(0)

                    def step(g, s):
                        if not is_last(g):
                            pe.wait_ge(k_out2, g + 1)
                            turn_z(g + 1, 1 - s)
                        pe.wait_ge(w_masked, g + 1)
                        pe.wait_ge(q_ready, g + 3)
                        pe.wait_ge(k_ready, g + 3)
                        for i in range(TG):
                            t = slice(i * 128, (i + 1) * 128)
                            last = nc.tensor.matmul(ps_w[:, i, :], qk_t[:, s, 1, t], qk_t[:, s, 0, t],
                                                    start=True, stop=True)
                        last.then_inc(w_made, 1)
                        if is_last(g):
                            pe.wait_ge(k_out2, g + 1)
                        else:
                            pe.wait_ge(z_out, g + 2)
                        for i in range(TG):
                            last = nc.tensor.transpose(ps_z[:, i, :], qk_t[:, s, 1, i * 128:(i + 1) * 128], ident[:])
                        last.then_inc(k_turned, 1)
                        if not is_last(g):
                            make_qk(g + 1, 1 - s)
                        if not is_first(g):
                            outputs(g - 1, 1 - s)
                        pe.wait_ge(v_ready, g + 1)
                        if not is_last(g):
                            make_v(1 - s)
                        pe.wait_ge(k_out2, g + 2)
                        for i in range(TG):
                            if i == TG - 1 and not is_first(g):
                                pe.wait_ge(res_ready, g * TG - (TG - 2))
                            last = nc.tensor.matmul(kv_bank(i), k_tok[:, s, i, :], v_one[:, s, i, :],
                                                    start=True, stop=True)
                        last.then_inc(kv_made, 1)

                    def outputs(g, s):
                        pe.wait_ge(w_masked, g + 2)
                        pe.wait_ge(kv_step, g * (TG + 1) + (TG + 1))
                        pe.wait_ge(res_ready, g * TG + 1)
                        for i in range(TG):
                            nc.tensor.matmul(n_bank(i), weights[:, s, i, :], v_one[:, s, i, :], start=True, stop=False)
                            last = nc.tensor.matmul(n_bank(i), qk_t[:, s, 0, i * 128:(i + 1) * 128], kv[:, s, i, :],
                                                    start=False, stop=True)
                        last.then_inc(n_made, 1)

                    steps(pe, ahead, step)
                    outputs(NG - 1, 1)

                @block.scalar
                def _(act):
                    layernorm_scalar(act, ln_step, ln_root)
                    nc.scalar.preload_act_table(ACT.Exp)
                    act.sem_inc(qk_read, 2)
                    act.sem_inc(k_out2, 1)
                    act.wait_ge(shifted, 1)

                    def normalise(g, s):
                        for i in range(TG):
                            t = g * TG + i
                            last = nc.scalar.activation(z[:, s, i, :], tile(res, t), ACT.Identity,
                                                        bias=z_shift[:, ds(t, 1)], scale=ln_rstd[:, ds(t, 1)])
                        last.then_inc(z_ready, 1)

                    def copy_z(g, s):
                        act.wait_ge(z_turned, g + 1)
                        nc.scalar.activation(z_t[:, s, :], ps_z[:].rearrange("p t c -> p (t c)"), ACT.Copy)\
                            .then_inc(z_out, 1)

                    def exponentials(g, s):
                        for m, bank, free in ((0, ps_q, q_ready), (1, ps_k, k_ready)):
                            act.wait_ge(qk_made, g * 2 + (m + 1))
                            act.wait_ge(free, g + 1)
                            nc.scalar.activation(expo[:, s, m, :], bank[:], ACT.Exp, bias=attn_bqk[:, m:m + 1])
                            nc.scalar.activation(relu[:, s, m, :], bank[:], ACT.Relu, bias=attn_bqk[:, m:m + 1])\
                                .then_inc(qk_read, 1)

                    def ahead():
                        normalise(0, 0)
                        copy_z(0, 0)
                        exponentials(0, 0)
                        normalise(1, 1)

                    def step(g, s):
                        if not is_last(g):
                            copy_z(g + 1, 1 - s)
                        act.wait_ge(k_turned, g + 1)
                        nc.scalar.activation(k_tok[:, s], ps_z[:], ACT.Copy).then_inc(k_out2, 1)
                        if not is_last(g):
                            exponentials(g + 1, 1 - s)
                        if not is_last(g, 2):
                            normalise(g + 2, s)

                    steps(act, ahead, step)

                @block.vector
                def _(dve):
                    layernorm_vector(dve, ln_step, ln_root)
                    dve.wait_ge(ln_step, 8)
                    nc.vector.scalar_tensor_tensor(out=z_shift[:], in0=ln_mean[:], scalar=-1.0, in1=ln_rstd[:],
                                                   op0=ALU.mult, op1=ALU.mult).then_inc(shifted, 1)
                    dve.wait_ge(one_set, 1)
                    dve.sem_inc(w_masked, 1)
                    dve.sem_inc(res_ready, 1)
                    dve.sem_inc(k_ready, 2)
                    nc.vector.memset(kv[:, 1, TG, :], 0.0).then_inc(kv_zeroed, 1)
                    dve.wait_ge(kv_zeroed, 1)

                    def combine(g, s):
                        dve.wait_ge(qk_read, g * 2 + 4)
                        nc.vector.scalar_tensor_tensor(out=qk_t[:, s, 1, :], in0=expo[:, s, 1, :], scalar=1.0,
                                                       in1=relu[:, s, 1, :], op0=ALU.min, op1=ALU.add)\
                            .then_inc(k_ready, 1)

                    def values(g, s):
                        dve.wait_ge(v_made, g + 1)
                        nc.vector.tensor_tensor(v_one[:, s, :, 0:C], ps_v[:],
                                                attn_bv[:].unsqueeze(1).broadcast_to([128, TG, C]), ALU.add)\
                            .then_inc(v_ready, 1)

                    def outputs(g):
                        dve.wait_ge(n_made, g + 2)
                        nc.vector.tensor_scalar(den[:, 0:3], ps_n[:, 0:3 * KVC]
                                                .rearrange("p (t c) -> p t c", c=KVC)[:, :, C],
                                                DEN_EPS, None, ALU.add).then_inc(den_ready, 1)
                        nc.vector.tensor_scalar(den[:, 3:4], ps_last[:, 2 * KVC - 1:2 * KVC], DEN_EPS, None, ALU.add)\
                            .then_inc(den_ready, 1)
                        dve.wait_ge(den_ready, g * 3 + 2)
                        nc.vector.reciprocal(den[:], den[:]).then_inc(den_ready, 1)
                        dve.wait_ge(den_ready, g * 3 + 3)
                        for i in reversed(range(TG)):
                            t = g * TG + i
                            nc.vector.scalar_tensor_tensor(out=tile(res, t), in0=n_bank(i)[:, 0:C],
                                                           scalar=den[:, i:i + 1], in1=tile(res, t),
                                                           op0=ALU.mult, op1=ALU.add).then_inc(res_ready, 1)

                    def statistics(g):
                        dve.wait_ge(res_ready, g * TG + (TG + 1))
                        for i in range(TG):
                            t = g * TG + i
                            nc.vector.bn_stats(tile(ln_stats, t), tile(res, t)).then_inc(stats_ready, 1)

                    def step(g, s):
                        dve.wait_ge(w_made, g + 1)
                        nc.vector.tensor_tensor(weights[:, s], ps_w[:],
                                                tri[:].unsqueeze(1).broadcast_to([128, TG, 128]), ALU.mult)\
                            .then_inc(w_masked, 1)
                        if not is_first(g):
                            outputs(g - 1)
                        if not is_last(g):
                            combine(g + 1, 1 - s)
                            values(g + 1, 1 - s)
                        if not is_first(g):
                            statistics(g - 1)
                        dve.wait_ge(kv_made, g + 1)
                        nc.vector.tensor_copy(kv[:, s, 0, :], kv[:, 1 - s, TG, :]).then_inc(kv_step, 1)
                        for i in range(TG):
                            dve.wait_ge(kv_step, g * (TG + 1) + (i + 1))
                            nc.vector.tensor_tensor(kv[:, s, i + 1, :], kv_bank(i), kv[:, s, i, :], ALU.add)\
                                .then_inc(kv_step, 1)
                        dve.wait_ge(kv_step, g * (TG + 1) + (TG + 1))

                    def new_batch():
                        nc.vector.memset(kv[:, 1, TG, :], 0.0).then_inc(kv_zeroed, 1)
                        dve.wait_ge(kv_zeroed, 2)

                    def ahead():
                        values(0, 0)
                        combine(0, 0)

                    steps(dve, ahead, step, new_batch)
                    outputs(NG - 1)
                    statistics(NG - 1)

        with ExitStack() as stage:
            sb = tensors(stage)
            w_scaled = sb("w_scaled", [128, C])
            wn_t = sb("wn_t", [128, C])
            z = sb("z4", [128, 2, TG, C])
            z_t = sb("z4_t", [128, L, COLS])
            states = sb("states", [128, L, COLS])
            bstats = sb("bstats", [128, NG, 6])
            bmv = sb("bmv", [128, 2])
            bvar = sb("bvar", [128, 1])
            bstd = sb("bstd", [128, 1])
            bscale = sb("bscale", [128, 1])
            bshift = sb("bshift", [128, 1])
            warm = sb("warm", [128, B, 2, CH])
            start = sb("start", [128, B, CH])
            gap = sb("gap", [128, B, CH])
            worst = sb("worst", [128, 1])
            worst_all = sb("worst_all", [1, 1])
            apart = sb("apart", [1, 1], i32)
            one_state = sb("one_state", [128, B])

            ln_step = sem("ln4_step")
            ln_root = sem("ln4_root")
            shifted = sem("shifted4")
            z_ready = sem("z4_ready")
            z_ready_v = sem("z4_ready_v")
            HALVES = TG // 2
            z_turned = sem("z4_turned")
            z_out = sem("z4_out")
            wx_made = sem("wx_made")
            wx_read = sem("wx_read")
            bn_step = sem("bn_step")
            bn_root = sem("bn_root")
            wn_turned = sem("wn_turned")
            wn_ready = sem("wn_ready")

            with ExitStack() as stage4:
                pb = banks(stage4)
                ps_z = [pb(f"ps4_z{i}", [128, TG, 128]) for i in range(2)]
                ps_x = [pb(f"ps4_x{i}", [128, G]) for i in range(2)]
                ps_w = pb("ps4_w", [128, C])
                with nc.Block() as block:
                    @block.tensor
                    def _(pe):

                        def turn(g, s):
                            pe.wait_ge(z_ready, g + 1)
                            pe.wait_ge(z_ready_v, g + 1)
                            pe.wait_ge(z_out, g + 1)
                            for i in range(TG):
                                last = nc.tensor.transpose(ps_z[s][:, i, :], z[:, s, i, :], ident[:])
                            last.then_inc(z_turned, 1)

                        def product(g, s):
                            pe.wait_ge(z_out, g + 3)
                            pe.wait_ge(wx_read, g + 1)
                            nc.tensor.matmul(ps_x[s][:], ffn_wt, z_t[:, :, ds(g * CG, CG)], start=True, stop=True)\
                                .then_inc(wx_made, 1)

                        turn(0, 0)
                        with pe.Fori(0, NG // 2 - 1) as r:
                            turn(r * 2 + 1, 1)
                            product(r * 2, 0)
                            turn(r * 2 + 2, 0)
                            product(r * 2 + 1, 1)
                        turn(NG - 1, 1)
                        product(NG - 2, 0)
                        product(NG - 1, 1)
                        pe.wait_ge(bn_step, 4)
                        nc.tensor.transpose(ps_w[:], w_scaled[:], ident[:]).then_inc(wn_turned, 1)

                    @block.scalar
                    def _(act):
                        layernorm_scalar(act, ln_step, ln_root)
                        act.sem_inc(z_out, 2)
                        act.wait_ge(shifted, 1)

                        def normalise(g, s):
                            for i in range(HALVES):
                                t = g * TG + i
                                last = nc.scalar.activation(z[:, s, i, :], tile(res, t), ACT.Identity,
                                                            bias=ln_diff[:, ds(t, 1)], scale=ln_rstd[:, ds(t, 1)])
                            last.then_inc(z_ready, 1)

                        normalise(0, 0)
                        normalise(1, 1)

                        def copy_z(g, s):
                            act.wait_ge(z_turned, g + 1)
                            nc.scalar.activation(z_t[:, :, ds(g * CG, CG)].rearrange("p s c -> p c s"),
                                                 ps_z[s][:].rearrange("p t (c s) -> p (t c) s", s=L), ACT.Copy)\
                                .then_inc(z_out, 1)

                        with act.Fori(0, NG // 2 - 1) as r:
                            for s in range(2):
                                copy_z(r * 2 + s, s)
                                normalise(r * 2 + (s + 2), s)
                        copy_z(NG - 2, 0)
                        copy_z(NG - 1, 1)
                        act.wait_ge(bn_step, 2)
                        nc.scalar.activation(bstd[:], bvar[:], ACT.Sqrt).then_inc(bn_root, 1)
                        act.wait_ge(wn_turned, 1)
                        nc.scalar.activation(wn_t[:], ps_w[:], ACT.Copy).then_inc(wn_ready, 1)

                    @block.vector
                    def _(dve):
                        layernorm_vector(dve, ln_step, ln_root)
                        dve.wait_ge(ln_step, 8)
                        nc.vector.scalar_tensor_tensor(out=ln_diff[:], in0=ln_mean[:], scalar=-1.0, in1=ln_rstd[:],
                                                       op0=ALU.mult, op1=ALU.mult).then_inc(shifted, 1)
                        dve.sem_inc(wx_read, 2)

                        def normalise(g, s):
                            for i in range(HALVES, TG):
                                t = g * TG + i
                                last = nc.vector.tensor_scalar(z[:, s, i, :], tile(res, t),
                                                               ln_mean[:, ds(t, 1)], ln_rstd[:, ds(t, 1)],
                                                               ALU.subtract, ALU.mult)
                            last.then_inc(z_ready_v, 1)

                        def statistics(g, s):
                            dve.wait_ge(wx_made, g + 1)
                            nc.vector.bn_stats(tile(bstats, g), ps_x[s][:]).then_inc(wx_read, 1)

                        normalise(0, 0)
                        normalise(1, 1)
                        with dve.Fori(0, NG // 2 - 1) as r:
                            for s in range(2):
                                dve.wait_ge(z_turned, r * 2 + (s + 1))
                                normalise(r * 2 + (s + 2), s)
                                statistics(r * 2 + s, s)
                        statistics(NG - 2, 0)
                        statistics(NG - 1, 1)
                        dve.wait_ge(wx_read, NG + 2)
                        nc.vector.bn_aggr(bmv[:], bstats[:].rearrange("p g s -> p (g s)")).then_inc(bn_step, 1)
                        dve.wait_ge(bn_step, 1)
                        nc.vector.tensor_scalar(bvar[:], bmv[:, 1:2], BN_EPS, None, ALU.add).then_inc(bn_step, 1)
                        dve.wait_ge(bn_root, 1)
                        nc.vector.reciprocal(bscale[:], bstd[:]).then_inc(bn_step, 1)
                        dve.wait_ge(bn_step, 3)
                        nc.vector.tensor_scalar(w_scaled[:], weights1[:, 3, :], bscale[:], gamma_c[:], ALU.mult, ALU.mult)\
                            .then_inc(bn_step, 1)
                        nc.vector.scalar_tensor_tensor(out=bshift[:], in0=bmv[:, 0:1], scalar=bscale[:],
                                                       in1=gamma_c[:], op0=ALU.mult, op1=ALU.mult).then_inc(bn_step, 1)
                        dve.wait_ge(bn_step, 5)
                        nc.vector.tensor_tensor(bshift[:], beta_c[:], bshift[:], ALU.subtract).then_inc(bn_step, 1)

            middling = sem("middling")
            warmed = [sem(f"warmed{b}") for b in range(B)]
            warm_made = [sem(f"warm_made{b}") for b in range(B)]
            started = sem("started")
            step_made = [sem(f"step_made{b}") for b in range(B)]
            step_done = [sem(f"step_done{b}") for b in range(B)]
            seam_step = sem("seam_step")
            gap_turned = sem("gap_turned")
            apart_set = sem("apart_set")
            single_made = sem("single_made")
            single_done = sem("single_done")
            single_start = sem("single_start")
            with ExitStack() as stage5:
                pb = banks(stage5)
                ps_r = [[pb(f"ps_r{b}{i}", [128, 512]) for i in range(2)] for b in range(B)]
                ps_1 = pb("ps_one", [128, 512])
                U = 6
                assert WARM % U == 0 and (L - 2) % U == 0

                def half(a, t, b):
                    return tile(a, t)[:, b * CH:(b + 1) * CH]

                with nc.Block() as block:
                    @block.tensor
                    def _(pe):
                        def step(b, s, x_cols, y, ahead, made):
                            nc.tensor.matmul(ps_r[b][s][:, 0:CH], wn_t[:], x_cols, start=True, stop=False)
                            pe.wait_ge(*ahead)
                            nc.tensor.matmul(ps_r[b][s][:, 0:CH], v_t, y, start=False, stop=True).then_inc(made, 1)

                        pe.wait_ge(middling, 1)
                        with pe.Fori(0, WARM // U) as r:
                            for u in range(U):
                                for b in range(B):
                                    step(b, u % 2, half(z_t, r * U + (u + L - WARM), b), warm[:, b, u % 2, :],
                                         (warmed[b], r * U + (u + 1)), warm_made[b])

                        for b in range(B):
                            pe.wait_ge(warmed[b], WARM + 1)
                            step(b, 0, z_t[:, 0, b * CH:(b + 1) * CH], start[:, b, :], (started, 1), step_made[b])
                        for b in range(B):
                            step(b, 1, z_t[:, 1, b * CH:(b + 1) * CH], states[:, 0, b * CH:(b + 1) * CH],
                                 (step_done[b], 1), step_made[b])
                        with pe.Fori(0, (L - 2) // U) as r:
                            for u in range(U):
                                for b in range(B):
                                    step(b, u % 2, half(z_t, r * U + (u + 2), b), half(states, r * U + (u + 1), b),
                                         (step_done[b], r * U + (u + 2)), step_made[b])
                        pe.wait_ge(seam_step, 3)
                        nc.tensor.transpose(ps_1[0:1, 0:128], worst[:], ident[:]).then_inc(gap_turned, 1)

                    @block.scalar
                    def _(act):
                        nc.scalar.preload_act_table(ACT.Sigmoid)
                        for b in range(B):
                            act.sem_inc(warmed[b], 1)
                        with act.Fori(0, WARM // U) as r:
                            for u in range(U):
                                for b in range(B):
                                    act.wait_ge(warm_made[b], r * U + (u + 1))
                                    nc.scalar.activation(warm[:, b, 1 - u % 2, :], ps_r[b][u % 2][:, 0:CH], ACT.Sigmoid,
                                                         bias=bshift[:]).then_inc(warmed[b], 1)
                        with act.Fori(0, L // 8) as r:
                            for u in range(8):
                                for b in range(B):
                                    act.wait_ge(step_made[b], r * 8 + (u + 1))
                                    nc.scalar.activation(half(states, r * 8 + u, b), ps_r[b][u % 2][:, 0:CH], ACT.Sigmoid,
                                                         bias=bshift[:]).then_inc(step_done[b], 1)

                    @block.vector
                    def _(dve):
                        nc.vector.memset(warm[:, :, 0, :], 0.5).then_inc(middling, 1)
                        nc.vector.memset(start[:], 0.0).then_inc(seam_step, 1)
                        for b in range(B):
                            dve.wait_ge(warmed[b], WARM + 1)
                        dve.wait_ge(seam_step, 1)
                        nc.vector.tensor_copy(start[:, :, 1:CH], warm[:, :, 0, 0:CH - 1]).then_inc(started, 1)
                        for b in range(B):
                            dve.wait_ge(step_done[b], L)
                        nc.vector.tensor_tensor(gap[:], states[:, L - 1, :].rearrange("p (b c) -> p b c", b=B),
                                                warm[:, :, 0, :], ALU.subtract).then_inc(seam_step, 1)
                        dve.wait_ge(seam_step, 2)
                        nc.vector.tensor_reduce(worst[:], gap[:].rearrange("p b c -> p (b c)"), AX.X, ALU.max,
                                                apply_absolute_value=True).then_inc(seam_step, 1)
                        dve.wait_ge(gap_turned, 1)
                        nc.vector.tensor_reduce(worst_all[:], ps_1[0:1, 0:128], AX.X, ALU.max).then_inc(seam_step, 1)
                        dve.wait_ge(seam_step, 4)
                        nc.vector.tensor_scalar(apart[:], worst_all[:], AGREE, None, ALU.is_gt).then_inc(apart_set, 1)

                with nc.Block() as block:
                    @block.tensor
                    def _(pe):
                        flag = pe.alloc_register("pe_apart")
                        pe.reg_load(flag, apart[0:1, 0:1])
                        with pe.If_ne(flag, 0):
                            pe.wait_ge(single_start, 1)
                            with pe.Fori(0, CH) as c:
                                with pe.Fori(0, L) as i:
                                    cols = z_t[:, ds(i, 1), :].rearrange("p s (b c) -> p (s b) c", b=B)[:, :, ds(c, 1)]\
                                        .rearrange("p b c -> p (b c)")
                                    pe.wait_ge(single_done, c * L + i + 1)
                                    nc.tensor.matmul(ps_1[:, 0:B], wn_t[:], cols, start=True, stop=False)
                                    nc.tensor.matmul(ps_1[:, 0:B], v_t, one_state[:], start=False, stop=True)\
                                        .then_inc(single_made, 1)

                    @block.scalar
                    def _(act):
                        flag = act.alloc_register("act_apart")
                        act.reg_load(flag, apart[0:1, 0:1])
                        with act.If_ne(flag, 0):
                            act.wait_ge(single_start, 1)
                            act.sem_inc(single_done, 1)
                            with act.Fori(0, CH) as c:
                                with act.Fori(0, L) as i:
                                    act.wait_ge(single_made, c * L + i + 1)
                                    cols = states[:, ds(i, 1), :].rearrange("p s (b c) -> p (s b) c", b=B)\
                                        [:, :, ds(c, 1)].rearrange("p b c -> p (b c)")
                                    nc.scalar.activation(cols, ps_1[:, 0:B], ACT.Sigmoid, bias=bshift[:])
                                    nc.scalar.activation(one_state[:], ps_1[:, 0:B], ACT.Sigmoid, bias=bshift[:])\
                                        .then_inc(single_done, 1)

                    @block.vector
                    def _(dve):
                        nc.vector.memset(one_state[:], 0.0).then_inc(single_start, 1)

            with ExitStack() as stage6:
                pb = banks(stage6)
                sb = tensors(stage6)
                y_t = sb("y_t", [128, 2, CG, L])
                y_out = sb("y_out", [128, 4, TG, C])
                ps_y = [pb(f"ps6_y{i}", [128, TG, 128]) for i in range(2)]
                y_ready = sem("y_ready")
                y_turned = sem("y_turned")
                y_added = sem("y_added")
                y_stored = [sem(f"y_stored{i}") for i in range(4)]
                with nc.Block() as block:
                    @block.scalar
                    def _(act):
                        act.sem_inc(y_turned, 2)
                        with act.Fori(0, NG // 2) as r:
                            for s in range(2):
                                act.wait_ge(y_turned, r * 2 + (s + 1))
                                nc.scalar.activation(
                                    y_t[:, s], states[:, :, ds(r * (2 * CG) + s * CG, CG)]
                                    .rearrange("p s c -> p c s"), ACT.Copy).then_inc(y_ready, 1)

                    @block.tensor
                    def _(pe):
                        with pe.Fori(0, NG // 2) as r:
                            for s in range(2):
                                pe.wait_ge(y_ready, r * 2 + (s + 1))
                                pe.wait_ge(y_added, r * 2 + (s + 1))
                                flat = y_t[:, s].rearrange("p c s -> p (c s)")
                                for i in range(TG):
                                    last = nc.tensor.transpose(ps_y[s][:, i, :], flat[:, i * 128:(i + 1) * 128],
                                                               ident[:])
                                last.then_inc(y_turned, 1)

                    @block.vector
                    def _(dve):
                        dve.sem_inc(y_added, 2)
                        with dve.Fori(0, NG // 4) as r:
                            for s in range(4):
                                dve.wait_ge(y_turned, r * 4 + (s + 3))
                                dve.wait_ge(y_stored[s], r * 16 + 16)
                                nc.vector.tensor_tensor(y_out[:, s], ps_y[s % 2][:],
                                                        res[:, ds(r * (4 * TG) + s * TG, TG), :], ALU.add)\
                                    .then_inc(y_added, 1)

                    @block.sync
                    def _(sp):
                        for s in range(4):
                            sp.sem_inc(y_stored[s], 16)
                        with sp.Fori(0, NG // 4) as r:
                            for s in range(4):
                                sp.wait_ge(y_added, r * 4 + (s + 3))
                                sp.dma_start(out_tok[:, ds(r * (4 * TG) + s * TG, TG), :], y_out[:, s])\
                                    .then_inc(y_stored[s], 16)
                        for s in range(4):
                            sp.wait_ge(y_stored[s], 16 * (NG // 4 + 1))


_INS = ["x", "L0_conv_w_qkv", "L0_conv_b_qkv", "L0_conv_rpb", "L0_conv_w_proj", "L0_conv_b_proj",
        "L1_attn_W", "L1_attn_b", "L1_ffn_W", "L1_ffn_V", "L1_ffn_gamma", "L1_ffn_beta"]


def _window_mask():
    import numpy as np

    size, k, qr, qc, heads = 64, 7, 4, 8, 4
    kr, kc = qr + k - 1, qc + k - 1

    def inside(first, n, keys):
        at = first + np.arange(n)
        start = np.clip(at - k // 2, 0, size - k)
        key = first - k // 2 + np.arange(keys)
        return (key[None] >= start[:, None]) & (key[None] < start[:, None] + k)

    rows = [inside(f, qr, kr) for f in (0, qr, size - qr)]
    cols = [inside(f, qc, kc) for f in (0, qc, size - qc)]
    mask = np.empty((heads, qr, qc, 3, 3, kr, kc), np.float32)
    for a, r in enumerate(rows):
        for b, c in enumerate(cols):
            both = r[:, None, :, None] & c[None, :, None, :]
            mask[:, :, :, a, b] = np.where(both, 0.0, -1e30)
    return mask.reshape(128, 3, 3, kr * kc)


def _constants():
    import numpy as np

    group = np.kron(np.eye(32), np.full((4, 4), 0.25)).astype(np.float32)
    return {"window_mask": _window_mask(), "group_mean": group, "identity": np.eye(128, dtype=np.float32),
            "causal": np.triu(np.ones((128, 128), np.float32))}


def kernel(**inputs):
    import numpy as np
    import concourse.bacc as bacc
    from concourse import mybir
    from concourse.bass_utils import run_bass_kernel_spmd

    nc = bacc.Bacc("TRN2", target_bir_lowering=False, num_devices=1)
    arrays, args = {}, []
    for name, a in [(n, inputs[n]) for n in _INS] + list(_constants().items()):
        a = np.ascontiguousarray(a)
        arrays[f"in_{name}"] = a
        args.append(nc.dram_tensor(f"in_{name}", a.shape, mybir.dt.from_np(a.dtype), kind="ExternalInput").ap())
    args.append(nc.dram_tensor("out_0", (2, 64, 64, 128), mybir.dt.float32, kind="ExternalOutput").ap())
    neighborhood_attention_linear_attention_rnn_kernel(nc, *args)
    r = run_bass_kernel_spmd(nc, [arrays], core_ids=[0])
    return r.results[0]["out_0"]
```

```python
import concourse.bass as bass
from concourse import mybir
from contextlib import ExitStack


def neighborhood_attention_linear_attention_rnn_kernel(
    nc: bass.Bass,
    x: bass.AP,
    w_qkv: bass.AP,
    b_qkv: bass.AP,
    rpb: bass.AP,
    w_proj: bass.AP,
    b_proj: bass.AP,
    attn_w: bass.AP,
    attn_b: bass.AP,
    ffn_w: bass.AP,
    ffn_v: bass.AP,
    gamma: bass.AP,
    beta: bass.AP,
    window_mask: bass.AP,
    group_mean: bass.AP,
    identity: bass.AP,
    causal: bass.AP,
    out: bass.AP,
):
    f32 = mybir.dt.float32
    i32 = mybir.dt.int32
    ALU = mybir.AluOpType
    ACT = mybir.ActivationFunctionType
    AX = mybir.AxisListType
    ds = bass.ds

    B, H, W, C = 2, 64, 64, 128
    NH, K = 4, 7
    HD = C // NH
    SCALE = HD ** -0.5
    PAD = K // 2
    HP, WP = H + 2 * PAD, W + 2 * PAD
    T = H * W
    NT = B * T // 128
    QR, QC = 4, 8
    Q = QR * QC
    KR, KC = QR + K - 1, QC + K - 1
    KEYS = KR * KC
    MR = 128 // KC - 1
    MAIN = MR * KC
    REST = KEYS - MAIN
    RB = 4
    NB = W // QC
    SB = H // QR
    ST = QR * W // 128
    GN_EPS, LN_EPS, BN_EPS, DEN_EPS = 1e-5, 1e-5, 1e-5, 1e-6
    G = 512
    NG = B * T // G
    GB = T // G
    GR = G // W
    TG = G // 128
    CH = 128
    L = T // CH
    WARM = 12
    COLS = B * CH
    CG = G // L
    AGREE = 2.0 ** -21

    def row(v):
        return v.rearrange("(a n) -> a n", a=1)

    def column(v):
        return v.rearrange("(p a) -> p a", a=1)

    def tile(a, t):
        return a[:, bass.ds(t, 1), :].rearrange("p t c -> p (t c)")

    def wait(e, s, value):
        if not isinstance(value, int) or value > 0:
            e.wait_ge(s, value)

    with ExitStack() as whole:
        def tensors(stack):
            return lambda name, shape, dt=f32: stack.enter_context(nc.sbuf_tensor(name, shape, dt))

        def banks(stack):
            return lambda name, shape: stack.enter_context(nc.psum_tensor(name, shape, f32))

        def sem(name):
            return whole.enter_context(nc.semaphore(name))

        v_map = nc.dram_tensor("v_map", (B, H, WP, C), f32, kind="Internal").ap()
        v_windows = nc.dram_tensor("v_windows", (B, NB, HP, KC * C), f32, kind="Internal").ap()
        rpb_pad = nc.dram_tensor("rpb_pad", (NH, 2 * K - 1, KC + QC - 1), f32, kind="Internal").ap()

        sb = tensors(whole)
        res = sb("res", [128, NT, C])
        ident = sb("ident", [128, 128])
        ln_stats = sb("ln_stats", [128, NT, 6])
        ln_diff = sb("ln_diff", [128, NT])
        ln_var = sb("ln_var", [128, NT])
        ln_std = sb("ln_std", [128, NT])
        ln_mean = sb("ln_mean", [128, NT])
        ln_rstd = sb("ln_rstd", [128, NT])
        weights1 = sb("weights1", [128, 5, C])
        weights1_t = sb("weights1_t", [128, 5, C])
        attn_wt, ffn_wt, v_t = weights1_t[:, 0:3, :], weights1_t[:, 3, :], weights1_t[:, 4, :]
        attn_bqk = sb("attn_bqk", [128, 2])
        attn_bv = sb("attn_bv", [128, C])
        tri = sb("tri", [128, 128])
        gamma_c = sb("gamma_c", [128, 1])
        beta_c = sb("beta_c", [128, 1])
        weights1_in = sem("weights1_in")
        weights1_turned = sem("weights1_turned")
        weights1_ready = sem("weights1_ready")

        x_tok = x.rearrange("b h w c -> (b h w) c").rearrange("(t p) c -> p t c", p=128)
        out_tok = out.rearrange("b h w c -> (b h w) c").rearrange("(t p) c -> p t c", p=128)

        EARLY, LATE = slice(0, NT - TG), slice(NT - TG, NT)
        ln_step = [sem(f"ln_step{i}") for i in range(2)]
        ln_root = [sem(f"ln_root{i}") for i in range(2)]
        LN_STEPS = 9

        def layernorm_vector(dve, norm, part):
            step, before, t = ln_step[norm], part * LN_STEPS, (EARLY, LATE)[part]
            me, mo = ln_stats[:, t, 1], ln_stats[:, t, 4]
            se, so = ln_stats[:, t, 2], ln_stats[:, t, 5]
            diff, mean, var, std, rstd = ln_diff[:, t], ln_mean[:, t], ln_var[:, t], ln_std[:, t], ln_rstd[:, t]
            nc.vector.tensor_tensor(diff, me, mo, ALU.subtract).then_inc(step, 1)
            nc.vector.tensor_tensor(mean, me, mo, ALU.add).then_inc(step, 1)
            nc.vector.tensor_tensor(var, se, so, ALU.add).then_inc(step, 1)
            dve.wait_ge(step, before + 3)
            nc.vector.tensor_tensor(diff, diff, diff, ALU.mult).then_inc(step, 1)
            nc.vector.tensor_scalar(var, var, 1.0 / C, LN_EPS, ALU.mult, ALU.add).then_inc(step, 1)
            nc.vector.tensor_scalar(mean, mean, 0.5, None, ALU.mult).then_inc(step, 1)
            dve.wait_ge(step, before + 6)
            nc.vector.scalar_tensor_tensor(out=var, in0=diff, scalar=0.25, in1=var,
                                           op0=ALU.mult, op1=ALU.add).then_inc(step, 1)
            dve.wait_ge(ln_root[norm], part + 1)
            nc.vector.reciprocal(rstd, std).then_inc(step, 1)
            dve.wait_ge(step, before + 8)
            nc.vector.scalar_tensor_tensor(out=ln_diff[:, t], in0=mean, scalar=-1.0, in1=rstd,
                                           op0=ALU.mult, op1=ALU.mult).then_inc(step, 1)

        def layernorm_scalar(act, norm, part):
            t = (EARLY, LATE)[part]
            act.wait_ge(ln_step[norm], part * LN_STEPS + 7)
            nc.scalar.activation(ln_std[:, t], ln_var[:, t], ACT.Sqrt).then_inc(ln_root[norm], 1)

        with ExitStack() as layer0:
            sb = tensors(layer0)
            q_map = sb("q_map", [128, B * H, W])
            k_map = sb("k_map", [128, B, HP, WP])
            bias_tab = sb("bias_tab", [128, 3, 3, KEYS])
            wp = sb("wp", [128, C])
            bp = sb("bp", [128, C])
            q_heads = sb("q_heads", [128, 2, NB, 128])
            v_rest = sb("v_rest", [RB * REST, 2, NB, C])
            q_cleared = sem("q_cleared")

            q_placed = sem("q_placed")
            v_stored = [sem(f"v_stored{i}") for i in range(2)]
            v_border_set = sem("v_border_set")
            v_side_set = sem("v_side_set")
            v_windowed = [sem(f"v_windowed{b}") for b in range(B)]
            v_cleared = sem("v_cleared")
            res_in = sem("res_in")
            bp_in = sem("bp_in")
            wp_in = sem("wp_in")

            GP = GB // 2

            def window(sp, b, r):
                for s in range(2):
                    sp.wait_ge(v_stored[s], r * 32 + 64)
                rows = v_map[b, ds(r * (2 * GR) - b * H, 1), 0, :]
                wins = v_windows[b, 0, ds(r * (2 * GR) + (PAD - b * H), 1), :]
                sp.dma_start(bass.AP(wins.tensor, wins.offset,
                                     [[HP * KC * C, NB], [KC * C, 2 * GR], [1, KC * C]]),
                             bass.AP(rows.tensor, rows.offset,
                                     [[QC * C, NB], [WP * C, 2 * GR], [1, KC * C]]))\
                    .then_inc(v_windowed[b], 16)

            def place_queries(n, s):
                for h in range(NH):
                    hd = slice(h * HD, (h + 1) * HD)
                    last = nc.gpsimd.tensor_copy(
                        q_heads[hd, s, :, hd].rearrange("p j (r c) -> p r j c", r=QR),
                        q_map[hd, ds(n * QR, QR), :].rearrange("p r (j c) -> p r j c", j=NB))
                last.then_inc(q_placed, 1)

            with ExitStack() as stage:
                sb = tensors(stage)
                pb = banks(stage)
                XS = 8
                x_stage = sb("x_stage", [128, XS, TG, C])
                x_t = sb("x_t", [128, B * T])
                gm = sb("gm", [128, 128])
                wqkv = sb("wqkv", [128, 3 * C])
                wn = sb("wn", [128, B, 3 * C])
                bqk = sb("bqk", [128, 2])
                bqk_n = sb("bqk_n", [128, B, 2])
                bv = sb("bv", [128, C])
                bv_n = sb("bv_n", [128, B, C])
                gstats = sb("gstats", [128, NG, 6])
                moments = sb("moments", [128, B, 2])
                group = sb("group", [128, B, 2])
                gsq = sb("gsq", [128, B])
                gstd = sb("gstd", [128, B])
                gscale = sb("gscale", [128, B])
                gshift = sb("gshift", [128, B])
                gshift_cols = sb("gshift_cols", [128, B, 128])
                zeros = sb("zeros", [128, PAD * C])
                v_tok = sb("v_tok", [128, 2, TG, C])
                toeplitz = sb("toeplitz", [128, KEYS])
                x_now = sb("x_now", [128, 2, G])

                ps_t = [pb(f"ps_t{i}", [128, G]) for i in range(2)]
                ps_q = pb("ps_q", [128, G])
                ps_k = pb("ps_k", [128, G])
                ps_v = [pb(f"ps_v{i}", [128, TG, C]) for i in range(2)]
                ps_g = pb("ps_g", [128, G])

                ident_in = sem("ident_in")
                weights_in = sem("weights_in")
                x_in = [sem(f"x_in{i}") for i in range(XS)]
                transposed = sem("transposed")
                xt_ready = sem("xt_ready")
                gn_stats = sem("gn_stats")
                gn_step = sem("gn_step")
                gn_group = sem("gn_group")
                gn_root = sem("gn_root")
                gn_fold = sem("gn_fold")
                zero_set = sem("zero_set")
                k_border_set = sem("k_border_set")
                rpb_zeroed = sem("rpb_zeroed")
                rpb_placed = sem("rpb_placed")
                toeplitz_in = sem("toeplitz_in")
                mask_in = sem("mask_in")
                bias_built = sem("bias_built")
                folded = sem("folded")
                bias_mm = sem("bias_mm")
                bias_folded = sem("bias_folded")
                staged = sem("staged")
                qk_mm = sem("qk_mm")
                v_mm = sem("v_mm")
                q_out = sem("q_out")
                k_out = sem("k_out")
                v_out = sem("v_out")

                with nc.Block() as block:
                    @block.sync
                    def _(sp):
                        sp.dma_start(ident[:], identity).then_inc(ident_in, 16)
                        for s in range(XS):
                            sp.dma_start(x_stage[:, s], x_tok[:, s * TG:(s + 1) * TG, :]).then_inc(x_in[s], 16)
                        with sp.Fori(1, NG // XS) as r:
                            for s in range(XS):
                                sp.wait_ge(transposed, r * XS + (s - XS + 1))
                                sp.dma_start(x_stage[:, s], x_tok[:, ds(r * (XS * TG) + s * TG, TG), :])\
                                    .then_inc(x_in[s], 16)
                        sp.wait_ge(zero_set, 1)
                        sp.dma_start(rpb_pad.rearrange("h a b -> (h a) b"),
                                     zeros[0:NH * (2 * K - 1), 0:KC + QC - 1]).then_inc(rpb_zeroed, 16)
                        sp.wait_ge(rpb_zeroed, 16)
                        sp.dma_start(rpb_pad[:, :, QC - PAD - 1:QC - PAD - 1 + 2 * K - 1], rpb)\
                            .then_inc(rpb_placed, 16)
                        sp.dma_start(weights1[:, 0:3, :], attn_w.rearrange("(m p) c -> p m c", p=128))\
                            .then_inc(weights1_in, 16)
                        sp.dma_start(weights1[:, 3, :], ffn_w).then_inc(weights1_in, 16)
                        sp.dma_start(weights1[:, 4, :], ffn_v).then_inc(weights1_in, 16)
                        sp.dma_start(attn_bqk[:, 0:1], column(attn_b[0:C])).then_inc(weights1_in, 16)
                        sp.dma_start(attn_bqk[:, 1:2], column(attn_b[C:2 * C])).then_inc(weights1_in, 16)
                        sp.dma_start(attn_bv[:], row(attn_b[2 * C:3 * C]).partition_broadcast(128))\
                            .then_inc(weights1_in, 16)
                        sp.dma_start(tri[:], causal).then_inc(weights1_in, 16)
                        sp.dma_start(gamma_c[:], column(gamma)).then_inc(weights1_in, 16)
                        sp.dma_start(beta_c[:], column(beta)).then_inc(weights1_in, 16)
                        sp.dma_start(wp[:], w_proj).then_inc(wp_in, 16)
                        sp.dma_start(bp[:], row(b_proj).partition_broadcast(128)).then_inc(bp_in, 16)

                    @block.scalar
                    def _(act):
                        act.sem_inc(xt_ready, 2)
                        nc.scalar.preload_act_table(ACT.Identity)
                        with act.Fori(0, NG // 2) as r:
                            for s in range(2):
                                act.wait_ge(transposed, r * 2 + (s + 1))
                                nc.scalar.activation(x_t[:, ds(r * (2 * G) + s * G, G)], ps_t[s][:],
                                                     ACT.Identity).then_inc(xt_ready, 1)
                        nc.scalar.preload_act_table(ACT.Sqrt)
                        act.wait_ge(gn_step, 5)
                        nc.scalar.activation(gstd[:], gsq[:], ACT.Sqrt).then_inc(gn_root, 1)
                        nc.scalar.preload_act_table(ACT.Identity)

                    @block.tensor
                    def _(pe):
                        pe.wait_ge(ident_in, 16)
                        with pe.Fori(0, NG // XS) as r:
                            for s in range(XS):
                                pe.wait_ge(x_in[s], r * 16 + 16)
                                pe.wait_ge(xt_ready, r * XS + (s + 1))
                                for i in range(TG):
                                    last = nc.tensor.transpose(ps_t[s % 2][:, i * 128:(i + 1) * 128],
                                                               x_stage[:, s, i, :], ident[:])
                                last.then_inc(transposed, 1)
                        pe.wait_ge(weights_in, 16 * 5)
                        pe.wait_ge(gn_step, 4)
                        nc.tensor.matmul(ps_g[:, 0:2 * B], gm[:], moments[:].rearrange("p b m -> p (b m)"),
                                         start=True, stop=True).then_inc(gn_group, 1)

                    @block.vector
                    def _(dve):
                        with dve.Fori(0, NG) as g:
                            dve.wait_ge(xt_ready, g + 3)
                            nc.vector.bn_stats(gstats[:, ds(g, 1), :], x_t[:, ds(g * G, G)]).then_inc(gn_stats, 1)
                        dve.wait_ge(gn_stats, NG)
                        for b in range(B):
                            nc.vector.bn_aggr(moments[:, b, :], gstats[:, b * GB:(b + 1) * GB, :]
                                              .rearrange("p g s -> p (g s)")).then_inc(gn_step, 1)
                        dve.wait_ge(gn_step, 2)
                        nc.vector.tensor_tensor(gsq[:], moments[:, :, 0], moments[:, :, 0], ALU.mult)\
                            .then_inc(gn_step, 1)
                        dve.wait_ge(gn_step, 3)
                        nc.vector.tensor_tensor(moments[:, :, 1], moments[:, :, 1], gsq[:], ALU.add)\
                            .then_inc(gn_step, 1)
                        dve.wait_ge(gn_group, 1)
                        nc.vector.tensor_copy(group[:].rearrange("p b m -> p (b m)"), ps_g[:, 0:2 * B])\
                            .then_inc(gn_fold, 1)
                        dve.wait_ge(gn_fold, 1)
                        nc.vector.tensor_tensor(gstd[:], group[:, :, 0], group[:, :, 0], ALU.mult).then_inc(gn_fold, 1)
                        nc.vector.tensor_scalar(gshift[:], group[:, :, 1], GN_EPS, None, ALU.add).then_inc(gn_fold, 1)
                        dve.wait_ge(gn_fold, 3)
                        nc.vector.tensor_tensor(gsq[:], gshift[:], gstd[:], ALU.subtract).then_inc(gn_step, 1)
                        dve.wait_ge(gn_root, 1)
                        nc.vector.reciprocal(gscale[:], gstd[:]).then_inc(gn_step, 1)
                        dve.wait_ge(gn_step, 6)
                        nc.vector.scalar_tensor_tensor(out=gshift[:], in0=group[:, :, 0], scalar=-1.0,
                                                       in1=gscale[:], op0=ALU.mult, op1=ALU.mult).then_inc(gn_step, 1)
                        dve.wait_ge(gn_step, 7)
                        nc.vector.tensor_copy(gshift_cols[:], gshift[:].unsqueeze(2).broadcast_to([128, B, 128]))\
                            .then_inc(gn_step, 1)
                        dve.wait_ge(weights_in, 16 * 5)
                        for b in range(B):
                            nc.vector.tensor_scalar(wn[:, b, :], wqkv[:], gscale[:, b:b + 1], None, ALU.mult)\
                                .then_inc(folded, 1)

                    @block.gpsimd
                    def _(pool):
                        pool.dma_start(wqkv[:], w_qkv).then_inc(weights_in, 16)
                        pool.dma_start(gm[:], group_mean).then_inc(weights_in, 16)
                        pool.dma_start(bqk[:, 0:1], column(b_qkv[0:C])).then_inc(weights_in, 16)
                        pool.dma_start(bqk[:, 1:2], column(b_qkv[C:2 * C])).then_inc(weights_in, 16)
                        pool.dma_start(bv[:], row(b_qkv[2 * C:3 * C]).partition_broadcast(128)).then_inc(weights_in, 16)
                        nc.gpsimd.memset(zeros[:], 0.0).then_inc(zero_set, 1)
                        for b in range(B):
                            for edge in (slice(0, PAD), slice(HP - PAD, HP)):
                                nc.gpsimd.memset(k_map[:, b, edge, :], 0.0).then_inc(k_border_set, 1)
                            for edge in (slice(0, PAD), slice(WP - PAD, WP)):
                                nc.gpsimd.memset(k_map[:, b, PAD:PAD + H, edge], 0.0).then_inc(k_border_set, 1)

                with nc.Block() as block:
                    @block.gpsimd
                    def _(pool):
                        nc.gpsimd.memset(q_heads[:], 0.0).then_inc(q_cleared, 1)
                        nc.gpsimd.memset(v_rest[:], 0.0).then_inc(v_cleared, 1)
                        pool.wait_ge(rpb_placed, 16)
                        for i in range(QR):
                            for j in range(QC):
                                first = i * QC + j
                                pool.dma_start(
                                    toeplitz[first:first + Q * (NH - 1) + 1:Q, :].rearrange("h (a b) -> h a b", a=KR),
                                    rpb_pad[:, PAD - i:PAD - i + KR, QC - 1 - j:QC - 1 - j + KC])\
                                    .then_inc(toeplitz_in, 16)
                        pool.wait_ge(q_cleared, 1)
                        pool.wait_ge(v_cleared, 1)
                        pool.wait_ge(q_out, 2)
                        for n in range(2):
                            place_queries(n, n)

                    @block.tensor
                    def _(pe):
                        pe.sem_inc(v_mm, 2)
                        for m in range(2):
                            nc.tensor.matmul(ps_g[:, m * B:(m + 1) * B], wqkv[:, m * C:(m + 1) * C], gshift[:],
                                             start=True, stop=True)
                        for b in range(B):
                            last = nc.tensor.matmul(ps_g[:, (b + 1) * C:(b + 2) * C], gshift_cols[:, b, :],
                                                    wqkv[:, 2 * C:3 * C], start=True, stop=True)
                        last.then_inc(bias_mm, 1)
                        for b in range(B):
                            with pe.Fori(b * GB // 2, (b + 1) * GB // 2) as r:
                                for s in range(2):
                                    pe.wait_ge(q_out, r * 2 + (s + 1))
                                    nc.tensor.matmul(ps_q[:], wn[:, b, 0:C], x_t[:, ds(r * (2 * G) + s * G, G)],
                                                     start=True, stop=True).then_inc(qk_mm, 1)
                                    pe.wait_ge(k_out, r * 2 + (s + 1))
                                    nc.tensor.matmul(ps_k[:], wn[:, b, C:2 * C], x_t[:, ds(r * (2 * G) + s * G, G)],
                                                     start=True, stop=True).then_inc(qk_mm, 1)
                                    pe.wait_ge(staged, r * 2 + (s + 1))
                                    pe.wait_ge(v_out, r * 2 + (s + 1))
                                    for i in range(TG):
                                        last = nc.tensor.matmul(ps_v[s][:, i, :], x_now[:, s, i * 128:(i + 1) * 128],
                                                                wn[:, b, 2 * C:3 * C], start=True, stop=True)
                                    last.then_inc(v_mm, 1)
                        pe.wait_ge(weights1_in, 16 * 9)
                        for m in range(5):
                            last = nc.tensor.transpose(ps_t[m // 4][:, m % 4 * 128:(m % 4 + 1) * 128],
                                                       weights1[:, m, :], ident[:])
                        last.then_inc(weights1_turned, 1)

                    @block.scalar
                    def _(act):
                        act.sem_inc(q_out, 1)
                        act.wait_ge(folded, 5)
                        for b in range(B):
                            with act.Fori(b * GB, (b + 1) * GB) as g:
                                act.wait_ge(qk_mm, g * 2 + 1)
                                nc.scalar.activation(q_map[:, ds(g * GR, GR), :].rearrange("p h w -> p (h w)"),
                                                     ps_q[:], ACT.Identity,
                                                     bias=bqk_n[:, b, 0:1], scale=SCALE).then_inc(q_out, 1)
                        act.wait_ge(weights1_turned, 1)
                        nc.scalar.activation(weights1_t[:, 0:4, :].rearrange("p m c -> p (m c)"), ps_t[0][:], ACT.Copy)
                        nc.scalar.activation(weights1_t[:, 4, :], ps_t[1][:, 0:128], ACT.Copy)\
                            .then_inc(weights1_ready, 1)
                        nc.scalar.preload_act_table(ACT.Exp)

                    @block.vector
                    def _(dve):
                        dve.sem_inc(k_out, 1)
                        dve.sem_inc(v_out, 2)
                        dve.wait_ge(bias_mm, 1)
                        nc.vector.tensor_tensor(bqk_n[:], ps_g[:, 0:2 * B].rearrange("p (m b) -> p b m", b=B),
                                                bqk[:].unsqueeze(1).broadcast_to([128, B, 2]), ALU.add)\
                            .then_inc(folded, 1)
                        nc.vector.tensor_tensor(bv_n[:], ps_g[:, C:(B + 1) * C].rearrange("p (b c) -> p b c", b=B),
                                                bv[:].unsqueeze(1).broadcast_to([128, B, C]), ALU.add)\
                            .then_inc(folded, 1)
                        dve.wait_ge(folded, 4)
                        nc.vector.tensor_scalar(bqk_n[:, :, 0], bqk_n[:, :, 0], SCALE, None, ALU.mult)\
                            .then_inc(folded, 1)
                        dve.wait_ge(folded, 5)
                        for b in range(B):
                            with dve.Fori(b * GB // 2, (b + 1) * GB // 2) as r:
                                for s in range(2):
                                    dve.wait_ge(v_mm, r * 2 + (s + 1))
                                    nc.vector.tensor_copy(x_now[:, s, :], x_t[:, ds(r * (2 * G) + s * G, G)])\
                                        .then_inc(staged, 1)
                                    dve.wait_ge(qk_mm, r * 4 + (2 * s + 2))
                                    nc.vector.tensor_scalar(
                                        k_map[:, b, ds(r * (2 * GR) + (s * GR + PAD - b * H), GR), PAD:PAD + W],
                                        ps_k[:].rearrange("p (h w) -> p h w", w=W),
                                        bqk_n[:, b, 1:2], None, ALU.add).then_inc(k_out, 1)
                                    dve.wait_ge(v_mm, r * 2 + (s + 3))
                                    dve.wait_ge(v_stored[s], r * 32 + 32)
                                    nc.vector.tensor_tensor(v_tok[:, s], ps_v[s][:],
                                                            bv_n[:, b, :].unsqueeze(1).broadcast_to([128, TG, C]),
                                                            ALU.add).then_inc(v_out, 1)
                        dve.wait_ge(mask_in, 16)
                        dve.wait_ge(toeplitz_in, 16 * Q)
                        nc.vector.tensor_tensor(bias_tab[:].rearrange("p r c k -> p (r c) k"),
                                                bias_tab[:].rearrange("p r c k -> p (r c) k"),
                                                toeplitz[:].unsqueeze(1).broadcast_to([128, 9, KEYS]), ALU.add)\
                            .then_inc(bias_built, 1)

                    @block.sync
                    def _(sp):
                        sp.dma_start(bias_tab[:], window_mask).then_inc(mask_in, 16)
                        for b in range(B):
                            for c in (0, WP - PAD):
                                sp.dma_start(v_map[b, :, c:c + PAD, :],
                                             zeros[0:H, :].rearrange("p (a c) -> p a c", a=PAD))\
                                    .then_inc(v_side_set, 16)
                        for b in range(B):
                            for r in (0, HP - PAD):
                                edge = v_windows[b, 0, r, :]
                                n = NB * PAD * KC * C // 128
                                sp.dma_start(bass.AP(edge.tensor, edge.offset,
                                                     [[HP * KC * C, NB], [n, 128 // NB], [1, n]]),
                                             zeros[:, 0:n]).then_inc(v_border_set, 16)
                        for s in range(2):
                            sp.sem_inc(v_stored[s], 32)

                        def store(b, r):
                            for s in range(2):
                                sp.wait_ge(v_out, r * 2 + (s + 3))
                                for odd in range(2):
                                    sp.dma_start(
                                        v_map[b, ds(r * (2 * GR) + (s * GR - b * H), GR), PAD:PAD + W, :]
                                        .rearrange("(t o) w c -> o w t c", o=2)[odd],
                                        v_tok[odd * W:(odd + 1) * W, s]).then_inc(v_stored[s], 16)

                        for b in range(B):
                            store(b, b * GP)
                            if b == 0:
                                sp.wait_ge(v_side_set, 16 * 2 * B)
                            else:
                                window(sp, b - 1, b * GP - 1)
                            with sp.Fori(b * GP + 1, (b + 1) * GP - (b == B - 1)) as r:
                                store(b, r)
                                window(sp, b, r - 1)
                        window(sp, B - 1, B * GP - 2)
                        store(B - 1, B * GP - 1)

            with ExitStack() as stage:
                sb = tensors(stage)
                pb = banks(stage)
                scores = sb("scores", [128, 4, KEYS])
                negmax = sb("negmax", [128, NB])
                probs = sb("probs", [128, NB // RB, KEYS, RB])
                total = sb("total", [128, NB])
                inverse = sb("inverse", [128, NB])
                main_t = sb("main_t", [MAIN, NB, 128])
                rest_t = sb("rest_t", [RB * REST, NB // RB, 128])
                v_main = sb("v_main", [MAIN, 2, NB, C])
                o_t = sb("o_t", [128, 2, QR * W])

                ps_s = [pb(f"ps_s{i}", [128, 512]) for i in range(4)]
                ps_k = [pb(f"ps_key{i}", [128, 4, 128]) for i in range(2)]
                ps_o = [pb(f"ps_o{i}", [128, 512]) for i in range(2)]
                OC = NB * Q

                scored = sem("scored")
                biased = sem("biased")
                exponentiated = sem("exponentiated")
                inverted = sem("inverted")
                normalised = sem("normalised")
                turned = sem("turned")
                turned_out = sem("turned_out")
                weighed = sem("weighed")
                v_in = [sem(f"v_in{i}") for i in range(2)]
                o_out = sem("o_out")
                projected = sem("projected")
                added = sem("added")
                measured = sem("measured")
                bias_added = sem("bias_added")

                PB = SB // 2
                LN, LT, LC = 2, 3, 4

                def pairs(e, classes=False):
                    yield 0, 0, (0, 1)
                    with e.Fori(1, PB - 1 if classes else PB) as p:
                        yield 0, p, (1, 1)
                    if classes:
                        yield 0, PB - 1, (1, 2)
                        yield 1, PB, (0, 1)
                        with e.Fori(PB + 1, 2 * PB - 1) as p:
                            yield 1, p, (1, 1)
                        yield 1, 2 * PB - 1, (1, 2)
                    else:
                        with e.Fori(PB, 2 * PB) as p:
                            yield 1, p, (1, 1)

                BLOCKS = B * SB * NB
                STRIPS = B * SB

                def weigh(pe, n, j, k, s):
                    if j % RB == 0:
                        pe.wait_ge(turned_out, k + RB)
                    if j == 0:
                        pe.wait_ge(v_in[s], (n - s) * 40 + 80)
                        pe.wait_ge(o_out, n + 1)
                        pe.wait_ge(added, n + 1)
                    for values, by_key in ((v_main, main_t[:, j, :]), (v_rest, rest_t[:, j // RB, :])):
                        for h in range(NH):
                            hd = slice(h * HD, (h + 1) * HD)
                            last = nc.tensor.matmul(ps_o[s][hd, j * Q:(j + 1) * Q], values[:, s, j, hd], by_key[:, hd],
                                                    start=(values is v_main), stop=(values is v_rest),
                                                    tile_position=(0, h * HD))
                    last.then_inc(weighed, 1)

                def turn(pe, j, k):
                    pe.wait_ge(normalised, k + 1)
                    wait(pe, turned_out, k - 1)
                    last = nc.tensor.transpose(ps_k[j % 2][0:MAIN, 0, :], probs[:, j // RB, 0:MAIN, j % RB], ident[:])
                    if j % RB == RB - 1:
                        last = nc.tensor.transpose(ps_k[j % 2][0:RB * REST, 1, :],
                                                   probs[:, j // RB, MAIN:KEYS, :].rearrange("p k i -> p (k i)"),
                                                   ident[:])
                    last.then_inc(turned, 1)

                def project(pe, n, s):
                    pe.wait_ge(o_out, n + 3)
                    for i in range(ST):
                        last = nc.tensor.matmul(ps_o[s][:, OC + i * C:OC + (i + 1) * C],
                                                o_t[:, s, i * 128:(i + 1) * 128], wp[:], start=True, stop=True)
                    last.then_inc(projected, 1)

                with nc.Block() as block:
                    @block.gpsimd
                    def _(pool):
                        def add_bias(n):
                            nc.gpsimd.tensor_tensor(res[:, ds(n * ST, ST), :], res[:, ds(n * ST, ST), :],
                                                    bp[:].unsqueeze(1).broadcast_to([128, ST, C]), ALU.add)\
                                .then_inc(bias_added, 1)

                        def place(n, s, biases):
                            wait(pool, scored, (n - 1) * NB)
                            pool.wait_ge(bias_added, biases)
                            place_queries(n, s)

                        pool.wait_ge(res_in, 16)
                        pool.wait_ge(bp_in, 16)
                        add_bias(0)
                        pool.wait_ge(bias_added, 1)
                        add_bias(1)
                        with pool.Fori(1, STRIPS // 2) as p:
                            place(p * 2, 0, p * 2)
                            place(p * 2 + 1, 1, p * 2)
                            pool.wait_ge(res_in, p * 16 + 16)
                            pool.wait_ge(q_placed, p * 2 + 2)
                            add_bias(p * 2)
                            add_bias(p * 2 + 1)

                    @block.sync
                    def _(sp):
                        def load_residual(p):
                            sp.dma_start(res[:, ds(p * (2 * ST), 2 * ST), :],
                                         x_tok[:, ds(p * (2 * ST), 2 * ST), :]).then_inc(res_in, 16)

                        sp.wait_ge(v_border_set, 16 * 2 * B)
                        sp.wait_ge(v_cleared, 1)
                        for b, p, _ in pairs(sp):
                            sp.wait_ge(v_windowed[b], 16 * GP)
                            first = isinstance(p, int) and p == 0
                            if not first:
                                sp.wait_ge(res_in, p * 16)
                                load_residual(p)
                            for s in range(2):
                                n = p * 2 + s
                                if not first:
                                    sp.wait_ge(weighed, (n - 1) * NB)
                                win = v_windows[b, 0, ds(n * QR - b * H, 1), :]
                                sp.dma_start(v_main[:, s], bass.AP(win.tensor, win.offset,
                                                                   [[C, MAIN], [HP * KC * C, NB], [1, C]]))\
                                    .then_inc(v_in[s], 16)
                                for i in range(RB):
                                    win = v_windows[b, i, ds(n * QR + (MR - b * H), 1), :]
                                    sp.dma_start(v_rest[i:RB * REST:RB, s, i:NB:RB, :],
                                                 bass.AP(win.tensor, win.offset,
                                                         [[C, REST], [RB * HP * KC * C, NB // RB], [1, C]]))\
                                        .then_inc(v_in[s], 16)
                                if first and s == 0:
                                    load_residual(0)
                            if first:
                                window(sp, B - 1, B * GP - 1)

                    @block.tensor
                    def _(pe):
                        pe.wait_ge(wp_in, 16)
                        pe.sem_inc(projected, 2)
                        for b, p, _ in pairs(pe):
                            first = isinstance(p, int) and p == 0
                            for s in range(2):
                                n = p * 2 + s
                                for j in range(NB):
                                    k = n * NB + j
                                    if j == 0:
                                        pe.wait_ge(q_placed, n + 1)
                                    wait(pe, biased, k - 3)
                                    nc.tensor.matmul(
                                        ps_s[j % 4][:, 0:KEYS], q_heads[:, s, j, :],
                                        k_map[:, b, ds(n * QR - b * H, KR), j * QC:j * QC + KC],
                                        start=True, stop=True).then_inc(scored, 1)
                                    if not (first and s == 0):
                                        weigh(pe, n - 1, j, k - NB, 1 - s)
                                    if not (first and s == 0 and j < LT):
                                        turn(pe, (j - LT) % NB, k - LT)
                                    if j == 3 and not first:
                                        project(pe, n - 2, s)
                        for i in range(LT, 0, -1):
                            turn(pe, NB - i, BLOCKS - i)
                        project(pe, STRIPS - 2, 0)
                        for j in range(NB):
                            weigh(pe, STRIPS - 1, j, BLOCKS - NB + j, 1)
                        project(pe, STRIPS - 1, 1)

                    @block.vector
                    def _(dve):
                        dve.sem_inc(added, 2)

                        def invert(j, k):
                            dve.wait_ge(exponentiated, k + 1)
                            nc.vector.reciprocal(inverse[:, j:j + 1], total[:, j:j + 1]).then_inc(inverted, 1)

                        def normalise(j, k):
                            dve.wait_ge(inverted, k + 1)
                            nc.vector.tensor_scalar(probs[:, j // RB, :, j % RB], probs[:, j // RB, :, j % RB],
                                                    inverse[:, j:j + 1], None, ALU.mult).then_inc(normalised, 1)

                        def residual(n, s):
                            dve.wait_ge(projected, n + 3)
                            dve.wait_ge(bias_added, n + 1)
                            nc.vector.tensor_tensor(res[:, ds(n * ST, ST), :],
                                                    ps_o[s][:, OC:OC + ST * C].rearrange("p (t c) -> p t c", c=C),
                                                    res[:, ds(n * ST, ST), :], ALU.add).then_inc(added, 1)

                        def measure(n, i):
                            dve.wait_ge(added, n + 3)
                            nc.vector.bn_stats(
                                ln_stats[:, ds(n * ST + i, 1), :].rearrange("p t s -> p (t s)"),
                                res[:, ds(n * ST + i, 1), :].rearrange("p t c -> p (t c)")).then_inc(measured, 1)

                        for b, p, windows in pairs(dve, classes=True):
                            first = isinstance(p, int) and p == 0
                            for s in range(2):
                                n = p * 2 + s
                                for j in range(NB):
                                    k = n * NB + j
                                    c = 0 if j == 0 else 2 if j == NB - 1 else 1
                                    dve.wait_ge(scored, k + 1)
                                    if not (first and s == 0 and j < LN):
                                        invert((j - LN) % NB, k - LN)
                                    nc.vector.tensor_tensor_reduce(
                                        out=scores[:, j % 4, :], in0=ps_s[j % 4][:, 0:KEYS],
                                        in1=bias_tab[:, windows[s], c, :], scale=-1.0, scalar=3.0e38,
                                        op0=ALU.add, op1=ALU.min,
                                        accum_out=negmax[:, j:j + 1]).then_inc(biased, 1)
                                    if not (first and s == 0 and j < LN):
                                        normalise((j - LN) % NB, k - LN)
                                    if j == 5 and not first:
                                        residual(n - 2, s)
                                    if 5 < j <= 5 + ST and not first:
                                        measure(n - 2, j - 6)
                        for i in range(LN, 0, -1):
                            invert(NB - i, BLOCKS - i)
                            normalise(NB - i, BLOCKS - i)
                        for n in (STRIPS - 2, STRIPS - 1):
                            residual(n, n % 2)
                            for i in range(ST):
                                measure(n, i)
                            if n == STRIPS - 2:
                                dve.wait_ge(measured, EARLY.stop)
                                layernorm_vector(dve, 0, 0)

                    @block.scalar
                    def _(act):
                        act.sem_inc(o_out, 2)

                        def turned_copy(j, k):
                            act.wait_ge(turned, k + 1)
                            wait(act, weighed, k - (NB - 1))
                            last = nc.scalar.activation(main_t[:, j, :], ps_k[j % 2][0:MAIN, 0, :], ACT.Copy)
                            if j % RB == RB - 1:
                                last = nc.scalar.activation(rest_t[:, j // RB, :], ps_k[j % 2][0:RB * REST, 1, :],
                                                            ACT.Copy)
                            last.then_inc(turned_out, 1)

                        def strip_out(n, s):
                            act.wait_ge(weighed, n * NB + NB)
                            act.wait_ge(projected, n + 1)
                            nc.scalar.activation(
                                o_t[:, s, :].rearrange("p (r j c) -> p j r c", r=QR, j=NB),
                                ps_o[s][:, 0:OC].rearrange("p (j r c) -> p j r c", j=NB, r=QR), ACT.Copy)\
                                .then_inc(o_out, 1)

                        for b, p, _ in pairs(act):
                            first = isinstance(p, int) and p == 0
                            for s in range(2):
                                n = p * 2 + s
                                for j in range(NB):
                                    k = n * NB + j
                                    if not (first and s == 0 and j < LC):
                                        turned_copy((j - LC) % NB, k - LC)
                                    act.wait_ge(biased, k + 1)
                                    if not (first and s == 0) and j % RB == 0:
                                        act.wait_ge(turned, k - (NB - RB))
                                    nc.scalar.activation(probs[:, j // RB, :, j % RB], scores[:, j % 4, :], ACT.Exp,
                                                         bias=negmax[:, j:j + 1], scale=-1.0,
                                                         accum_out=total[:, j:j + 1]).then_inc(exponentiated, 1)
                                    if j == 1 and not first:
                                        strip_out(n - 2, s)
                        for i in range(LC, 0, -1):
                            turned_copy(NB - i, BLOCKS - i)
                        strip_out(STRIPS - 2, 0)
                        nc.scalar.preload_act_table(ACT.Sqrt)
                        layernorm_scalar(act, 0, 0)
                        strip_out(STRIPS - 1, 1)

        with ExitStack() as stage:
            sb = tensors(stage)
            pb = banks(stage)
            z = sb("z", [128, 2, TG, C])
            z_t = sb("z_t", [128, 2, G])
            expo = sb("expo", [128, 2, 2, G])
            relu = sb("relu", [128, 2, 2, G])
            qk_t = sb("qk_t", [128, 2, 2, G])
            k_tok = sb("k_tok", [128, 2, TG, C])
            v_one = sb("v_one", [128, 2, TG, C + 1])
            weights = sb("weights", [128, 2, TG, 128])
            kv = sb("kv", [128, 2, TG + 1, C + 1])
            den = sb("den", [128, TG])

            z_shift = ln_diff

            ps_z = pb("ps_z", [128, TG, 128])
            ps_q = pb("ps1_q", [128, G])
            ps_k = pb("ps1_k", [128, G])
            ps_v = pb("ps1_v", [128, TG, C])
            ps_w = pb("ps_w", [128, TG, 128])
            ps_kv = pb("ps_kv", [128, 512])
            ps_n = pb("ps_n", [128, 512])
            ps_last = pb("ps_last", [128, 512])

            one_set = sem("one_set")
            z_ready = sem("z_ready")
            z_turned = sem("z_turned")
            z_out = sem("z_out")
            clipped = sem("clipped")
            clip_begun = sem("clip_begun")
            qk_made = sem("qk_made")
            qk_read = sem("qk_read")
            q_ready = sem("q_ready")
            k_ready = sem("k_ready")
            v_made = sem("v_made")
            v_ready = sem("v_ready")
            k_turned = sem("k_turned")
            k_out2 = sem("k_out2")
            w_made = sem("w_made")
            w_masked = sem("w_masked")
            kv_made = sem("kv_made")
            kv_zeroed = sem("kv_zeroed")
            kv_step = sem("kv_step")
            n_made = sem("n_made")
            den_ready = sem("den_ready")
            res_ready = sem("res_ready")
            stats_ready = sem("stats_ready")

            KVC = C + 1

            def kv_bank(t):
                return ps_kv[:, t * KVC:(t + 1) * KVC] if t < 3 else ps_last[:, 0:KVC]

            def n_bank(t):
                return ps_n[:, t * KVC:(t + 1) * KVC] if t < 3 else ps_last[:, KVC:2 * KVC]

            def steps(e, ahead, step, between=None):
                ahead()
                step(0, 0)
                step(1, 1)
                for b in range(B):
                    if b and between:
                        between()
                    with e.Fori(b * GB // 2 + (b == 0), (b + 1) * GB // 2 - (b == B - 1)) as r:
                        step(r * 2, 0)
                        step(r * 2 + 1, 1)
                step(NG - 2, 0)
                step(NG - 1, 1)

            def is_first(g):
                return isinstance(g, int) and g == 0

            def is_last(g, n=1):
                return isinstance(g, int) and g >= NG - n

            with nc.Block() as block:
                @block.gpsimd
                def _(pool):
                    nc.gpsimd.memset(v_one[:], 1.0).then_inc(one_set, 1)
                    pool.wait_ge(one_set, 1)
                    pool.sem_inc(q_ready, 2)

                    def combine(g, s):
                        pool.wait_ge(qk_read, g * 2 + 3)
                        pool.sem_inc(clip_begun, 1)
                        nc.gpsimd.tensor_scalar(expo[:, s, 0, :], expo[:, s, 0, :], 1.0, None, ALU.min)\
                            .then_inc(clipped, 1)
                        pool.wait_ge(clipped, g)
                        wait(pool, n_made, g)
                        nc.gpsimd.tensor_tensor(qk_t[:, s, 0, :], expo[:, s, 0, :], relu[:, s, 0, :], ALU.add)\
                            .then_inc(q_ready, 1)

                    def step(g, s):
                        if not is_last(g):
                            combine(g + 1, 1 - s)

                    steps(pool, lambda: None, step)

                @block.tensor
                def _(pe):
                    pe.sem_inc(n_made, 1)

                    def turn_z(g, s):
                        pe.wait_ge(z_ready, g + 1)
                        for i in range(TG):
                            last = nc.tensor.transpose(ps_z[:, i, :], z[:, s, i, :], ident[:])
                        last.then_inc(z_turned, 1)

                    def make_qk(g, s):
                        pe.wait_ge(z_out, g + 1)
                        for m, bank in ((0, ps_q), (1, ps_k)):
                            pe.wait_ge(qk_read, g * 2 + (m + 1))
                            nc.tensor.matmul(bank[:], attn_wt[:, m, :], z_t[:, s, :], start=True, stop=True)\
                                .then_inc(qk_made, 1)

                    def make_v(s):
                        for i in range(TG):
                            last = nc.tensor.matmul(ps_v[:, i, :], z_t[:, s, i * 128:(i + 1) * 128], attn_wt[:, 2, :],
                                                    start=True, stop=True)
                        last.then_inc(v_made, 1)

                    def ahead():
                        turn_z(0, 0)
                        make_qk(0, 0)
                        make_v(0)

                    def step(g, s):
                        if not is_last(g):
                            pe.wait_ge(k_out2, g + 1)
                            turn_z(g + 1, 1 - s)
                        pe.wait_ge(w_masked, g + 1)
                        pe.wait_ge(q_ready, g + 3)
                        pe.wait_ge(k_ready, g + 3)
                        for i in range(TG):
                            t = slice(i * 128, (i + 1) * 128)
                            last = nc.tensor.matmul(ps_w[:, i, :], qk_t[:, s, 1, t], qk_t[:, s, 0, t],
                                                    start=True, stop=True)
                        last.then_inc(w_made, 1)
                        if is_last(g):
                            pe.wait_ge(k_out2, g + 1)
                        else:
                            pe.wait_ge(z_out, g + 2)
                        for i in range(TG):
                            last = nc.tensor.transpose(ps_z[:, i, :], qk_t[:, s, 1, i * 128:(i + 1) * 128], ident[:])
                        last.then_inc(k_turned, 1)
                        if not is_last(g):
                            make_qk(g + 1, 1 - s)
                        if not is_first(g):
                            outputs(g - 1, 1 - s)
                        pe.wait_ge(v_ready, g + 1)
                        if not is_last(g):
                            make_v(1 - s)
                        pe.wait_ge(k_out2, g + 2)
                        for i in range(TG):
                            if i == TG - 1 and not is_first(g):
                                pe.wait_ge(res_ready, g * TG - (TG - 2))
                            last = nc.tensor.matmul(kv_bank(i), k_tok[:, s, i, :], v_one[:, s, i, :],
                                                    start=True, stop=True)
                        last.then_inc(kv_made, 1)

                    def outputs(g, s):
                        pe.wait_ge(w_masked, g + 2)
                        pe.wait_ge(kv_step, g * (TG + 1) + (TG + 1))
                        pe.wait_ge(res_ready, g * TG + 1)
                        for i in range(TG):
                            nc.tensor.matmul(n_bank(i), weights[:, s, i, :], v_one[:, s, i, :], start=True, stop=False)
                            last = nc.tensor.matmul(n_bank(i), qk_t[:, s, 0, i * 128:(i + 1) * 128], kv[:, s, i, :],
                                                    start=False, stop=True)
                        last.then_inc(n_made, 1)

                    steps(pe, ahead, step)
                    outputs(NG - 1, 1)

                @block.scalar
                def _(act):
                    act.sem_inc(qk_read, 2)
                    act.sem_inc(k_out2, 1)

                    def normalise(g, s):
                        for i in range(TG):
                            t = g * TG + i
                            last = nc.scalar.activation(z[:, s, i, :], tile(res, t), ACT.Identity,
                                                        bias=z_shift[:, ds(t, 1)], scale=ln_rstd[:, ds(t, 1)])
                        last.then_inc(z_ready, 1)

                    def copy_z(g, s):
                        act.wait_ge(z_turned, g + 1)
                        nc.scalar.activation(z_t[:, s, :], ps_z[:].rearrange("p t c -> p (t c)"), ACT.Copy)\
                            .then_inc(z_out, 1)

                    def exponentials(g, s):
                        for m, bank, free in ((0, ps_q, q_ready), (1, ps_k, k_ready)):
                            act.wait_ge(qk_made, g * 2 + (m + 1))
                            act.wait_ge(free, g + 1)
                            nc.scalar.activation(expo[:, s, m, :], bank[:], ACT.Exp, bias=attn_bqk[:, m:m + 1])
                            nc.scalar.activation(relu[:, s, m, :], bank[:], ACT.Relu, bias=attn_bqk[:, m:m + 1])\
                                .then_inc(qk_read, 1)

                    def ahead():
                        copy_z(0, 0)
                        layernorm_scalar(act, 0, 1)
                        nc.scalar.preload_act_table(ACT.Exp)
                        normalise(1, 1)
                        exponentials(0, 0)
                        act.wait_ge(ln_step[0], 2 * LN_STEPS)

                    def step(g, s):
                        if not is_last(g):
                            copy_z(g + 1, 1 - s)
                        act.wait_ge(k_turned, g + 1)
                        nc.scalar.activation(k_tok[:, s], ps_z[:], ACT.Copy).then_inc(k_out2, 1)
                        if not is_last(g):
                            exponentials(g + 1, 1 - s)
                        if not is_last(g, 2):
                            normalise(g + 2, s)

                    steps(act, ahead, step)
                    nc.scalar.preload_act_table(ACT.Sqrt)
                    layernorm_scalar(act, 1, 0)

                @block.vector
                def _(dve):
                    for i in range(TG):
                        last = nc.vector.tensor_scalar(z[:, 0, i, :], res[:, i, :], ln_mean[:, i:i + 1],
                                                       ln_rstd[:, i:i + 1], ALU.subtract, ALU.mult)
                    last.then_inc(z_ready, 1)
                    layernorm_vector(dve, 0, 1)
                    dve.wait_ge(one_set, 1)
                    dve.sem_inc(w_masked, 1)
                    dve.sem_inc(res_ready, 1)
                    dve.sem_inc(k_ready, 2)
                    nc.vector.memset(kv[:, 1, TG, :], 0.0).then_inc(kv_zeroed, 1)
                    dve.wait_ge(kv_zeroed, 1)

                    def combine(g, s):
                        dve.wait_ge(qk_read, g * 2 + 4)
                        nc.vector.scalar_tensor_tensor(out=qk_t[:, s, 1, :], in0=expo[:, s, 1, :], scalar=1.0,
                                                       in1=relu[:, s, 1, :], op0=ALU.min, op1=ALU.add)\
                            .then_inc(k_ready, 1)

                    def values(g, s):
                        dve.wait_ge(v_made, g + 1)
                        nc.vector.tensor_tensor(v_one[:, s, :, 0:C], ps_v[:],
                                                attn_bv[:].unsqueeze(1).broadcast_to([128, TG, C]), ALU.add)\
                            .then_inc(v_ready, 1)

                    def outputs(g):
                        dve.wait_ge(n_made, g + 2)
                        nc.vector.tensor_scalar(den[:, 0:3], ps_n[:, 0:3 * KVC]
                                                .rearrange("p (t c) -> p t c", c=KVC)[:, :, C],
                                                DEN_EPS, None, ALU.add).then_inc(den_ready, 1)
                        nc.vector.tensor_scalar(den[:, 3:4], ps_last[:, 2 * KVC - 1:2 * KVC], DEN_EPS, None, ALU.add)\
                            .then_inc(den_ready, 1)
                        dve.wait_ge(den_ready, g * 3 + 2)
                        nc.vector.reciprocal(den[:], den[:]).then_inc(den_ready, 1)
                        dve.wait_ge(den_ready, g * 3 + 3)
                        for i in reversed(range(TG)):
                            t = g * TG + i
                            nc.vector.scalar_tensor_tensor(out=tile(res, t), in0=n_bank(i)[:, 0:C],
                                                           scalar=den[:, i:i + 1], in1=tile(res, t),
                                                           op0=ALU.mult, op1=ALU.add).then_inc(res_ready, 1)

                    def statistics(g):
                        dve.wait_ge(res_ready, g * TG + (TG + 1))
                        for i in range(TG):
                            t = g * TG + i
                            nc.vector.bn_stats(tile(ln_stats, t), tile(res, t)).then_inc(stats_ready, 1)

                    def step(g, s):
                        dve.wait_ge(w_made, g + 1)
                        nc.vector.tensor_tensor(weights[:, s], ps_w[:],
                                                tri[:].unsqueeze(1).broadcast_to([128, TG, 128]), ALU.mult)\
                            .then_inc(w_masked, 1)
                        if not is_last(g):
                            combine(g + 1, 1 - s)
                        if not is_first(g):
                            outputs(g - 1)
                        if not is_last(g):
                            values(g + 1, 1 - s)
                        if not is_first(g):
                            statistics(g - 1)
                        dve.wait_ge(kv_made, g + 1)
                        nc.vector.tensor_copy(kv[:, s, 0, :], kv[:, 1 - s, TG, :]).then_inc(kv_step, 1)
                        for i in range(TG):
                            dve.wait_ge(kv_step, g * (TG + 1) + (i + 1))
                            nc.vector.tensor_tensor(kv[:, s, i + 1, :], kv_bank(i), kv[:, s, i, :], ALU.add)\
                                .then_inc(kv_step, 1)
                        dve.wait_ge(kv_step, g * (TG + 1) + (TG + 1))

                    def new_batch():
                        nc.vector.memset(kv[:, 1, TG, :], 0.0).then_inc(kv_zeroed, 1)
                        dve.wait_ge(kv_zeroed, 2)

                    def ahead():
                        dve.wait_ge(qk_read, 3)
                        nc.vector.scalar_tensor_tensor(out=qk_t[:, 0, 0, :], in0=expo[:, 0, 0, :], scalar=1.0,
                                                       in1=relu[:, 0, 0, :], op0=ALU.min, op1=ALU.add)\
                            .then_inc(q_ready, 1)
                        combine(0, 0)
                        values(0, 0)

                    steps(dve, ahead, step, new_batch)
                    dve.wait_ge(z_ready, NG)
                    dve.wait_ge(stats_ready, EARLY.stop)
                    layernorm_vector(dve, 1, 0)
                    outputs(NG - 1)
                    statistics(NG - 1)

        with ExitStack() as stage:
            sb = tensors(stage)
            w_scaled = sb("w_scaled", [128, C])
            wn_t = sb("wn_t", [128, C])
            z = sb("z4", [128, 2, TG, C])
            z_t = sb("z4_t", [128, L, COLS])
            states = sb("states", [128, L, COLS])
            bstats = sb("bstats", [128, NG, 6])
            bmv = sb("bmv", [128, 2])
            bvar = sb("bvar", [128, 1])
            bstd = sb("bstd", [128, 1])
            bscale = sb("bscale", [128, 1])
            bshift = sb("bshift", [128, 1])
            warm = sb("warm", [128, B, 2, CH])
            start = sb("start", [128, B, CH])
            latest = sb("latest", [128, B, 2, CH])
            gap = sb("gap", [128, B, CH])
            worst = sb("worst", [128, 1])
            worst_all = sb("worst_all", [1, 1])
            apart = sb("apart", [1, 1], i32)
            one_state = sb("one_state", [128, B])

            z_ready = sem("z4_ready")
            z_ready_v = sem("z4_ready_v")
            HALVES = TG // 2
            z_turned = sem("z4_turned")
            z_out = sem("z4_out")
            wx_made = sem("wx_made")
            wx_read = sem("wx_read")
            bn_step = sem("bn_step")
            bn_root = sem("bn_root")
            wn_turned = sem("wn_turned")
            wn_ready = sem("wn_ready")

            with ExitStack() as stage4:
                pb = banks(stage4)
                ps_z = [pb(f"ps4_z{i}", [128, TG, 128]) for i in range(2)]
                ps_x = [pb(f"ps4_x{i}", [128, G]) for i in range(2)]
                ps_w = pb("ps4_w", [128, C])
                with nc.Block() as block:
                    @block.tensor
                    def _(pe):

                        def turn(g, s):
                            pe.wait_ge(z_ready, g + 1)
                            pe.wait_ge(z_ready_v, g + 1)
                            pe.wait_ge(z_out, g + 1)
                            for i in range(TG):
                                last = nc.tensor.transpose(ps_z[s][:, i, :], z[:, s, i, :], ident[:])
                            last.then_inc(z_turned, 1)

                        def product(g, s):
                            pe.wait_ge(z_out, g + 3)
                            pe.wait_ge(wx_read, g + 1)
                            nc.tensor.matmul(ps_x[s][:], ffn_wt, z_t[:, :, ds(g * CG, CG)], start=True, stop=True)\
                                .then_inc(wx_made, 1)

                        turn(0, 0)
                        with pe.Fori(0, NG // 2 - 1) as r:
                            turn(r * 2 + 1, 1)
                            product(r * 2, 0)
                            turn(r * 2 + 2, 0)
                            product(r * 2 + 1, 1)
                        turn(NG - 1, 1)
                        product(NG - 2, 0)
                        product(NG - 1, 1)
                        pe.wait_ge(bn_step, 4)
                        nc.tensor.transpose(ps_w[:], w_scaled[:], ident[:]).then_inc(wn_turned, 1)

                    @block.scalar
                    def _(act):
                        act.sem_inc(z_out, 2)

                        def normalise(g, s):
                            for i in range(HALVES):
                                t = g * TG + i
                                last = nc.scalar.activation(z[:, s, i, :], tile(res, t), ACT.Identity,
                                                            bias=ln_diff[:, ds(t, 1)], scale=ln_rstd[:, ds(t, 1)])
                            last.then_inc(z_ready, 1)

                        normalise(0, 0)
                        layernorm_scalar(act, 1, 1)
                        normalise(1, 1)
                        act.wait_ge(ln_step[1], 2 * LN_STEPS)

                        def copy_z(g, s):
                            act.wait_ge(z_turned, g + 1)
                            nc.scalar.activation(z_t[:, :, ds(g * CG, CG)].rearrange("p s c -> p c s"),
                                                 ps_z[s][:].rearrange("p t (c s) -> p (t c) s", s=L), ACT.Copy)\
                                .then_inc(z_out, 1)

                        with act.Fori(0, NG // 2 - 1) as r:
                            for s in range(2):
                                copy_z(r * 2 + s, s)
                                normalise(r * 2 + (s + 2), s)
                        copy_z(NG - 2, 0)
                        copy_z(NG - 1, 1)
                        nc.scalar.preload_act_table(ACT.Sqrt)
                        act.wait_ge(bn_step, 2)
                        nc.scalar.activation(bstd[:], bvar[:], ACT.Sqrt).then_inc(bn_root, 1)
                        nc.scalar.preload_act_table(ACT.Sigmoid)
                        act.wait_ge(wn_turned, 1)
                        nc.scalar.activation(wn_t[:], ps_w[:], ACT.Copy).then_inc(wn_ready, 1)

                    @block.vector
                    def _(dve):
                        dve.sem_inc(wx_read, 2)

                        def normalise(g, s):
                            for i in range(HALVES, TG):
                                t = g * TG + i
                                last = nc.vector.tensor_scalar(z[:, s, i, :], tile(res, t),
                                                               ln_mean[:, ds(t, 1)], ln_rstd[:, ds(t, 1)],
                                                               ALU.subtract, ALU.mult)
                            last.then_inc(z_ready_v, 1)

                        def statistics(g, s):
                            dve.wait_ge(wx_made, g + 1)
                            nc.vector.bn_stats(tile(bstats, g), ps_x[s][:]).then_inc(wx_read, 1)

                        normalise(0, 0)
                        normalise(1, 1)
                        layernorm_vector(dve, 1, 1)
                        dve.wait_ge(ln_step[1], 2 * LN_STEPS)
                        with dve.Fori(0, NG // 2 - 1) as r:
                            for s in range(2):
                                dve.wait_ge(z_turned, r * 2 + (s + 1))
                                normalise(r * 2 + (s + 2), s)
                                statistics(r * 2 + s, s)
                        statistics(NG - 2, 0)
                        statistics(NG - 1, 1)
                        dve.wait_ge(wx_read, NG + 2)
                        nc.vector.bn_aggr(bmv[:], bstats[:].rearrange("p g s -> p (g s)")).then_inc(bn_step, 1)
                        dve.wait_ge(bn_step, 1)
                        nc.vector.tensor_scalar(bvar[:], bmv[:, 1:2], BN_EPS, None, ALU.add).then_inc(bn_step, 1)
                        dve.wait_ge(bn_root, 1)
                        nc.vector.reciprocal(bscale[:], bstd[:]).then_inc(bn_step, 1)
                        dve.wait_ge(bn_step, 3)
                        nc.vector.tensor_scalar(w_scaled[:], weights1[:, 3, :], bscale[:], gamma_c[:],
                                                ALU.mult, ALU.mult)\
                            .then_inc(bn_step, 1)
                        nc.vector.scalar_tensor_tensor(out=bshift[:], in0=bmv[:, 0:1], scalar=bscale[:],
                                                       in1=gamma_c[:], op0=ALU.mult, op1=ALU.mult).then_inc(bn_step, 1)
                        dve.wait_ge(bn_step, 5)
                        nc.vector.tensor_tensor(bshift[:], beta_c[:], bshift[:], ALU.subtract).then_inc(bn_step, 1)

            middling = sem("middling")
            warmed = [sem(f"warmed{b}") for b in range(B)]
            warm_made = [sem(f"warm_made{b}") for b in range(B)]
            started = sem("started")
            step_made = [sem(f"step_made{b}") for b in range(B)]
            step_done = [sem(f"step_done{b}") for b in range(B)]
            kept = [sem(f"kept{b}") for b in range(B)]
            seam_step = sem("seam_step")
            gap_turned = sem("gap_turned")
            apart_set = sem("apart_set")
            single_made = sem("single_made")
            single_done = sem("single_done")
            single_start = sem("single_start")
            with ExitStack() as stage5:
                pb = banks(stage5)
                ps_r = [[pb(f"ps_r{b}{i}", [128, 512]) for i in range(2)] for b in range(B)]
                ps_1 = pb("ps_one", [128, 512])
                UW, U, UA = 6, 10, 16
                assert WARM % UW == 0 and (L - 2) % U == 0 and L % UA == 0

                def half(a, t, b):
                    return tile(a, t)[:, b * CH:(b + 1) * CH]

                with nc.Block() as block:
                    @block.tensor
                    def _(pe):
                        def step(b, s, x_cols, y, ahead, made):
                            nc.tensor.matmul(ps_r[b][s][:, 0:CH], wn_t[:], x_cols, start=True, stop=False)
                            pe.wait_ge(*ahead)
                            nc.tensor.matmul(ps_r[b][s][:, 0:CH], v_t, y, start=False, stop=True).then_inc(made, 1)

                        pe.wait_ge(middling, 1)
                        with pe.Fori(0, WARM // UW) as r:
                            for u in range(UW):
                                for b in range(B):
                                    step(b, u % 2, half(z_t, r * UW + (u + L - WARM), b), warm[:, b, u % 2, :],
                                         (warmed[b], r * UW + (u + 1)), warm_made[b])

                        for b in range(B):
                            pe.wait_ge(warmed[b], WARM + 1)
                            step(b, 0, z_t[:, 0, b * CH:(b + 1) * CH], start[:, b, :], (started, 1), step_made[b])
                        for b in range(B):
                            step(b, 1, z_t[:, 1, b * CH:(b + 1) * CH], latest[:, b, 0, :],
                                 (step_done[b], 1), step_made[b])
                        with pe.Fori(0, (L - 2) // U) as r:
                            for u in range(U):
                                for b in range(B):
                                    step(b, u % 2, half(z_t, r * U + (u + 2), b), latest[:, b, 1 - u % 2, :],
                                         (step_done[b], r * U + (u + 2)), step_made[b])
                        pe.wait_ge(seam_step, 3)
                        nc.tensor.transpose(ps_1[0:1, 0:128], worst[:], ident[:]).then_inc(gap_turned, 1)

                    @block.scalar
                    def _(act):
                        for b in range(B):
                            act.sem_inc(warmed[b], 1)
                        with act.Fori(0, WARM // UW) as r:
                            for u in range(UW):
                                for b in range(B):
                                    act.wait_ge(warm_made[b], r * UW + (u + 1))
                                    nc.scalar.activation(warm[:, b, 1 - u % 2, :], ps_r[b][u % 2][:, 0:CH], ACT.Sigmoid,
                                                         bias=bshift[:]).then_inc(warmed[b], 1)
                        with act.Fori(0, L // UA) as r:
                            for u in range(UA):
                                for b in range(B):
                                    act.wait_ge(kept[b], r * UA + (u + 1))
                                    act.wait_ge(step_made[b], r * UA + (u + 1))
                                    nc.scalar.activation(latest[:, b, u % 2, :], ps_r[b][u % 2][:, 0:CH],
                                                         ACT.Sigmoid, bias=bshift[:]).then_inc(step_done[b], 1)

                    @block.vector
                    def _(dve):
                        nc.vector.memset(warm[:, :, 0, :], 0.5).then_inc(middling, 1)
                        nc.vector.memset(start[:], 0.0).then_inc(seam_step, 1)
                        for b in range(B):
                            dve.wait_ge(warmed[b], WARM + 1)
                        dve.wait_ge(seam_step, 1)
                        nc.vector.tensor_copy(start[:, :, 1:CH], warm[:, :, 0, 0:CH - 1]).then_inc(started, 1)
                        for b in range(B):
                            dve.sem_inc(kept[b], 2)
                        with dve.Fori(0, L // UA) as r:
                            for u in range(UA):
                                for b in range(B):
                                    dve.wait_ge(step_done[b], r * UA + (u + 1))
                                    nc.vector.tensor_copy(half(states, r * UA + u, b), latest[:, b, u % 2, :])\
                                        .then_inc(kept[b], 1)
                        for b in range(B):
                            dve.wait_ge(kept[b], L + 2)
                        nc.vector.tensor_tensor(gap[:], states[:, L - 1, :].rearrange("p (b c) -> p b c", b=B),
                                                warm[:, :, 0, :], ALU.subtract).then_inc(seam_step, 1)
                        dve.wait_ge(seam_step, 2)
                        nc.vector.tensor_reduce(worst[:], gap[:].rearrange("p b c -> p (b c)"), AX.X, ALU.max,
                                                apply_absolute_value=True).then_inc(seam_step, 1)
                        dve.wait_ge(gap_turned, 1)
                        nc.vector.tensor_reduce(worst_all[:], ps_1[0:1, 0:128], AX.X, ALU.max).then_inc(seam_step, 1)
                        dve.wait_ge(seam_step, 4)
                        nc.vector.tensor_scalar(apart[:], worst_all[:], AGREE, None, ALU.is_gt).then_inc(apart_set, 1)

                with nc.Block() as block:
                    @block.tensor
                    def _(pe):
                        flag = pe.alloc_register("pe_apart")
                        pe.reg_load(flag, apart[0:1, 0:1])
                        with pe.If_ne(flag, 0):
                            pe.wait_ge(single_start, 1)
                            with pe.Fori(0, CH) as c:
                                with pe.Fori(0, L) as i:
                                    cols = z_t[:, ds(i, 1), :].rearrange("p s (b c) -> p (s b) c", b=B)[:, :, ds(c, 1)]\
                                        .rearrange("p b c -> p (b c)")
                                    pe.wait_ge(single_done, c * L + i + 1)
                                    nc.tensor.matmul(ps_1[:, 0:B], wn_t[:], cols, start=True, stop=False)
                                    nc.tensor.matmul(ps_1[:, 0:B], v_t, one_state[:], start=False, stop=True)\
                                        .then_inc(single_made, 1)

                    @block.scalar
                    def _(act):
                        flag = act.alloc_register("act_apart")
                        act.reg_load(flag, apart[0:1, 0:1])
                        with act.If_ne(flag, 0):
                            act.wait_ge(single_start, 1)
                            act.sem_inc(single_done, 1)
                            with act.Fori(0, CH) as c:
                                with act.Fori(0, L) as i:
                                    act.wait_ge(single_made, c * L + i + 1)
                                    cols = states[:, ds(i, 1), :].rearrange("p s (b c) -> p (s b) c", b=B)\
                                        [:, :, ds(c, 1)].rearrange("p b c -> p (b c)")
                                    nc.scalar.activation(cols, ps_1[:, 0:B], ACT.Sigmoid, bias=bshift[:])
                                    nc.scalar.activation(one_state[:], ps_1[:, 0:B], ACT.Sigmoid, bias=bshift[:])\
                                        .then_inc(single_done, 1)

                    @block.vector
                    def _(dve):
                        nc.vector.memset(one_state[:], 0.0).then_inc(single_start, 1)

            with ExitStack() as stage6:
                pb = banks(stage6)
                sb = tensors(stage6)
                YS = 4
                y_t = sb("y_t", [128, YS, CG, L])
                OS = 8
                y_out = sb("y_out", [128, OS, TG, C])
                ps_y = [pb(f"ps6_y{i}", [128, TG, 128]) for i in range(YS)]
                y_ready = sem("y_ready")
                y_turned = sem("y_turned")
                y_added = sem("y_added")
                y_stored = [sem(f"y_stored{i}") for i in range(OS)]
                with nc.Block() as block:
                    @block.scalar
                    def _(act):
                        act.sem_inc(y_turned, YS)
                        with act.Fori(0, NG // YS) as r:
                            for s in range(YS):
                                act.wait_ge(y_turned, r * YS + (s + 1))
                                nc.scalar.activation(
                                    y_t[:, s], states[:, :, ds(r * (YS * CG) + s * CG, CG)]
                                    .rearrange("p s c -> p c s"), ACT.Copy).then_inc(y_ready, 1)

                    @block.tensor
                    def _(pe):
                        with pe.Fori(0, NG // YS) as r:
                            for s in range(YS):
                                pe.wait_ge(y_ready, r * YS + (s + 1))
                                pe.wait_ge(y_added, r * YS + (s + 1))
                                flat = y_t[:, s].rearrange("p c s -> p (c s)")
                                for i in range(TG):
                                    last = nc.tensor.transpose(ps_y[s][:, i, :], flat[:, i * 128:(i + 1) * 128],
                                                               ident[:])
                                last.then_inc(y_turned, 1)

                    @block.vector
                    def _(dve):
                        dve.sem_inc(y_added, YS)
                        with dve.Fori(0, NG // OS) as r:
                            for s in range(OS):
                                dve.wait_ge(y_turned, r * OS + (s + YS + 1))
                                dve.wait_ge(y_stored[s], r * 16 + 16)
                                nc.vector.tensor_tensor(y_out[:, s], ps_y[s % YS][:],
                                                        res[:, ds(r * (OS * TG) + s * TG, TG), :], ALU.add)\
                                    .then_inc(y_added, 1)

                    @block.sync
                    def _(sp):
                        for s in range(OS):
                            sp.sem_inc(y_stored[s], 16)
                        with sp.Fori(0, NG // OS) as r:
                            for s in range(OS):
                                sp.wait_ge(y_added, r * OS + (s + YS + 1))
                                sp.dma_start(out_tok[:, ds(r * (OS * TG) + s * TG, TG), :], y_out[:, s])\
                                    .then_inc(y_stored[s], 16)
                        for s in range(OS):
                            sp.wait_ge(y_stored[s], 16 * (NG // OS + 1))


_INS = ["x", "L0_conv_w_qkv", "L0_conv_b_qkv", "L0_conv_rpb", "L0_conv_w_proj", "L0_conv_b_proj",
        "L1_attn_W", "L1_attn_b", "L1_ffn_W", "L1_ffn_V", "L1_ffn_gamma", "L1_ffn_beta"]


def _window_mask():
    import numpy as np

    size, k, qr, qc, heads = 64, 7, 4, 8, 4
    kr, kc = qr + k - 1, qc + k - 1

    def inside(first, n, keys):
        at = first + np.arange(n)
        start = np.clip(at - k // 2, 0, size - k)
        key = first - k // 2 + np.arange(keys)
        return (key[None] >= start[:, None]) & (key[None] < start[:, None] + k)

    rows = [inside(f, qr, kr) for f in (0, qr, size - qr)]
    cols = [inside(f, qc, kc) for f in (0, qc, size - qc)]
    mask = np.empty((heads, qr, qc, 3, 3, kr, kc), np.float32)
    for a, r in enumerate(rows):
        for b, c in enumerate(cols):
            both = r[:, None, :, None] & c[None, :, None, :]
            mask[:, :, :, a, b] = np.where(both, 0.0, -1e30)
    return mask.reshape(128, 3, 3, kr * kc)


def _constants():
    import numpy as np

    group = np.kron(np.eye(32), np.full((4, 4), 0.25)).astype(np.float32)
    return {"window_mask": _window_mask(), "group_mean": group, "identity": np.eye(128, dtype=np.float32),
            "causal": np.triu(np.ones((128, 128), np.float32))}


def kernel(**inputs):
    import numpy as np
    import concourse.bacc as bacc
    from concourse import mybir
    from concourse.bass_utils import run_bass_kernel_spmd

    nc = bacc.Bacc("TRN2", target_bir_lowering=False, num_devices=1)
    arrays, args = {}, []
    for name, a in [(n, inputs[n]) for n in _INS] + list(_constants().items()):
        a = np.ascontiguousarray(a)
        arrays[f"in_{name}"] = a
        args.append(nc.dram_tensor(f"in_{name}", a.shape, mybir.dt.from_np(a.dtype), kind="ExternalInput").ap())
    args.append(nc.dram_tensor("out_0", (2, 64, 64, 128), mybir.dt.float32, kind="ExternalOutput").ap())
    neighborhood_attention_linear_attention_rnn_kernel(nc, *args)
    r = run_bass_kernel_spmd(nc, [arrays], core_ids=[0])
    return r.results[0]["out_0"]
```
